# Optimizing a Trainium2 kernel written in Bass

```python
import numpy as np
import jax
import jax.numpy as jnp

def _softmax(x, axis=-1):
    return jax.nn.softmax(x, axis=axis)

def _gelu(x):
    return jax.nn.gelu(x, approximate=True)

def _silu(x):
    return jax.nn.silu(x)

def _sigmoid(x):
    return jax.nn.sigmoid(x)

def _layernorm(x, axis=-1, eps=1e-05):
    m = jnp.mean(x, axis=axis, keepdims=True)
    v = jnp.var(x, axis=axis, keepdims=True)
    return (x - m) / jnp.sqrt(v + eps)

def _scatter_add(tgt, idx, src, axis=0):
    return tgt.at[idx].add(src)

def _segment_sum(src, seg, n):
    return jax.ops.segment_sum(src, seg, n)
kernel_name = 'mk_hybrid_d1_jaxref_r8_69a1b1'

def setup_inputs(seed: int=0):
    np.random.seed(seed)
    _w = jnp.asarray

    def _L0_attn_a_setup():
        import jax, jax.numpy as jnp
        import numpy as np
        B, T, D = (4, 256, 128)
        H = 4
        K = D // H
        V = D // H
        M = 64
        GATE_LOGIT_NORMALIZER = 8.0
        NORM_EPS = 1e-05

        def _swish(x):
            return x * jax.nn.sigmoid(x)

        def _gsa_recurrence(q, k, v, s, g, scale):
            b, t, h, dk = q.shape
            dv = v.shape[-1]
            m = s.shape[-1]

            def step(carry, inp):
                hk, hv = carry
                q_t, k_t, v_t, s_t, g_t = inp
                ge = jnp.exp(g_t)
                hk = hk * ge[:, :, None, :] + k_t[..., :, None] * s_t[..., None, :]
                logits = jnp.einsum('bhk,bhkm->bhm', q_t * scale, hk)
                p = jax.nn.softmax(logits, axis=-1)
                hv = hv * ge[..., :, None] + s_t[..., :, None] * v_t[..., None, :]
                o_t = jnp.einsum('bhm,bhmv->bhv', p, hv)
                return ((hk, hv), o_t)
            init = (jnp.zeros((b, h, dk, m), q.dtype), jnp.zeros((b, h, m, dv), q.dtype))
            xs = tuple((jnp.moveaxis(a, 1, 0) for a in (q, k, v, s, g)))
            _, o = jax.lax.scan(step, init, xs)
            return jnp.moveaxis(o, 0, 1)
        key = jax.random.key(seed)
        ks = jax.random.split(key, 6)
        sc = lambda n: 1.0 / np.sqrt(n)
        return {'x': jax.random.normal(ks[0], (B, T, D), jnp.float32), 'Wq': jax.random.normal(ks[1], (D, H * K), jnp.float32) * sc(D), 'Wk': jax.random.normal(ks[2], (D, H * K), jnp.float32) * sc(D), 'Wv': jax.random.normal(ks[3], (D, H * V), jnp.float32) * sc(D), 'Wf': jax.random.normal(ks[4], (D, H * M), jnp.float32) * sc(D), 'g_norm_w': jnp.ones((V,), jnp.float32), 'Wo': jax.random.normal(ks[5], (H * V, D), jnp.float32) * sc(H * V)}
    _L0_attn_a_in = _L0_attn_a_setup()

    def _L0_attn_b_setup():
        import math
        import jax, jax.numpy as jnp
        import numpy as np
        D_MODEL = 128
        D_STATE = 64
        BATCH = 8
        SEQLEN = 256

        def _reference_tuple_inner(x, log_Lam_real, Lam_imag, B_real, B_imag, C_real, C_imag, D, log_dt, W_out, b_out):
            B, L, H = x.shape
            N = log_Lam_real.shape[0]
            dt = jnp.exp(log_dt)
            Lam_r = -jnp.exp(log_Lam_real)
            mag = jnp.exp(Lam_r * dt)
            Lbar_r = mag * jnp.cos(Lam_imag * dt)
            Lbar_i = mag * jnp.sin(Lam_imag * dt)
            Bu_r = jnp.einsum('blh,nh->bln', x, dt * B_real)
            Bu_i = jnp.einsum('blh,nh->bln', x, dt * B_imag)

            def step(carry, bu):
                sr, si = carry
                bur, bui = bu
                nr = Lbar_r * sr - Lbar_i * si + bur
                ni = Lbar_r * si + Lbar_i * sr + bui
                return ((nr, ni), (nr, ni))
            sr0 = jnp.zeros((B, N), dtype=x.dtype)
            si0 = jnp.zeros((B, N), dtype=x.dtype)
            (sr, si), (SR, SI) = jax.lax.scan(step, (sr0, si0), (jnp.swapaxes(Bu_r, 0, 1), jnp.swapaxes(Bu_i, 0, 1)))
            y = jnp.einsum('lbn,hn->blh', SR, C_real) - jnp.einsum('lbn,hn->blh', SI, C_imag) + D * x
            out = y @ W_out.T + b_out
            return (out, (sr, si))
        key = jax.random.key(seed)
        ks = jax.random.split(key, 8)
        x = jax.random.normal(ks[0], (BATCH, SEQLEN, D_MODEL), dtype=jnp.float32)
        log_Lam_real = jnp.log(0.5 * jnp.ones((D_STATE,), dtype=jnp.float32))
        Lam_imag = math.pi * jnp.arange(D_STATE, dtype=jnp.float32)
        B_real = 0.02 * jax.random.normal(ks[1], (D_STATE, D_MODEL), dtype=jnp.float32)
        B_imag = 0.02 * jax.random.normal(ks[2], (D_STATE, D_MODEL), dtype=jnp.float32)
        C_real = 0.02 * jax.random.normal(ks[3], (D_MODEL, D_STATE), dtype=jnp.float32)
        C_imag = 0.02 * jax.random.normal(ks[4], (D_MODEL, D_STATE), dtype=jnp.float32)
        Dp = jnp.ones((D_MODEL,), dtype=jnp.float32)
        log_dt = jnp.zeros((1,), dtype=jnp.float32)
        W_out = 0.02 * jax.random.normal(ks[5], (D_MODEL, D_MODEL), dtype=jnp.float32)
        b_out = jnp.zeros((D_MODEL,), dtype=jnp.float32)
        return {'x': x, 'log_Lam_real': log_Lam_real, 'Lam_imag': Lam_imag, 'B_real': B_real, 'B_imag': B_imag, 'C_real': C_real, 'C_imag': C_imag, 'D': Dp, 'log_dt': log_dt, 'W_out': W_out, 'b_out': b_out}
    _L0_attn_b_in = _L0_attn_b_setup()

    def _L0_ffn_setup():
        import jax, jax.numpy as jnp
        import numpy as np
        D_MODEL = 128
        D_FF = 512
        NUM_EXPERTS = 8
        TOP_K = 2
        BATCH = 4
        SEQ = 256
        key = jax.random.key(seed)
        ks = jax.random.split(key, 8)
        s = 0.02
        x = jax.random.normal(ks[0], (BATCH, SEQ, D_MODEL), dtype=jnp.float32)
        router_w = jax.random.normal(ks[1], (D_MODEL, NUM_EXPERTS), dtype=jnp.float32) * s
        router_b = jnp.zeros((NUM_EXPERTS,), dtype=jnp.float32)
        W1 = jax.random.normal(ks[2], (NUM_EXPERTS, D_MODEL, D_FF), dtype=jnp.float32) * s
        b1 = jnp.zeros((NUM_EXPERTS, D_FF), dtype=jnp.float32)
        W2 = jax.random.normal(ks[3], (NUM_EXPERTS, D_FF, D_MODEL), dtype=jnp.float32) * s
        b2 = jnp.zeros((NUM_EXPERTS, D_MODEL), dtype=jnp.float32)
        return {'x': x, 'router_w': router_w, 'router_b': router_b, 'W1': W1, 'b1': b1, 'W2': W2, 'b2': b2}
    _L0_ffn_in = _L0_ffn_setup()
    _d = {'L0_attn_a_x': _L0_attn_a_in['x'], 'L0_attn_a_Wq': _L0_attn_a_in['Wq'], 'L0_attn_a_Wk': _L0_attn_a_in['Wk'], 'L0_attn_a_Wv': _L0_attn_a_in['Wv'], 'L0_attn_a_Wf': _L0_attn_a_in['Wf'], 'L0_attn_a_g_norm_w': _L0_attn_a_in['g_norm_w'], 'L0_attn_a_Wo': _L0_attn_a_in['Wo'], 'L0_attn_b_log_Lam_real': _L0_attn_b_in['log_Lam_real'], 'L0_attn_b_Lam_imag': _L0_attn_b_in['Lam_imag'], 'L0_attn_b_B_real': _L0_attn_b_in['B_real'], 'L0_attn_b_B_imag': _L0_attn_b_in['B_imag'], 'L0_attn_b_C_real': _L0_attn_b_in['C_real'], 'L0_attn_b_C_imag': _L0_attn_b_in['C_imag'], 'L0_attn_b_D': _L0_attn_b_in['D'], 'L0_attn_b_log_dt': _L0_attn_b_in['log_dt'], 'L0_attn_b_W_out': _L0_attn_b_in['W_out'], 'L0_attn_b_b_out': _L0_attn_b_in['b_out'], 'L0_ffn_router_w': _L0_ffn_in['router_w'], 'L0_ffn_router_b': _L0_ffn_in['router_b'], 'L0_ffn_W1': _L0_ffn_in['W1'], 'L0_ffn_b1': _L0_ffn_in['b1'], 'L0_ffn_W2': _L0_ffn_in['W2'], 'L0_ffn_b2': _L0_ffn_in['b2']}
    _x0 = _d['L0_attn_a_x']
    _d['L0_attn_a_x'] = jax.random.normal(jax.random.fold_in(jax.random.key(seed), 1), (2, 1024, 128), dtype=_x0.dtype)
    del _x0
    return _d

def reference(L0_attn_a_x, L0_attn_a_Wq, L0_attn_a_Wk, L0_attn_a_Wv, L0_attn_a_Wf, L0_attn_a_g_norm_w, L0_attn_a_Wo, L0_attn_b_log_Lam_real, L0_attn_b_Lam_imag, L0_attn_b_B_real, L0_attn_b_B_imag, L0_attn_b_C_real, L0_attn_b_C_imag, L0_attn_b_D, L0_attn_b_log_dt, L0_attn_b_W_out, L0_attn_b_b_out, L0_ffn_router_w, L0_ffn_router_b, L0_ffn_W1, L0_ffn_b1, L0_ffn_W2, L0_ffn_b2):

    def _L0_attn_a_ref(x, Wq, Wk, Wv, Wf, g_norm_w, Wo):
        import jax, jax.numpy as jnp
        import numpy as np
        B, T, D = (4, 256, 128)
        H = 4
        K = D // H
        V = D // H
        M = 64
        GATE_LOGIT_NORMALIZER = 8.0
        NORM_EPS = 1e-05

        def _swish(x):
            return x * jax.nn.sigmoid(x)

        def _gsa_recurrence(q, k, v, s, g, scale):
            b, t, h, dk = q.shape
            dv = v.shape[-1]
            m = s.shape[-1]

            def step(carry, inp):
                hk, hv = carry
                q_t, k_t, v_t, s_t, g_t = inp
                ge = jnp.exp(g_t)
                hk = hk * ge[:, :, None, :] + k_t[..., :, None] * s_t[..., None, :]
                logits = jnp.einsum('bhk,bhkm->bhm', q_t * scale, hk)
                p = jax.nn.softmax(logits, axis=-1)
                hv = hv * ge[..., :, None] + s_t[..., :, None] * v_t[..., None, :]
                o_t = jnp.einsum('bhm,bhmv->bhv', p, hv)
                return ((hk, hv), o_t)
            init = (jnp.zeros((b, h, dk, m), q.dtype), jnp.zeros((b, h, m, dv), q.dtype))
            xs = tuple((jnp.moveaxis(a, 1, 0) for a in (q, k, v, s, g)))
            _, o = jax.lax.scan(step, init, xs)
            return jnp.moveaxis(o, 0, 1)
        b, t, d = x.shape
        q = _swish((x @ Wq).reshape(b, t, H, K))
        k = _swish((x @ Wk).reshape(b, t, H, K))
        v = (x @ Wv).reshape(b, t, H, V)
        f = jax.nn.log_sigmoid((x @ Wf).reshape(b, t, H, M)) / GATE_LOGIT_NORMALIZER
        s = 1.0 - jnp.exp(f)
        o = _gsa_recurrence(q, k, v, s, f, scale=K ** (-0.5))
        o = o * jax.lax.rsqrt(jnp.mean(o * o, axis=-1, keepdims=True) + NORM_EPS) * g_norm_w
        return o.reshape(b, t, H * V) @ Wo

    def _L0_attn_b_ref(x, log_Lam_real, Lam_imag, B_real, B_imag, C_real, C_imag, D, log_dt, W_out, b_out):
        import math
        import jax, jax.numpy as jnp
        import numpy as np
        D_MODEL = 128
        D_STATE = 64
        BATCH = 8
        SEQLEN = 256

        def _reference_tuple_inner(x, log_Lam_real, Lam_imag, B_real, B_imag, C_real, C_imag, D, log_dt, W_out, b_out):
            B, L, H = x.shape
            N = log_Lam_real.shape[0]
            dt = jnp.exp(log_dt)
            Lam_r = -jnp.exp(log_Lam_real)
            mag = jnp.exp(Lam_r * dt)
            Lbar_r = mag * jnp.cos(Lam_imag * dt)
            Lbar_i = mag * jnp.sin(Lam_imag * dt)
            Bu_r = jnp.einsum('blh,nh->bln', x, dt * B_real)
            Bu_i = jnp.einsum('blh,nh->bln', x, dt * B_imag)

            def step(carry, bu):
                sr, si = carry
                bur, bui = bu
                nr = Lbar_r * sr - Lbar_i * si + bur
                ni = Lbar_r * si + Lbar_i * sr + bui
                return ((nr, ni), (nr, ni))
            sr0 = jnp.zeros((B, N), dtype=x.dtype)
            si0 = jnp.zeros((B, N), dtype=x.dtype)
            (sr, si), (SR, SI) = jax.lax.scan(step, (sr0, si0), (jnp.swapaxes(Bu_r, 0, 1), jnp.swapaxes(Bu_i, 0, 1)))
            y = jnp.einsum('lbn,hn->blh', SR, C_real) - jnp.einsum('lbn,hn->blh', SI, C_imag) + D * x
            out = y @ W_out.T + b_out
            return (out, (sr, si))
        return _reference_tuple_inner(x, log_Lam_real, Lam_imag, B_real, B_imag, C_real, C_imag, D, log_dt, W_out, b_out)[0]

    def _L0_ffn_ref(x, router_w, router_b, W1, b1, W2, b2):
        import jax, jax.numpy as jnp
        import numpy as np
        D_MODEL = 128
        D_FF = 512
        NUM_EXPERTS = 8
        TOP_K = 2
        BATCH = 4
        SEQ = 256
        logits = jnp.einsum('bsd,de->bse', x, router_w) + router_b
        topk_scores, topk_idx = jax.lax.top_k(logits, TOP_K)
        topk_gates = jax.nn.softmax(topk_scores, axis=-1)
        onehot = jax.nn.one_hot(topk_idx, NUM_EXPERTS, dtype=x.dtype)
        combine = jnp.einsum('bsk,bske->bse', topk_gates, onehot)
        combine_e = jnp.moveaxis(combine, -1, 0)

        def expert_step(acc, params):
            w1, bb1, w2, bb2, c = params
            h = jax.nn.relu(jnp.einsum('bsd,df->bsf', x, w1) + bb1)
            y = jnp.einsum('bsf,fd->bsd', h, w2) + bb2
            return (acc + y * c[..., None], None)
        out, _ = jax.lax.scan(expert_step, jnp.zeros_like(x), (W1, b1, W2, b2, combine_e))
        return out
    x = L0_attn_a_x
    x = x + _L0_attn_a_ref(_layernorm(x, axis=-1), L0_attn_a_Wq, L0_attn_a_Wk, L0_attn_a_Wv, L0_attn_a_Wf, L0_attn_a_g_norm_w, L0_attn_a_Wo)
    x = x + _L0_ffn_ref(_layernorm(x, axis=-1), L0_ffn_router_w, L0_ffn_router_b, L0_ffn_W1, L0_ffn_b1, L0_ffn_W2, L0_ffn_b2)
    x = x + _L0_attn_b_ref(_layernorm(x, axis=-1), L0_attn_b_log_Lam_real, L0_attn_b_Lam_imag, L0_attn_b_B_real, L0_attn_b_B_imag, L0_attn_b_C_real, L0_attn_b_C_imag, L0_attn_b_D, L0_attn_b_log_dt, L0_attn_b_W_out, L0_attn_b_b_out)
    x = x + _L0_ffn_ref(_layernorm(x, axis=-1), L0_ffn_router_w, L0_ffn_router_b, L0_ffn_W1, L0_ffn_b1, L0_ffn_W2, L0_ffn_b2)
    return x

_drawn_inputs = setup_inputs


def setup_inputs(seed=0):
    import zlib

    import numpy as np

    out = dict(_drawn_inputs(seed))
    spreads = {'L0_attn_a_g_norm_w': (1.0, 0.2),
     'L0_attn_b_log_Lam_real': (-0.6931471824645996, 0.6),
     'L0_attn_b_D': (1.0, 0.599),
     'L0_attn_b_b_out': (0.0, 0.1),
     'L0_ffn_router_b': (0.0, 0.1),
     'L0_ffn_b1': (0.0, 0.281),
     'L0_ffn_b2': (0.0, 0.1)}
    factors = {'L0_attn_a_Wq': 5.49,
     'L0_attn_a_Wk': 5.035,
     'L0_attn_b_Lam_imag': 64.0,
     'L0_attn_b_B_real': 5.828,
     'L0_attn_b_B_imag': 5.936,
     'L0_attn_b_C_real': 5.871,
     'L0_attn_b_C_imag': 5.958}
    for name, (base, spread) in spreads.items():
        noise = np.random.default_rng([zlib.crc32(name.encode()), seed]).standard_normal(out[name].shape)
        drawn = base * np.exp(spread * noise) if base else spread * noise
        out[name] = jnp.asarray(drawn.astype(out[name].dtype))
    for name, factor in factors.items():
        out[name] = (out[name] * factor).astype(out[name].dtype)
    return out
```

```python
from contextlib import ExitStack

import numpy as np

import concourse.bass as bass
from concourse import mybir

F32 = mybir.dt.float32
U32 = mybir.dt.uint32
I32 = mybir.dt.int32
ALU = mybir.AluOpType
ACT = mybir.ActivationFunctionType
AX_X = mybir.AxisListType.X

P = 128
B = 2
T = 1024
D = 128
H = 4
K = D // H
M = 64
C = 64
NCHUNK = T // C
NPAIR = NCHUNK // 2
GATE_NORM = 8.0
EPS = 1e-5
E = 8
FF = 512
FB = FF // P
N = 64
NTILE = B * T * 2 // P + E
GROUP = 4
NGROUP = NTILE // GROUP
REGION = B * T + P
SPARE = E * REGION - (NTILE - E) * P
ROWS = E * REGION + E * P
LN_MAX = float(2 ** 60)
TWO_PI_1 = 6.28125
TWO_PI_2 = round((2 * np.pi - TWO_PI_1) * 2 ** 20) / 2 ** 20
TWO_PI_3 = 2 * np.pi - TWO_PI_1 - TWO_PI_2
ROUND = 12582912.0
LEVELS = 10
BIN_AT, ANGLES_AT, MAPS_AT = 4, 17, 44


class Names:
    pass


def constants():
    p = np.arange(P)
    b, t = p // C, p % C
    same = b[:, None] == b[None, :]
    mid = t <= C // 2 - 1
    cols = {
        "ident": np.eye(P),
        "cum": -1 / GATE_NORM * same * ((t[:, None] <= t[None, :]) * 1.0 - mid[:, None] * 1.0),
        "causal": (t[:, None] <= np.arange(C)[None, :]) * 1.0,
        "spans": -1 / GATE_NORM * np.stack([(b == 0) & ~mid, (b == 0) & mid, (b == 1) & ~mid, (b == 1) & mid], 1),
        "earlier": (p[:, None] < p[None, :]) * 1.0,
        "ones": np.ones((P, P)),
        "experts": np.tile(np.arange(E), (P, 1)),
        "base": np.tile(np.arange(E) * REGION, (P, 1)),
        "tiles": np.tile(np.arange(NTILE), (P, 1)),
        "tile_rows": np.tile(np.arange(NTILE) * P, (P, 1)),
        "digits": np.tile(float(E) ** (np.arange(NTILE + GROUP) % GROUP), (P, 1)),
        "powers": np.tile(2.0 ** np.arange(LEVELS), (P, 1)),
        "sign": np.where(p < N, 1.0, -1.0)[:, None],
    }
    at, where = 0, {}
    for name, a in cols.items():
        where[name] = (at, at + a.shape[1])
        at += a.shape[1]
    return np.concatenate(list(cols.values()), 1).astype(np.float32), where


def wait(eng, sem, count):
    if isinstance(count, int) and count <= 0:
        return
    eng.wait_ge(sem, count)


def wait_apart(eng, sem, count, reached):
    eng.wait_ge(reached, 1)
    wait(eng, sem, count)


class Pair:

    def __init__(self, n, half, par):
        self.n, self.half, self.par = n, half, par

    def step(self, k):
        return Pair(self.n + k, self.half + (self.par + k) // 2, (self.par + k) % 2)


def over_pairs(eng, body):
    for n in range(3):
        body(Pair(n, n // 2, n % 2))
    with eng.Fori(1, NPAIR // 2 - 1) as i:
        body(Pair(i * 2 + 1, i, 1))
        body(Pair(i * 2 + 2, i + 1, 0))
    body(Pair(NPAIR - 1, (NPAIR - 1) // 2, (NPAIR - 1) % 2))


FIRST, LAST = Pair(0, 0, 0), Pair(NPAIR - 1, (NPAIR - 1) // 2, (NPAIR - 1) % 2)


def is_first(pair):
    return isinstance(pair.n, int) and pair.n == 0


def is_last(pair):
    return isinstance(pair.n, int) and pair.n == NPAIR - 1


def semaphores(ctx, nc, prefix, names):
    sems = [nc.alloc_semaphore(name=prefix + n) for n in names.split()]
    ctx.callback(nc.clear_and_free_semaphores, sems)
    return sems


def memory(ctx, nc):
    def sb(name, *free, dt=F32):
        return ctx.enter_context(nc.sbuf_tensor(name, [P, *free], dt))

    _, where = constants()
    width = max(b for _, b in where.values())
    m = Names()
    m.const = sb("const", width)
    m.c = {name: m.const[:, a:b] for name, (a, b) in where.items()}
    m.psum = ctx.enter_context(nc.psum_tensor("banks", [P, 8, 512], F32))
    m.bank = [m.psum[:, i, :] for i in range(8)]
    m.bank12 = m.psum[:, 1:3, :]

    m.x = sb("x_rows", NCHUNK * D)

    m.w_zkv = sb("w_zkv", 512)
    m.w_q = sb("w_q", D)
    m.w_qk = sb("w_qk", 2, 2, 2 * K)
    m.w_o = sb("w_o", D)
    m.g_norm = sb("g_norm", 1)
    m.w_router = sb("w_router", E)
    m.b_router = sb("b_router", E)
    m.w1 = sb("w1", E * FF)
    m.b1_rows = sb("b1_rows", P)
    m.b1 = sb("b1", E * FB)
    m.b2 = sb("b2_all", E * D)
    m.w2 = sb("w2", E * FB * D)
    m.b_in = sb("b_in", D)
    m.b_in_t = sb("b_in_t", P)
    m.b_in_swap = sb("b_in_swap", P)
    m.c_mats = sb("c_mats", 2 * P)
    m.w_out = sb("w_out", D)
    m.w_out_t = sb("w_out_t", D)
    m.out_cos = sb("out_cos", D)
    m.out_sin = sb("out_sin", D)
    m.out_x = sb("out_x", D)
    m.d_col = sb("d_col", 1)
    m.b_out = sb("b_out_rows", D)
    m.lam = sb("lam", 4)
    m.mag = sb("mag", P)
    m.cos = sb("cos_table", T)
    m.sin = sb("sin_table", T)
    m.gates = sb("gates", NPAIR * 4)
    m.chosen = sb("chosen", NPAIR * 4)
    m.slot_of = sb("slot_of", NPAIR * 4)
    m.slots = sb("slots", NPAIR * 4, dt=U32)
    m.next_slot = sb("next_slot", E)
    m.plan = sb("plan", NTILE + NGROUP + E, dt=I32)
    m.zero = sb("zero_rows", D)
    return m


def setup(nc, m, a, dram):
    with ExitStack() as ctx:
        def sb(name, *free, dt=F32):
            return ctx.enter_context(nc.sbuf_tensor(name, [P, *free], dt))

        s = Names()
        s.const_in, s.attn_in, s.x_in, s.expert_in, s.route_in, s.space_in, s.zero = \
            semaphores(ctx, nc, "su_", "const_in attn_in x_in expert_in route_in space_in zero")
        s.zeroed, s.g_norm_w, s.dve, s.act, s.pe = \
            semaphores(ctx, nc, "su_", "zeroed g_norm_w dve act pe")
        th = sb("su_theta", 2)
        ang = sb("su_angles", LEVELS)
        turns = sb("su_turns", LEVELS)
        half = sb("su_half_sine", LEVELS)
        wc = sb("su_level_cos", LEVELS)
        ws = sb("su_level_sin", LEVELS)
        wn = sb("su_level_negated_sin", LEVELS)
        tmp = sb("su_product", T)
        tmp2 = sb("su_product2", T)
        eL = sb("su_decay_rate", 2)

        block = ctx.enter_context(nc.Block())

        @block.sync
        def _(sp):
            sp.dma_start(m.const[:], a["constants"]).then_inc(s.const_in, 16)
            for b in range(B):
                sp.dma_start(m.x[C * b:C * b + C, :].rearrange("p (c d) -> p c d", d=D),
                             a["L0_attn_a_x"][b].rearrange("(c t) d -> t c d", t=C)).then_inc(s.x_in, 16)
            for w, (lo, hi) in (("Wf", (0, 256)), ("Wk", (256, 384)), ("Wv", (384, 512))):
                sp.dma_start(m.w_zkv[:, lo:hi], a["L0_attn_a_" + w]).then_inc(s.attn_in, 16)
            sp.dma_start(m.w_q[:], a["L0_attn_a_Wq"]).then_inc(s.attn_in, 16)
            sp.dma_start(m.w_o[:], a["L0_attn_a_Wo"]).then_inc(s.attn_in, 16)
            g = a["L0_attn_a_g_norm_w"].rearrange("(v o) -> v o", o=1)
            for h in range(H):
                sp.dma_start(m.g_norm[K * h:K * h + K, :], g).then_inc(s.attn_in, 16)
            sp.dma_start(m.w_router[:], a["L0_ffn_router_w"]).then_inc(s.route_in, 16)
            sp.dma_start(m.b_router[0:1, :], a["L0_ffn_router_b"].rearrange("(o e) -> o e", o=1)).then_inc(s.route_in, 16)
            for i, side in enumerate(("real", "imag")):
                half_ = slice(N * i, N * i + N)
                for col, name in ((0, "log_Lam_real"), (1, "Lam_imag")):
                    sp.dma_start(m.lam[half_, col:col + 1],
                                 a["L0_attn_b_" + name].rearrange("(n o) -> n o", o=1)).then_inc(s.space_in, 16)
                sp.dma_start(m.b_in[half_, :], a["L0_attn_b_B_" + side]).then_inc(s.space_in, 16)
                sp.dma_start(m.c_mats[:, half_], a["L0_attn_b_C_" + side]).then_inc(s.space_in, 16)
            sp.dma_start(m.lam[:, 2:3], a["L0_attn_b_log_dt"].partition_broadcast(P)).then_inc(s.space_in, 16)
            sp.dma_start(m.w_out[:], a["L0_attn_b_W_out"]).then_inc(s.space_in, 16)
            sp.dma_start(m.d_col[:], a["L0_attn_b_D"].rearrange("(h o) -> h o", o=1)).then_inc(s.space_in, 16)
            sp.dma_start(m.b_out[:], a["L0_attn_b_b_out"].partition_broadcast(P)).then_inc(s.space_in, 16)
            sp.dma_start(m.w1[:].rearrange("p (e f) -> p e f", e=E),
                         a["L0_ffn_W1"].rearrange("e d f -> d e f")).then_inc(s.expert_in, 16)
            for e in range(E):
                sp.dma_start(m.w2[:, e * FF:(e + 1) * FF].rearrange("f (k d) -> f k d", k=FB),
                             a["L0_ffn_W2"][e].rearrange("(k f) d -> f k d", f=P)).then_inc(s.expert_in, 16)
            sp.dma_start(m.b1_rows[0:E * FB, :], a["L0_ffn_b1"].rearrange("e (k f) -> (e k) f", f=P)).then_inc(s.expert_in, 16)
            sp.dma_start(m.b2[:], a["L0_ffn_b2"].rearrange("e d -> (e d)").partition_broadcast(P)).then_inc(s.expert_in, 16)
            sp.wait_ge(s.zero, 1)
            for rows in dram.inputs:
                for i in range(E):
                    sp.dma_start(rows[E * REGION + i * P:E * REGION + (i + 1) * P, :], m.zero[:]).then_inc(s.zeroed, 16)
            sp.wait_ge(s.zeroed, 16 * E * len(dram.inputs))
            sp.wait_ge(s.x_in, 16 * B)
            sp.wait_ge(s.route_in, 32)

        @block.vector
        def _(dve):
            count = [0]

            def own(ins):
                count[0] += 1
                ins.then_inc(s.dve, 1)
                dve.wait_ge(s.dve, count[0])

            nc.vector.memset(m.zero[:], 0.0).then_inc(s.zero, 1)
            nc.vector.memset(m.mag[:], 1.0)
            nc.vector.memset(m.cos[:, 0:1], 1.0)
            own(nc.vector.memset(m.sin[:, 0:1], 0.0))
            dve.wait_ge(s.attn_in, 16 * (5 + H))
            own(nc.vector.tensor_scalar(m.w_o[:], m.w_o[:], m.g_norm[:], None, ALU.mult))
            for kind, w in enumerate((m.w_q[:], m.w_zkv[:, 256:384])):
                for e in range(2):
                    nc.vector.tensor_copy(m.w_qk[:, kind, e, :].rearrange("d (p k) -> d p k", p=2),
                                          w.rearrange("d (p e k) -> d p e k", p=2, e=2)[:, :, e, :])
            dve.wait_ge(s.const_in, 16)
            own(nc.vector.tensor_copy(m.next_slot[:], m.c["base"]))
            dve.wait_ge(s.space_in, 16 * 12)
            dve.wait_ge(s.act, 1)
            own(nc.vector.tensor_scalar(m.b_in[:], m.b_in[:], m.lam[:, 3:4], None, ALU.mult))
            own(nc.vector.tensor_tensor(th[:, 0:1], m.lam[:, 1:2], m.lam[:, 3:4], ALU.mult))

            def within_half_turn(x, k):
                own(nc.vector.tensor_scalar(k, x, float(1 / (2 * np.pi)), ROUND, ALU.mult, ALU.add))
                own(nc.vector.tensor_scalar(k, k, -ROUND, None, ALU.add))
                for part in (TWO_PI_1, TWO_PI_2, TWO_PI_3):
                    own(nc.vector.scalar_tensor_tensor(x, k, -part, x, ALU.mult, ALU.add))

            within_half_turn(th[:, 0:1], th[:, 1:2])
            own(nc.vector.tensor_scalar(ang[:], m.c["powers"], th[:, 0:1], None, ALU.mult))
            within_half_turn(ang[:], turns[:])
            own(nc.vector.tensor_scalar(ang[:], ang[:], 3.1415925, -3.1415925, ALU.min, ALU.max))
            angles_at = count[0]
            assert angles_at == ANGLES_AT
            dve.wait_ge(s.act, 6)
            own(nc.vector.tensor_tensor(wc[:], half[:], half[:], ALU.mult))
            own(nc.vector.tensor_scalar(wc[:], wc[:], -2.0, 1.0, ALU.mult, ALU.add))
            own(nc.vector.tensor_scalar(wn[:], ws[:], -1.0, None, ALU.mult))
            own(nc.vector.tensor_scalar(m.mag[:], m.mag[:], eL[:, 1:2], None, ALU.mult))
            for k in range(LEVELS):
                n = 2 ** k
                old, new = slice(0, n), slice(n, 2 * n)
                nc.vector.tensor_scalar(tmp[:, old], m.sin[:, old], wn[:, k:k + 1], None, ALU.mult)
                own(nc.vector.tensor_scalar(tmp2[:, old], m.cos[:, old], ws[:, k:k + 1], None, ALU.mult))
                nc.vector.scalar_tensor_tensor(m.cos[:, new], m.cos[:, old], wc[:, k:k + 1], tmp[:, old], ALU.mult, ALU.add)
                own(nc.vector.scalar_tensor_tensor(m.sin[:, new], m.sin[:, old], wc[:, k:k + 1], tmp2[:, old], ALU.mult, ALU.add))
            own(nc.vector.tensor_scalar(m.sin[:], m.sin[:], m.c["sign"], None, ALU.mult))
            nc.vector.tensor_copy(m.c_mats[:, 192:256], m.c_mats[:, 0:64])
            nc.vector.tensor_scalar(m.c_mats[:, 128:192], m.c_mats[:, 64:128], -1.0, None, ALU.mult)
            own(nc.vector.tensor_scalar(m.c_mats[:, 64:128], m.c_mats[:, 64:128], -1.0, None, ALU.mult))
            dve.wait_ge(s.pe, 1)
            nc.vector.tensor_copy(m.b_in_t[:], m.bank[0][:, 0:128])
            nc.vector.tensor_copy(m.b_in_swap[:, 0:64], m.bank[0][:, 64:128])
            nc.vector.tensor_copy(m.b_in_swap[:, 64:128], m.bank[0][:, 0:64])
            own(nc.vector.tensor_copy(m.w_out_t[:], m.bank[0][:, 128:256]))
            assert count[0] == MAPS_AT
            own(nc.vector.tensor_scalar(m.out_x[:], m.w_out_t[:], m.d_col[:], None, ALU.mult))
            dve.wait_ge(s.pe, 2)
            nc.vector.tensor_copy(m.out_cos[:], m.bank[1][:, 0:128])
            own(nc.vector.tensor_copy(m.out_sin[:], m.bank[1][:, 128:256]))
            dve.wait_ge(s.pe, 3)
            own(nc.vector.tensor_copy(m.b1[:], m.bank[2][:, 0:E * FB]))

        @block.scalar
        def _(act):
            act.wait_ge(s.space_in, 16 * 12)
            nc.scalar.activation(m.lam[:, 3:4], m.lam[:, 2:3], ACT.Exp).then_inc(s.act, 1)
            nc.scalar.activation(eL[:, 0:1], m.lam[:, 0:1], ACT.Exp).then_inc(s.act, 1)
            act.wait_ge(s.act, 2)
            nc.scalar.mul(eL[:, 0:1], eL[:, 0:1], m.lam[:, 3:4]).then_inc(s.act, 1)
            act.wait_ge(s.act, 3)
            nc.scalar.activation(eL[:, 1:2], eL[:, 0:1], ACT.Exp, scale=-1.0).then_inc(s.act, 1)
            act.wait_ge(s.dve, ANGLES_AT)
            nc.scalar.activation(ws[:], ang[:], ACT.Sin).then_inc(s.act, 1)
            nc.scalar.activation(half[:], ang[:], ACT.Sin, scale=0.5).then_inc(s.act, 1)

        @block.tensor
        def _(pe):
            pe.wait_ge(s.dve, BIN_AT)
            pe.transpose(m.bank[0][:, 0:128], m.b_in[:], m.c["ident"])
            pe.transpose(m.bank[0][:, 128:256], m.w_out[:], m.c["ident"]).then_inc(s.pe, 1)
            pe.wait_ge(s.dve, MAPS_AT)
            pe.matmul(m.bank[1][:, 0:128], m.c_mats[:, 0:128], m.w_out_t[:], start=True, stop=True)
            pe.matmul(m.bank[1][:, 128:256], m.c_mats[:, 128:256], m.w_out_t[:], start=True, stop=True).then_inc(s.pe, 1)
            pe.wait_ge(s.expert_in, 16 * (E + 3))
            pe.transpose(m.bank[2][:, 0:E * FB], m.b1_rows[0:E * FB, :], m.c["ident"][0:E * FB, 0:E * FB]).then_inc(s.pe, 1)


def chunk_rows(m, n, u):
    return m.x[:, bass.ds((n.n * 2 + u) * D, D)]


class Norm:

    def __init__(self, sb, name):
        self.stats = sb(name + "_stats", 2, 6)
        self.mv = sb(name + "_mv", 2, 2)
        self.ve = sb(name + "_var_eps", 2)
        self.rstd = sb(name + "_rstd", 2)
        self.carrier = sb(name + "_carrier", 1)


class Route:

    def __init__(self, ctx, nc, m, a, dram, prefix):
        def sb(name, *free, dt=F32):
            return ctx.enter_context(nc.sbuf_tensor(prefix + name, [P, *free], dt))

        self.nc, self.m = nc, m
        self.rows_out = dram.inputs[0] if prefix == "ra_" else dram.inputs[1]
        self.s = Names()
        self.s.stats, self.s.mv, self.s.var_eps, self.s.rstd, self.s.xn, self.s.x_t_ps, self.s.x_t = \
            semaphores(ctx, nc, prefix, "stats mv var_eps rstd xn x_t_ps x_t")
        self.s.logits_ps, self.s.logits, self.s.top, self.s.index, self.s.index_f, self.s.picks, self.s.marked = \
            semaphores(ctx, nc, prefix, "logits_ps logits top index index_f picks marked")
        self.s.margin, self.s.exp_margin, self.s.gate_sum, self.s.gate1, self.s.gates = \
            semaphores(ctx, nc, prefix, "margin exp_margin gate_sum gate1 gates")
        self.s.rank_ps, self.s.place, self.s.moved, self.s.picked, self.s.slot_f, self.s.slots = \
            semaphores(ctx, nc, prefix, "rank_ps place moved picked slot_f slots")
        self.s.scattered0, self.s.scattered1, self.s.plan = \
            semaphores(ctx, nc, prefix, "scattered0 scattered1 plan")
        self.s.planned, self.s.tails_out = \
            semaphores(ctx, nc, prefix, "planned tails_out")
        self.ln = Norm(sb, "ln")
        self.xn = [sb(f"xn{i}", 2, D) for i in range(2)]
        self.x_t = sb("x_t", 2, P)
        self.logits = sb("logits", 2, E)
        self.top = sb("top", 2, 8)
        self.index = sb("index", 2, 8, dt=U32)
        self.index_f = sb("index_f", 2, 2)
        self.picks = sb("picks", 2, 2, E)
        self.marked = sb("marked", 2, E)
        self.margin = sb("margin", 2)
        self.e_margin = sb("exp_margin", 2)
        self.gate_sum = sb("gate_sum", 2)
        self.gates = sb("gates", 2, 2)
        self.place = sb("place", 2, E)
        self.picked = sb("picked", 2, 2, E)
        self.carrier = sb("carrier", 1)
        self.slot_f = sb("slot_f", 4)
        self.slots = [sb(f"slots{i}", 4, dt=U32) for i in range(2)]
        self.count = sb("count", E)
        self.tiles = sb("expert_tiles", E)
        self.tiles_to = sb("tiles_up_to", E)
        self.cmp = sb("compare", NTILE, E)
        self.cmp_row = sb("compare_row", NPAIR * 4, E)
        self.lead = sb("lead", NPAIR * 4)
        self.owner = sb("owner", NTILE)
        self.digits = sb("digits", NTILE + GROUP)
        self.four = sb("four_digits", NGROUP + 1)
        self.three = sb("three_digits", NGROUP + 1)
        self.row = sb("row", NTILE)
        self.spare = sb("spare", NTILE)

    def scattered(self, par):
        return (self.s.scattered0, self.s.scattered1)[par]

    def vector_norm(self, dve, n):
        nc, s, ln = self.nc, self.s, self.ln
        wait(dve, self.x_written, n.n + 1)
        nc.vector.memset(ln.carrier[:], 0.0)
        for u in range(2):
            ins = nc.vector.bn_stats(ln.stats[:, u, :], chunk_rows(self.m, n, u))
        ins.then_inc(s.stats, 1)
        wait(dve, s.stats, n.n + 1)
        nc.vector.memset(ln.carrier[:], 0.0)
        for u in range(2):
            nc.vector.bn_aggr(ln.mv[:, u, :], ln.stats[:, u, :]).then_inc(s.mv, 1)
        wait(dve, s.mv, (n.n + 1) * 2)
        nc.vector.tensor_scalar(ln.ve[:], ln.mv[:, :, 1], EPS, None, ALU.add).then_inc(s.var_eps, 1)

    def gpsimd_norm(self, pool, n, minus_half):
        wait(pool, self.s.var_eps, n.n + 1)
        wait(pool, self.s.xn, n.n)
        self.nc.gpsimd.tensor_tensor(self.ln.rstd[:], self.ln.ve[:], minus_half[:, 0, 0:2], ALU.pow).then_inc(self.s.rstd, 1)

    def vector_normed(self, dve, n):
        wait(dve, self.s.rstd, n.n + 1)
        wait(dve, self.scattered(n.par), n.half * 64)
        for u in range(2):
            ins = self.nc.vector.tensor_scalar(self.xn[n.par][:, u, :], chunk_rows(self.m, n, u),
                                               self.ln.mv[:, u, 0:1], self.ln.rstd[:, u:u + 1], ALU.subtract, ALU.mult)
        ins.then_inc(self.s.xn, 1)

    def tensor_transposed(self, pe, n):
        m, s = self.m, self.s
        wait(pe, s.xn, n.n + 1)
        wait(pe, s.moved, n.n)
        for u in range(2):
            mm = pe.transpose(self.bank[:, P * u:P * u + P], self.xn[n.par][:, u, :], m.c["ident"])
        mm.then_inc(s.x_t_ps, 1)

    def tensor_logits(self, pe, n):
        m, s, bank = self.m, self.s, self.bank
        wait(pe, s.x_t, n.n + 1)
        for u in range(2):
            pe.matmul(bank[:, E * u:E * u + E], self.x_t[:, u, :], m.w_router[:], start=True, stop=False)
            mm = pe.matmul(bank[:, E * u:E * u + E], m.c["ones"][0:1, :], m.b_router[0:1, :], start=False, stop=True)
        mm.then_inc(s.logits_ps, 1)

    def tensor_ranks(self, pe, n):
        m, s, bank = self.m, self.s, self.bank
        wait(pe, s.marked, n.n + 1)
        pe.matmul(bank[:, 0:E], m.c["earlier"], self.marked[:, 0, :], start=True, stop=True)
        pe.matmul(bank[:, E:2 * E], m.c["earlier"], self.marked[:, 1, :], start=True, stop=False)
        pe.matmul(bank[:, E:2 * E], m.c["ones"], self.marked[:, 0, :], start=False, stop=True)
        pe.matmul(bank[:, 2 * E:3 * E], m.c["ones"], self.marked[:, 0, :], start=True, stop=False)
        pe.matmul(bank[:, 2 * E:3 * E], m.c["ones"], self.marked[:, 1, :], start=False, stop=True).then_inc(s.rank_ps, 1)

    def tensor(self, pe, n):
        self.tensor_transposed(pe, n)
        self.tensor_logits(pe, n)
        self.tensor_ranks(pe, n)

    def scalar_transposed(self, act, n):
        wait(act, self.s.x_t_ps, n.n + 1)
        wait(act, self.s.logits_ps, n.n)
        self.nc.scalar.copy(self.x_t[:].rearrange("p u t -> p (u t)"), self.bank[:, 0:256]).then_inc(self.s.x_t, 1)

    def scalar_margin(self, act, n):
        wait(act, self.s.margin, n.n + 1)
        wait(act, self.s.gates, n.n)
        self.nc.scalar.activation(self.e_margin[:], self.margin[:], ACT.Exp).then_inc(self.s.exp_margin, 1)

    def scalar(self, act, n):
        self.scalar_transposed(act, n)
        self.scalar_margin(act, n)

    def vector_choose(self, dve, n):
        nc, m, s = self.nc, self.m, self.s
        wait(dve, s.logits_ps, n.n + 1)
        nc.vector.tensor_copy(self.logits[:].rearrange("p u e -> p (u e)"),
                              self.bank[:, 0:2 * E]).then_inc(s.logits, 1)
        wait_apart(dve, s.logits, n.n + 1, self.ready)
        for u in range(2):
            nc.vector.max(self.top[:, u, :], self.logits[:, u, :]).then_inc(s.top, 1)
        wait(dve, s.top, (n.n + 1) * 2)
        nc.vector.tensor_tensor(self.margin[:], self.top[:, :, 1], self.top[:, :, 0], ALU.subtract).then_inc(s.margin, 1)
        for u in range(2):
            nc.vector.max_index(self.index[:, u, :], self.top[:, u, :], self.logits[:, u, :]).then_inc(s.index, 1)
        wait(dve, s.index, (n.n + 1) * 2)
        nc.vector.tensor_copy(self.index_f[:], self.index[:, :, 0:2]).then_inc(s.index_f, 1)
        wait(dve, s.index_f, n.n + 1)
        nc.vector.tensor_tensor(self.picks[:].rearrange("p u k e -> p (u k) e"),
                                m.c["experts"].unsqueeze(1).to_broadcast([P, 4, E]),
                                self.index_f[:].rearrange("p u k -> p (u k)").unsqueeze(2).to_broadcast([P, 4, E]),
                                ALU.is_equal).then_inc(s.picks, 1)
        nc.vector.tensor_copy(m.chosen[:, bass.ds(n.n * 4, 4)], self.index_f[:].rearrange("p u k -> p (u k)"))
        wait(dve, s.picks, n.n + 1)
        nc.vector.tensor_tensor(self.marked[:], self.picks[:, :, 0, :], self.picks[:, :, 1, :], ALU.add).then_inc(s.marked, 1)
        wait(dve, s.exp_margin, n.n + 1)
        nc.vector.tensor_scalar(self.gate_sum[:], self.e_margin[:], 1.0, None, ALU.add).then_inc(s.gate_sum, 1)
        wait(dve, s.gate_sum, n.n + 1)
        nc.vector.reciprocal(self.gates[:, :, 0], self.gate_sum[:]).then_inc(s.gate1, 1)
        wait(dve, s.gate1, n.n + 1)
        nc.vector.tensor_tensor(self.gates[:, :, 1], self.gates[:, :, 0], self.e_margin[:], ALU.mult).then_inc(s.gates, 1)
        wait(dve, s.gates, n.n + 1)
        nc.vector.memset(self.carrier[:], 0.0)
        nc.vector.tensor_copy(m.gates[:, bass.ds(n.n * 4, 4)], self.gates[:].rearrange("p u k -> p (u k)"))

    def vector_place(self, dve, n):
        nc, m, s = self.nc, self.m, self.s
        wait(dve, s.rank_ps, n.n + 1)
        nc.vector.tensor_tensor(self.place[:], self.bank[:, 0:2 * E].rearrange("p (u e) -> p u e", u=2),
                                m.next_slot[:].unsqueeze(1).to_broadcast([P, 2, E]), ALU.add).then_inc(s.place, 1)
        wait(dve, s.place, n.n + 1)
        nc.vector.tensor_tensor(m.next_slot[:], m.next_slot[:], self.bank[:, 2 * E:3 * E], ALU.add).then_inc(s.moved, 1)
        wait(dve, s.place, n.n + 1)
        for u in range(2):
            ins = nc.vector.tensor_tensor(self.picked[:, u], self.picks[:, u],
                                          self.place[:, u, :].unsqueeze(1).to_broadcast([P, 2, E]), ALU.mult)
        ins.then_inc(s.picked, 1)
        wait(dve, s.picked, n.n + 1)
        nc.vector.tensor_reduce(self.slot_f[:], self.picked[:].rearrange("p u k e -> p (u k) e"), AX_X,
                                ALU.add).then_inc(s.slot_f, 1)
        wait(dve, s.slot_f, n.n + 1)
        wait(dve, self.scattered(n.par), n.half * 64)
        nc.vector.tensor_copy(self.slots[n.par][:], self.slot_f[:]).then_inc(s.slots, 1)
        nc.vector.tensor_copy(m.slot_of[:, bass.ds(n.n * 4, 4)], self.slot_f[:])

    def gpsimd_scatter(self, pool, n):
        wait_apart(pool, self.s.slots, n.n + 1, self.ready)
        for u in range(2):
            for k in range(2):
                self.nc.gpsimd.indirect_dma_start(
                    self.rows_out[:, :], bass.IndirectOffsetOnAxis(ap=self.slots[n.par][:, 2 * u + k:2 * u + k + 1], axis=0),
                    self.xn[n.par][:, u, :], None).then_inc(self.scattered(n.par), 16)

    def gpsimd_wait(self, pool):
        for par in range(2):
            pool.wait_ge(self.scattered(par), 64 * (NPAIR // 2))

    def vector_plan(self, dve):
        nc, m, s = self.nc, self.m, self.s
        steps = [0]

        def own(ins):
            steps[0] += 1
            ins.then_inc(s.plan, 1)
            dve.wait_ge(s.plan, steps[0])

        dve.wait_ge(s.moved, NPAIR)
        own(nc.vector.tensor_tensor(self.count[:], m.next_slot[:], m.c["base"], ALU.subtract))
        own(nc.vector.tensor_scalar(self.tiles[:], self.count[:], 1.0 / P, 0.5 - 0.5 / P, ALU.mult, ALU.add))
        own(nc.vector.tensor_scalar(self.tiles[:], self.tiles[:], ROUND, None, ALU.add))
        own(nc.vector.tensor_scalar(self.tiles[:], self.tiles[:], -ROUND, None, ALU.add))
        own(nc.vector.tensor_tensor_scan(self.tiles_to[:], m.c["ones"][:, 0:E], self.tiles[:], 0.0, ALU.mult, ALU.add))
        by_tile = [P, NTILE, E]
        own(nc.vector.tensor_tensor(self.cmp[:], self.tiles_to[:].unsqueeze(1).to_broadcast(by_tile),
                                    m.c["tiles"].unsqueeze(2).to_broadcast(by_tile), ALU.is_le))
        own(nc.vector.tensor_reduce(self.owner[:], self.cmp[:], AX_X, ALU.add))
        own(nc.vector.tensor_tensor(self.tiles[:], self.tiles[:], self.tiles_to[:], ALU.subtract))
        own(nc.vector.scalar_tensor_tensor(self.tiles[:], self.tiles[:], float(P), m.c["base"], ALU.mult, ALU.add))
        own(nc.vector.tensor_tensor(self.cmp[:], self.owner[:].unsqueeze(2).to_broadcast(by_tile),
                                    m.c["experts"].unsqueeze(1).to_broadcast(by_tile), ALU.is_equal))
        own(nc.vector.tensor_tensor(self.cmp[:], self.cmp[:], self.tiles[:].unsqueeze(1).to_broadcast(by_tile), ALU.mult))
        own(nc.vector.tensor_reduce(self.row[:], self.cmp[:], AX_X, ALU.add))
        own(nc.vector.tensor_tensor(self.row[:], self.row[:], m.c["tile_rows"], ALU.add))
        own(nc.vector.tensor_scalar(self.spare[:], self.owner[:], float(E), float(SPARE), ALU.is_equal, ALU.mult))
        own(nc.vector.tensor_tensor(self.row[:], self.row[:], self.spare[:], ALU.add))
        by_row = [P, NPAIR * 4, E]
        own(nc.vector.tensor_tensor(self.cmp_row[:], m.chosen[:].unsqueeze(2).to_broadcast(by_row),
                                    m.c["experts"].unsqueeze(1).to_broadcast(by_row), ALU.is_equal))
        own(nc.vector.tensor_tensor(self.cmp_row[:], self.cmp_row[:], self.tiles[:].unsqueeze(1).to_broadcast(by_row), ALU.mult))
        own(nc.vector.tensor_reduce(self.lead[:], self.cmp_row[:], AX_X, ALU.add))
        nc.vector.tensor_tensor(m.slots[:], m.slot_of[:], self.lead[:], ALU.subtract)
        nc.vector.tensor_copy(m.plan[:, 0:NTILE], self.row[:])
        own(nc.vector.memset(self.digits[:], 0.0))
        own(nc.vector.scalar_tensor_tensor(self.digits[:, 0:NTILE], self.owner[:], float(E - 1), m.c["digits"][:, 0:NTILE],
                                           ALU.min, ALU.mult))
        by_group = self.digits[:].rearrange("p (q k) -> p q k", k=GROUP)
        own(nc.vector.tensor_reduce(self.four[:], by_group, AX_X, ALU.add))
        own(nc.vector.tensor_reduce(self.three[:], by_group[:, :, 0:3], AX_X, ALU.add))
        nc.vector.scalar_tensor_tensor(m.plan[:, NTILE:NTILE + NGROUP], self.three[:, 1:], float(E ** GROUP),
                                       self.four[:, 0:NGROUP], ALU.mult, ALU.add)
        nc.vector.tensor_copy(m.plan[:, NTILE + NGROUP:], m.next_slot[:]).then_inc(s.planned, 1)

    def sync_tails(self, sp):
        sp.wait_ge(self.s.planned, 1)
        for e in range(E):
            row = sp.value_load(self.m.plan[0:1, NTILE + NGROUP + e:NTILE + NGROUP + e + 1], min_val=e * REGION,
                                max_val=e * REGION + B * T)
            sp.dma_start(self.rows_out[bass.ds(row, P), :], self.m.zero[:]).then_inc(self.s.tails_out, 16)
        sp.wait_ge(self.s.tails_out, 16 * E)


def attention_and_route(nc, m, a, dram):
    with ExitStack() as ctx:
        def sb(name, *free, dt=F32):
            return ctx.enter_context(nc.sbuf_tensor("at_" + name, [P, *free], dt))

        def sb2(name, *free, dt=F32):
            return [sb(f"{name}{i}", *free, dt=dt) for i in range(2)]

        s = Names()
        s.stats, s.mv, s.var_eps, s.rstd, s.xn, s.x_t_ps, s.x_t = \
            semaphores(ctx, nc, "at_", "stats mv var_eps rstd xn x_t_ps x_t")
        s.z_ps, s.qk_ps, s.exp_z, s.exp_kqk, s.capped, s.log1, s.soft = \
            semaphores(ctx, nc, "at_", "z_ps qk_ps exp_z exp_kqk capped log1 soft")
        s.ge_ready, s.v_ready, s.sig_sum, s.sig, s.k_ready, s.q_ready, s.kt_ready = \
            semaphores(ctx, nc, "at_", "ge_ready v_ready sig_sum sig k_ready q_ready kt_ready")
        s.g_ps, s.d_ps, s.d_sb, s.decays, s.s_ready, s.a_ps, s.a_sb = \
            semaphores(ctx, nc, "at_", "g_ps d_ps d_sb decays s_ready a_ps a_sb")
        s.st_ps, s.st_sb, s.u_ps, s.t0, s.st1, s.t1, s.d01 = \
            semaphores(ctx, nc, "at_", "st_ps st_sb u_ps t0 st1 t1 d01")
        s.st0, s.sk_ps, s.sk_sb, s.r_ps, s.logits, s.maxes, s.shifted = \
            semaphores(ctx, nc, "at_", "st0 sk_ps sk_sb r_ps logits maxes shifted")
        s.probs, s.sums, s.pw, s.pt_ps, s.pt_sb, s.b_ps, s.b_sb = \
            semaphores(ctx, nc, "at_", "probs sums pw pt_ps pt_sb b_ps b_sb")
        s.o_ps, s.sq, s.ms, s.s2, s.oe, s.o_rstd, s.on = \
            semaphores(ctx, nc, "at_", "o_ps sq ms s2 oe o_rstd on")
        s.ot_ps, s.ot_sb, s.y_ps, s.x1, s.d10, s.const_ready, s.q_spread = \
            semaphores(ctx, nc, "at_", "ot_ps ot_sb y_ps x1 d10 const_ready q_spread")
        s.zeros_ready, = \
            semaphores(ctx, nc, "at_", "zeros_ready")
        r = Route(ctx, nc, m, a, dram, "ra_")
        ln = Norm(sb, "ln")
        xn = sb("xn", 2, D)
        x_t = sb("x_t", 2, P)
        exp_z = sb("exp_z", 2, 256)
        exp_kqk = sb("exp_kqk", 768)
        sig = sb("sigmoid", 768)
        soft = sb("softplus", 2, 256)
        ge = sb("ge", 2, 256)
        e_minus = sb("e_minus", 2, 256)
        e_plus = sb2("e_plus", 2, 256)
        slot = sb2("slot", 2, 256)
        kv = sb2("kv", 2, H, 2, B, K)
        q_raw = sb("q_raw", 2, 2, C)
        q_t = sb2("q_t", 2, 2, 2, P)
        k_t = sb2("k_t", 2, 2, C)
        d_sb = sb2("span_decays", 2, 2, 2, 2)
        a_sb = sb("a_masked", 2, 2, 2, C)
        st_sb = sb("slot_t", 2, 2, P)
        st0, st1 = sb("state_even", 2, 2, 2, K), sb("state_odd", 2, 2, 2, K)
        t0, t1 = sb("sum_even", 2, 2, 2, K), sb("sum_odd", 2, 2, 2, K)
        d01 = sb("decay_even", 2, 2)
        d10 = sb("decay_odd", 2, 2)
        sk_sb = sb2("state_k_t", P)
        logits = sb("logits", 2, H, M)
        maxes = sb("maxes", 2, H)
        probs = sb("probs", 2, H, M)
        sums = sb("sums", 2, H)
        pw = sb("weights", 2, H * M)
        pt_sb = sb("weights_t", 2, 2, 2, P)
        b_sb = sb("b_masked", 2, H, C)
        sq = sb("squares", 2, H, K)
        ms = sb("mean_squares", 2, H)
        s2 = sb("sums_squared", 2, H)
        o_rstd = sb("o_rstd", 2, H)
        minus_half = sb("minus_half", 2, H)
        on = sb("o_normed", 2, D)
        ot_sb = sb("o_t", 2, P)

        r.bank, r.ready, r.x_written = m.bank[7], s.const_ready, s.x1
        xt_ps = m.bank[0]
        z_ps = m.bank12
        qk_ps = m.bank[3]
        e_ps = m.bank[4]
        f_ps = m.bank[5]
        g_ps = m.bank[6]
        h_ps = m.bank[7]

        block = ctx.enter_context(nc.Block())

        @block.tensor
        def _(pe):
            def x_transposed(n):
                wait(pe, s.xn, n.n + 1)
                wait(pe, s.decays, n.n)
                for u in range(2):
                    mm = pe.transpose(xt_ps[:, P * u:P * u + P], xn[:, u, :], m.c["ident"])
                mm.then_inc(s.x_t_ps, 1)

            def project(n):
                wait(pe, s.x_t, n.n + 1)
                wait(pe, s.soft, n.n)
                wait(pe, s.k_ready, n.n)
                for u in range(2):
                    mm = pe.matmul(z_ps[:, u, :], x_t[:, u, :], m.w_zkv[:], start=True, stop=True)
                mm.then_inc(s.z_ps, 1)
                wait(pe, s.kt_ready, n.n)
                for kind in range(2):
                    for e in range(2):
                        for b in range(B):
                            mm = pe.matmul(qk_ps[64 * b:64 * b + 64, 256 * kind + 128 * e:256 * kind + 128 * e + 128]
                                           .rearrange("p (u t) -> p u t", u=2),
                                           m.w_qk[:, kind, e, :],
                                           x_t[:, :, C * b:C * b + C], start=True, stop=True)
                mm.then_inc(s.qk_ps, 1)

            def gate_sums(n):
                wait(pe, s.soft, n.n + 1)
                wait(pe, s.x_t, n.n + 1)
                for u in range(2):
                    mm = pe.matmul(xt_ps[:, 256 * u:256 * u + 256], m.c["cum"], soft[:, u, :], start=True, stop=True)
                mm.then_inc(s.g_ps, 1)
                for u in range(2):
                    for p in range(2):
                        mm = pe.matmul(h_ps[:, 8 * u:8 * u + 8].rearrange("s (b k p) -> s b k p", b=2, k=2)[:, :, :, p],
                                       soft[:, u, P * p:P * p + P], m.c["spans"], start=True, stop=True)
                mm.then_inc(s.d_ps, 1)

            def attend(n):
                wait(pe, s.kt_ready, n.n + 1)
                wait(pe, s.q_spread, n.n + 1)
                wait(pe, s.sq, n.n)
                wait(pe, s.on, n.n)
                for u in range(2):
                    for e in range(2):
                        for b in range(B):
                            at = 256 * u + 128 * e
                            mm = pe.matmul(e_ps[64 * b:64 * b + 64, at:at + 128].rearrange("j (p t) -> j p t", p=2),
                                           k_t[n.par][:, e, u, :], q_t[n.par][:, u, e, :, C * b:C * b + C],
                                           start=True, stop=True)
                mm.then_inc(s.a_ps, 1)

            def state_transposed(n, u):
                state = (st0, st1)[u]
                if u == 0:
                    wait(pe, s.st0, n.n + 1)
                else:
                    wait(pe, s.st1, n.n + 1)
                    wait(pe, s.sk_sb, n.n * 2 + 1)
                pe.transpose(h_ps[:, 0:P], state[:, 0].rearrange("p b h k -> p (b h k)"), m.c["ident"]).then_inc(s.sk_ps, 1)

            def slots_transposed(n):
                wait(pe, s.s_ready, n.n + 1)
                wait(pe, s.ot_sb, n.n)
                for u in range(2):
                    for p in range(2):
                        at = 256 * u + P * p
                        mm = pe.transpose(f_ps[:, at:at + P], slot[n.par][:, u, P * p:P * p + P], m.c["ident"])
                mm.then_inc(s.st_ps, 1)

            def updates(n):
                wait(pe, s.k_ready, n.n + 1)
                wait(pe, s.v_ready, n.n + 1)
                wait(pe, s.x1, n.n)
                for u in range(2):
                    for h in range(H):
                        out = (g_ps[64 * (h % 2):64 * (h % 2) + 64, 256 * u:256 * u + 256]
                               .rearrange("s (c b p k) -> s c b p k", c=2, b=2, p=2)[:, :, :, h // 2, :])
                        mm = pe.matmul(out, slot[n.par][:, u, M * h:M * h + M], kv[n.par][:, u, h], start=True, stop=True)
                mm.then_inc(s.u_ps, 1)

            def raw_logits(n, u):
                if u == 0:
                    wait(pe, s.a_sb, n.n + 1)
                wait(pe, s.sk_sb, n.n * 2 + u + 1)
                for h in range(H):
                    at, e = 256 * u + M * h, h % 2
                    pe.matmul(e_ps[:, at:at + M], q_t[n.par][:, u, e, h // 2, :], sk_sb[u][:, M * e:M * e + M],
                              start=(u == 0 and h == 0), stop=False, skip_group_check=True)
                for b in range(B):
                    for h in range(H):
                        rows, at = slice(64 * b, 64 * b + 64), 256 * u + M * h
                        mm = pe.matmul(e_ps[rows, at:at + M], a_sb[rows, u, h % 2, h // 2, :],
                                       slot[n.par][rows, u, M * h:M * h + M], start=False, stop=True,
                                       skip_group_check=True)
                if u == 1:
                    mm.then_inc(s.r_ps, 1)

            def weights_transposed(n):
                wait(pe, s.pw, n.n + 1)
                wait(pe, s.st_sb, n.n + 1)
                for u in range(2):
                    for p in range(2):
                        at = 256 * u + P * p
                        mm = pe.transpose(f_ps[:, at:at + P], pw[:, u, P * p:P * p + P], m.c["ident"])
                mm.then_inc(s.pt_ps, 1)

            def weights_by_slots(n):
                wait(pe, s.pt_sb, n.n + 1)
                wait(pe, s.t1, n.n + 1)
                for u in range(2):
                    for p in range(2):
                        for b in range(B):
                            at = 256 * u + 128 * p
                            mm = pe.matmul(g_ps[64 * b:64 * b + 64, at:at + 128].rearrange("j (e t) -> j e t", e=2),
                                           st_sb[:, u, p, C * b:C * b + C], pt_sb[:, u, p, :, C * b:C * b + C],
                                           start=True, stop=True)
                mm.then_inc(s.b_ps, 1)

            def outputs(n):
                wait(pe, s.b_sb, n.n + 1)
                for inter in (True, False):
                    for u in range(2):
                        for b in range(B):
                            for h in range(H):
                                rows = slice(64 * b, 64 * b + 64)
                                out = e_ps[rows, D * u + K * h:D * u + K * h + K]
                                if inter:
                                    pe.matmul(out, pt_sb[:, u, h // 2, h % 2, C * b:C * b + C],
                                              (st0, st1)[u][:, 1, b, h // 2, :], start=(u == 0 and h == 0), stop=False,
                                              skip_group_check=True)
                                else:
                                    mm = pe.matmul(out, b_sb[rows, u, h, :], kv[n.par][rows, u, h, 1, b, :],
                                                   start=False, stop=True, skip_group_check=True)
                mm.then_inc(s.o_ps, 1)

            def project_out(n):
                wait(pe, s.on, n.n + 1)
                for u in range(2):
                    mm = pe.transpose(f_ps[:, P * u:P * u + P], on[:, u, :], m.c["ident"])
                mm.then_inc(s.ot_ps, 1)
                wait(pe, s.ot_sb, n.n + 1)
                for u in range(2):
                    mm = pe.matmul(g_ps[:, D * u:D * u + D], ot_sb[:, u, :], m.w_o[:], start=True, stop=True)
                mm.then_inc(s.y_ps, 1)

            def body(n):
                attend(n)
                state_transposed(n, 0)
                slots_transposed(n)
                updates(n)
                if not is_last(n):
                    x_transposed(n.step(1))
                raw_logits(n, 0)
                state_transposed(n, 1)
                if not is_last(n):
                    project(n.step(1))
                raw_logits(n, 1)
                if not is_first(n):
                    wait(pe, s.sk_sb, n.n * 2 + 2)
                    r.tensor(pe, n.step(-1))
                weights_transposed(n)
                if not is_last(n):
                    if is_first(n):
                        wait(pe, s.sk_sb, 2)
                    else:
                        wait(pe, r.s.moved, n.n)
                    gate_sums(n.step(1))
                weights_by_slots(n)
                outputs(n)
                project_out(n)
                wait(pe, s.d_sb, n.n + 2 if not is_last(n) else NPAIR)

            x_transposed(FIRST)
            project(FIRST)
            gate_sums(FIRST)
            pe.wait_ge(s.d_sb, 1)
            over_pairs(pe, body)
            r.tensor(pe, LAST)

        @block.vector
        def _(dve):
            def norm_stats(n):
                for u in range(2):
                    ins = nc.vector.bn_stats(ln.stats[:, u, :], m.x[:, bass.ds((n.n * 2 + u) * D, D)])
                ins.then_inc(s.stats, 1)
                wait(dve, s.stats, n.n + 1)
                nc.vector.memset(ln.carrier[:], 0.0)
                for u in range(2):
                    nc.vector.bn_aggr(ln.mv[:, u, :], ln.stats[:, u, :]).then_inc(s.mv, 1)
                wait(dve, s.mv, (n.n + 1) * 2)
                nc.vector.tensor_scalar(ln.ve[:], ln.mv[:, :, 1], EPS, None, ALU.add).then_inc(s.var_eps, 1)

            def normed(n):
                wait(dve, s.rstd, n.n + 1)
                wait(dve, s.x_t_ps, n.n)
                for u in range(2):
                    ins = nc.vector.tensor_scalar(xn[:, u, :], m.x[:, bass.ds((n.n * 2 + u) * D, D)],
                                                  ln.mv[:, u, 0:1], ln.rstd[:, u:u + 1], ALU.subtract, ALU.mult)
                ins.then_inc(s.xn, 1)

            def projections(n):
                wait(dve, s.exp_z, n.n + 1)
                nc.vector.tensor_scalar(exp_z[:], exp_z[:], LN_MAX, None, ALU.min).then_inc(s.capped, 1)
                wait(dve, s.exp_kqk, n.n + 1)
                nc.vector.tensor_scalar(sig[:], exp_kqk[:], 1.0, None, ALU.add).then_inc(s.sig_sum, 1)
                wait(dve, s.o_ps, n.n - 1)
                for b in range(B):
                    rows = slice(64 * b, 64 * b + 64)
                    ins = nc.vector.tensor_copy(kv[n.par][rows, :, :, 1, b, :],
                                                z_ps[rows, :, 384:512].rearrange("p u (h k) -> p u h k", h=H))
                ins.then_inc(s.v_ready, 1)
                wait(dve, s.sig_sum, n.n + 1)
                nc.vector.reciprocal(sig[:], sig[:]).then_inc(s.sig, 1)
                wait(dve, s.sig, n.n + 1)
                for b in range(B):
                    rows = slice(64 * b, 64 * b + 64)
                    ins = nc.vector.tensor_tensor(kv[n.par][rows, :, :, 0, b, :],
                                                  z_ps[rows, :, 256:384].rearrange("p u (h k) -> p u h k", h=H),
                                                  sig[rows, 0:256].rearrange("p (u h k) -> p u h k", u=2, h=H), ALU.mult)
                ins.then_inc(s.k_ready, 1)
                wait(dve, s.q_spread, n.n)
                nc.vector.scalar_tensor_tensor(q_raw[:].rearrange("p e u t -> p (e u t)"), qk_ps[:, 0:256],
                                               float(K) ** -0.5, sig[:, 256:512], ALU.mult, ALU.mult).then_inc(s.q_ready, 1)
                nc.vector.tensor_tensor(k_t[n.par][:].rearrange("p e u t -> p (e u t)"), qk_ps[:, 256:512],
                                        sig[:, 512:768], ALU.mult).then_inc(s.kt_ready, 1)

            def softplus(n):
                wait(dve, s.log1, n.n + 1)
                nc.vector.scalar_tensor_tensor(soft[:], z_ps[:, :, 0:256], -1.0, exp_z[:], ALU.mult, ALU.max).then_inc(s.soft, 1)

            def slots(n):
                wait(dve, s.decays, n.n + 1)
                wait(dve, s.r_ps, n.n - 1)
                nc.vector.scalar_tensor_tensor(slot[n.par][:], ge[:], 1.0, e_minus[:], ALU.subtract, ALU.mult,
                                               reverse0=True).then_inc(s.s_ready, 1)

            def causal():
                return m.c["causal"].unsqueeze(1).to_broadcast([P, 2 * H, C])

            def mask_a(n):
                wait(dve, s.a_ps, n.n + 1)
                wait(dve, s.r_ps, n.n)
                nc.vector.tensor_tensor(a_sb[:].rearrange("j u e p t -> j (u e p) t"),
                                        e_ps.rearrange("p (a t) -> p a t", t=C), causal(), ALU.mult).then_inc(s.a_sb, 1)

            def new_states(n):
                wait(dve, s.u_ps, n.n + 1)
                wait(dve, s.d_sb, n.n + 1)
                nc.vector.tensor_tensor(t0[:].rearrange("p c b h k -> p (c b h k)"), st0[:].rearrange("p c b h k -> p (c b h k)"),
                                        g_ps[:, 0:256], ALU.add).then_inc(s.t0, 1)
                nc.vector.tensor_tensor(d01[:], d_sb[n.par][:, 0, :, 0, :], d_sb[n.par][:, 1, :, 1, :],
                                        ALU.mult).then_inc(s.d01, 1)
                wait(dve, s.d01, n.n + 1)
                nc.vector.tensor_tensor(st1[:].rearrange("p c b h k -> p c (b h) k"), t0[:].rearrange("p c b h k -> p c (b h) k"),
                                        d01[:].rearrange("p b h -> p (b h)").unsqueeze(2).unsqueeze(1).to_broadcast([P, 2, 4, K]),
                                        ALU.mult).then_inc(s.st1, 1)
                wait(dve, s.st1, n.n + 1)
                nc.vector.tensor_tensor(t1[:].rearrange("p c b h k -> p (c b h k)"), st1[:].rearrange("p c b h k -> p (c b h k)"),
                                        g_ps[:, 256:512], ALU.add).then_inc(s.t1, 1)

            def carry_state(n):
                wait(dve, s.d_sb, n.n + 2)
                nc.vector.tensor_tensor(d10[:], d_sb[n.par][:, 1, :, 0, :], d_sb[1 - n.par][:, 0, :, 1, :],
                                        ALU.mult).then_inc(s.d10, 1)
                wait(dve, s.d10, n.n + 1)
                wait(dve, s.o_ps, n.n + 1)
                nc.vector.tensor_tensor(st0[:].rearrange("p c b h k -> p c (b h) k"), t1[:].rearrange("p c b h k -> p c (b h) k"),
                                        d10[:].rearrange("p b h -> p (b h)").unsqueeze(2).unsqueeze(1).to_broadcast([P, 2, 4, K]),
                                        ALU.mult).then_inc(s.st0, 1)

            def flat(x):
                return x[:].rearrange("p u h m -> p (u h) m")

            def softmax_in(n):
                wait(dve, s.r_ps, n.n + 1)
                nc.vector.tensor_tensor(logits[:].rearrange("p u h m -> p (u h m)"), e_ps,
                                        e_plus[n.par][:].rearrange("p u m -> p (u m)"), ALU.mult).then_inc(s.logits, 1)
                wait(dve, s.logits, n.n + 1)
                nc.vector.tensor_reduce(maxes[:].rearrange("p u h -> p (u h)"), flat(logits), AX_X, ALU.max).then_inc(s.maxes, 1)
                wait(dve, s.maxes, n.n + 1)
                nc.vector.tensor_tensor(flat(logits), flat(logits),
                                        maxes[:].rearrange("p u h -> p (u h)").unsqueeze(2).to_broadcast([P, 2 * H, M]),
                                        ALU.subtract).then_inc(s.shifted, 1)

            def softmax_out(n):
                wait(dve, s.probs, n.n + 1)
                nc.vector.tensor_reduce(sums[:].rearrange("p u h -> p (u h)"), flat(probs), AX_X, ALU.add).then_inc(s.sums, 1)
                nc.vector.tensor_tensor(pw[:].rearrange("p u m -> p (u m)"), probs[:].rearrange("p u h m -> p (u h m)"),
                                        e_plus[n.par][:].rearrange("p u m -> p (u m)"), ALU.mult).then_inc(s.pw, 1)

            def mask_b(n):
                wait(dve, s.b_ps, n.n + 1)
                nc.vector.tensor_tensor(b_sb[:].rearrange("p u h t -> p (u h) t"),
                                        g_ps.rearrange("p (a t) -> p a t", t=C), causal(), ALU.mult).then_inc(s.b_sb, 1)

            def out_norm(n):
                wait(dve, s.sums, n.n + 1)
                nc.vector.tensor_tensor(s2[:], sums[:], sums[:], ALU.mult).then_inc(s.s2, 1)
                wait(dve, s.sq, n.n + 1)
                nc.vector.tensor_reduce(ms[:].rearrange("p u h -> p (u h)"), flat(sq), AX_X, ALU.add).then_inc(s.ms, 1)
                wait(dve, s.ms, n.n + 1)
                nc.vector.scalar_tensor_tensor(ms[:], s2[:], EPS, ms[:], ALU.mult, ALU.add).then_inc(s.oe, 1)
                wait(dve, s.o_rstd, n.n + 1)
                nc.vector.tensor_tensor(on[:].rearrange("p u (h k) -> p (u h) k", h=H),
                                        e_ps[:, 0:256].rearrange("p (a k) -> p a k", k=K),
                                        o_rstd[:].rearrange("p u h -> p (u h)").unsqueeze(2).to_broadcast([P, 2 * H, K]),
                                        ALU.mult).then_inc(s.on, 1)

            def residual(n):
                wait(dve, s.y_ps, n.n + 1)
                x = m.x[:, bass.ds(n.n * 2 * D, 2 * D)]
                nc.vector.tensor_tensor(x, g_ps[:, 0:256], x, ALU.add).then_inc(s.x1, 1)

            def body(n):
                if not is_last(n):
                    norm_stats(n.step(1))
                mask_a(n)
                if not is_first(n):
                    r.vector_norm(dve, n.step(-1))
                if not is_last(n):
                    normed(n.step(1))
                if not is_first(n):
                    r.vector_normed(dve, n.step(-1))
                new_states(n)
                if not is_last(n):
                    projections(n.step(1))
                softmax_in(n)
                if not is_last(n):
                    softplus(n.step(1))
                if not is_first(n):
                    r.vector_choose(dve, n.step(-1))
                softmax_out(n)
                if not is_first(n):
                    r.vector_place(dve, n.step(-1))
                if not is_last(n):
                    slots(n.step(1))
                mask_b(n)
                out_norm(n)
                if not is_last(n):
                    carry_state(n)
                residual(n)

            dve.wait_ge(s.zeros_ready, 1)
            nc.vector.memset(st0[:], 0.0).then_inc(s.st0, 1)
            nc.vector.memset(minus_half[:], -0.5).then_inc(s.const_ready, 1)
            norm_stats(FIRST)
            normed(FIRST)
            projections(FIRST)
            softplus(FIRST)
            slots(FIRST)
            over_pairs(dve, body)
            r.vector_norm(dve, LAST)
            r.vector_normed(dve, LAST)
            r.vector_choose(dve, LAST)
            r.vector_place(dve, LAST)
            r.vector_plan(dve)

        @block.scalar
        def _(act):
            def x_transposed(n):
                wait(act, s.x_t_ps, n.n + 1)
                wait(act, s.qk_ps, n.n)
                nc.scalar.copy(x_t[:].rearrange("p u t -> p (u t)"), xt_ps[:, 0:256]).then_inc(s.x_t, 1)

            def exps(n):
                wait(act, s.z_ps, n.n + 1)
                wait(act, s.soft, n.n)
                nc.scalar.activation(exp_z[:], z_ps[:, :, 0:256], ACT.Exp, scale=-1.0).then_inc(s.exp_z, 1)
                wait(act, s.sig_sum, n.n)
                nc.scalar.activation(exp_kqk[:, 0:256].rearrange("p (u d) -> p u d", u=2), z_ps[:, :, 256:384], ACT.Exp,
                                     scale=-1.0)
                wait(act, s.qk_ps, n.n + 1)
                nc.scalar.activation(exp_kqk[:, 256:768], qk_ps, ACT.Exp, scale=-1.0).then_inc(s.exp_kqk, 1)

            def spread_q(n):
                wait(act, s.q_ready, n.n + 1)
                wait(act, s.r_ps, n.n - 1)
                for b in range(B):
                    for p in range(2):
                        rows = slice(64 * b + 32 * p, 64 * b + 32 * p + 32)
                        ins = nc.scalar.copy(q_t[n.par][rows, :, :, p, C * b:C * b + C],
                                             q_raw[rows].rearrange("k e u t -> k u e t"))
                ins.then_inc(s.q_spread, 1)

            def log1(n):
                wait(act, s.capped, n.n + 1)
                nc.scalar.activation(exp_z[:], exp_z[:], ACT.Ln, bias=1.0).then_inc(s.log1, 1)

            def decays(n):
                wait(act, s.soft, n.n + 1)
                wait(act, s.s_ready, n.n)
                nc.scalar.activation(ge[:], soft[:], ACT.Exp, scale=-1 / GATE_NORM).then_inc(s.ge_ready, 1)
                wait(act, s.g_ps, n.n + 1)
                wait(act, s.pw, n.n - 1)
                nc.scalar.activation(e_plus[n.par][:].rearrange("p u m -> p (u m)"), xt_ps, ACT.Exp)
                nc.scalar.activation(e_minus[:].rearrange("p u m -> p (u m)"), xt_ps, ACT.Exp, scale=-1.0).then_inc(s.decays, 1)
                wait(act, s.d_ps, n.n + 1)
                wait(act, s.d10, n.n - 1)
                nc.scalar.activation(d_sb[n.par][:].rearrange("s u b k p -> s (u b k p)"), h_ps[:, 0:16],
                                     ACT.Exp).then_inc(s.d_sb, 1)

            def state_transposed(n, u):
                wait(act, s.sk_ps, n.n * 2 + u + 1)
                wait(act, s.r_ps, n.n)
                nc.scalar.copy(sk_sb[u][:], h_ps[:, 0:P]).then_inc(s.sk_sb, 1)

            def slots_transposed(n):
                wait(act, s.st_ps, n.n + 1)
                wait(act, s.b_ps, n.n)
                nc.scalar.copy(st_sb[:].rearrange("p u h t -> p (u h t)"), f_ps).then_inc(s.st_sb, 1)

            def probabilities(n):
                wait(act, s.shifted, n.n + 1)
                wait(act, s.pw, n.n)
                nc.scalar.activation(probs[:], logits[:], ACT.Exp).then_inc(s.probs, 1)

            def weights_transposed(n):
                wait(act, s.pt_ps, n.n + 1)
                wait(act, s.o_ps, n.n)
                for e in range(2):
                    rows = slice(64 * e, 64 * e + 64)
                    ins = nc.scalar.copy(pt_sb[rows, :, :, e, :], f_ps[rows, :].rearrange("s (u p t) -> s u p t", u=2, p=2))
                ins.then_inc(s.pt_sb, 1)

            def squares(n):
                wait(act, s.o_ps, n.n + 1)
                wait(act, s.ms, n.n)
                nc.scalar.activation(sq[:].rearrange("p u h k -> p (u h k)"), e_ps[:, 0:256], ACT.Square,
                                     scale=float(K) ** -0.5).then_inc(s.sq, 1)

            def o_transposed(n):
                wait(act, s.ot_ps, n.n + 1)
                wait(act, s.y_ps, n.n)
                nc.scalar.copy(ot_sb[:].rearrange("p u t -> p (u t)"), f_ps[:, 0:256]).then_inc(s.ot_sb, 1)

            def body(n):
                state_transposed(n, 0)
                slots_transposed(n)
                if not is_last(n):
                    x_transposed(n.step(1))
                state_transposed(n, 1)
                if not is_last(n):
                    exps(n.step(1))
                    log1(n.step(1))
                probabilities(n)
                if not is_first(n):
                    r.scalar(act, n.step(-1))
                weights_transposed(n)
                if not is_last(n):
                    spread_q(n.step(1))
                    decays(n.step(1))
                squares(n)
                o_transposed(n)

            act.wait_ge(s.zeros_ready, 1)
            x_transposed(FIRST)
            exps(FIRST)
            log1(FIRST)
            spread_q(FIRST)
            decays(FIRST)
            over_pairs(act, body)
            r.scalar(act, LAST)

        @block.gpsimd
        def _(pool):
            def input_rstd(n):
                wait(pool, s.var_eps, n.n + 1)
                wait(pool, s.xn, n.n)
                nc.gpsimd.tensor_tensor(ln.rstd[:], ln.ve[:], minus_half[:, 0, 0:2], ALU.pow).then_inc(s.rstd, 1)

            def output_rstd(n):
                wait(pool, s.oe, n.n + 1)
                wait(pool, s.on, n.n)
                nc.gpsimd.tensor_tensor(o_rstd[:], ms[:], minus_half[:], ALU.pow).then_inc(s.o_rstd, 1)

            def body(n):
                if not is_last(n):
                    input_rstd(n.step(1))
                if not is_first(n):
                    r.gpsimd_norm(pool, n.step(-1), minus_half)
                if not is_first(n):
                    r.gpsimd_scatter(pool, n.step(-1))
                output_rstd(n)

            for zeros in (kv[0], kv[1], q_t[0], q_t[1], pt_sb):
                ins = nc.gpsimd.memset(zeros[:], 0.0)
            ins.then_inc(s.zeros_ready, 1)
            pool.wait_ge(s.const_ready, 1)
            pool.wait_ge(s.zeros_ready, 1)
            input_rstd(FIRST)
            over_pairs(pool, body)
            r.gpsimd_norm(pool, LAST, minus_half)
            r.gpsimd_scatter(pool, LAST)
            r.gpsimd_wait(pool)

        @block.sync
        def _(sp):
            r.sync_tails(sp)


_INS = """L0_attn_a_x L0_attn_a_Wq L0_attn_a_Wk L0_attn_a_Wv L0_attn_a_Wf L0_attn_a_g_norm_w L0_attn_a_Wo
L0_attn_b_log_Lam_real L0_attn_b_Lam_imag L0_attn_b_B_real L0_attn_b_B_imag L0_attn_b_C_real L0_attn_b_C_imag
L0_attn_b_D L0_attn_b_log_dt L0_attn_b_W_out L0_attn_b_b_out L0_ffn_router_w L0_ffn_router_b L0_ffn_W1 L0_ffn_b1
L0_ffn_W2 L0_ffn_b2""".split()


def experts(nc, m, rows_in, rows_out, prefix):
    with ExitStack() as ctx:
        def sb(name, *free, dt=F32):
            return ctx.enter_context(nc.sbuf_tensor(prefix + name, [P, *free], dt))

        s = Names()
        s.x_t_ps, s.x_t, s.w1, s.h_ps, s.h_act, s.h_dve, s.y_ps, s.y = \
            semaphores(ctx, nc, prefix, "x_t_ps x_t w1 h_ps h_act h_dve y_ps y")
        loaded = semaphores(ctx, nc, prefix, "rows_in0 rows_in1 rows_in2 rows_in3")
        stored = semaphores(ctx, nc, prefix, "rows_out0 rows_out1 rows_out2 rows_out3")
        x_in = [sb(f"x_in{j}", D) for j in range(GROUP)]
        x_t = [sb(f"x_t{j}", P) for j in range(2)]
        w1 = [sb(f"w1_of_tile{j}", FF) for j in range(GROUP)]
        h = [sb(f"h{j}", FB, P) for j in range(2)]
        y = [sb(f"y{j}", D) for j in range(GROUP)]
        x_ps, h_ps, y_ps = m.bank[0:2], (m.bank[2:4], m.bank[4:6]), m.bank[6:8]

        block = ctx.enter_context(nc.Block())

        LASTQ = NGROUP - 1

        def ends(q, j):
            return isinstance(q, int) and q * GROUP + j >= NTILE

        def plan_value(eng, at, most):
            at = slice(at, at + 1) if isinstance(at, int) else bass.ds(at, 1)
            return eng.value_load(m.plan[0:1, at], min_val=0, max_val=most)

        def experts_of(eng, q):
            digits = plan_value(eng, q + NTILE, E ** (GROUP + 3) - 1)
            return [(digits >> (3 * k)) & (E - 1) for k in range(GROUP + 3)]

        def over_groups(eng, group):
            group(0)
            with eng.Fori(1, LASTQ) as q:
                group(q)
            group(LASTQ)

        @block.sync
        def _(sp):
            def load(t, q, j):
                row = plan_value(sp, t, ROWS - P)
                wait(sp, s.x_t_ps, t - GROUP + 1)
                sp.dma_start(x_in[j][:], rows_in[bass.ds(row, P), :]).then_inc(loaded[j], 16)

            def group(q):
                for j in range(GROUP):
                    load(q * GROUP + (j + GROUP), q + 1, j)

            for j in range(GROUP):
                load(j, 0, j)
            group(0)
            with sp.Fori(1, LASTQ) as q:
                group(q)

        @block.gpsimd
        def _(pool):
            def group(q):
                for j in range(GROUP):
                    t = q * GROUP + j
                    wait(pool, s.y, t + 1)
                    pool.dma_start(rows_out[bass.ds(t * P, P), :], y[j][:]).then_inc(stored[j], 16)

            over_groups(pool, group)
            for j in range(GROUP):
                pool.wait_ge(stored[j], 16 * NGROUP)

        @block.tensor
        def _(pe):
            def transposed(t, q, j):
                wait(pe, loaded[j], (q + 1) * 16)
                wait(pe, s.x_t, t - 1)
                pe.transpose(x_ps[j % 2][:, 0:P], x_in[j][:], m.c["ident"]).then_inc(s.x_t_ps, 1)

            def hidden(t, j):
                wait(pe, s.x_t, t + 1)
                wait(pe, s.w1, t + 1)
                wait(pe, s.h_act, t - 1)
                wait(pe, s.h_dve, t - 1)
                for f in range(FB):
                    mm = pe.matmul(h_ps[j % 2][f // 2][:, P * (f % 2):P * (f % 2) + P],
                                   w1[j % GROUP][:, P * f:P * f + P], x_t[j % 2][:], start=True, stop=True)
                mm.then_inc(s.h_ps, 1)

            def result(t, j, owner):
                wait(pe, s.h_act, t + 1)
                wait(pe, s.h_dve, t + 1)
                wait(pe, s.y, t - 1)
                for f in range(FB):
                    mm = pe.matmul(y_ps[j % 2][:, 0:D], h[j % 2][:, f, :], m.w2[:, bass.ds(owner * FF + D * f, D)],
                                   start=(f == 0), stop=(f == FB - 1))
                mm.then_inc(s.y_ps, 1)

            def group(q):
                owner = experts_of(pe, q)
                for j in range(GROUP):
                    t = q * GROUP + j
                    if not ends(q, j + 1):
                        hidden(t + 1, j + 1)
                    if not ends(q, j + 2):
                        transposed(t + 2, q + (j + 2) // GROUP, (j + 2) % GROUP)
                    result(t, j, owner[j])

            transposed(0, 0, 0)
            hidden(0, 0)
            transposed(1, 0, 1)
            over_groups(pe, group)

        @block.vector
        def _(dve):
            def hidden(t, j, owner):
                wait(dve, s.h_ps, t + 1)
                wait(dve, s.y_ps, t - 1)
                for f in range(FB // 2, FB):
                    ins = nc.vector.tensor_scalar(h[j % 2][:, f, :], h_ps[j % 2][1][:, P * (f % 2):P * (f % 2) + P],
                                                  m.b1[:, bass.ds(owner * FB + f, 1)], 0.0, ALU.add, ALU.max)
                ins.then_inc(s.h_dve, 1)

            def result(t, q, j, owner):
                wait(dve, s.y_ps, t + 1)
                wait(dve, stored[j], q * 16)
                nc.vector.tensor_tensor(y[j][:], y_ps[j % 2][:, 0:D], m.b2[:, bass.ds(owner * D, D)], ALU.add).then_inc(s.y, 1)

            def group(q):
                owner = experts_of(dve, q)
                for j in range(GROUP):
                    if not ends(q, j + 1):
                        hidden(q * GROUP + j + 1, j + 1, owner[j + 1])
                    result(q * GROUP + j, q, j, owner[j])

            hidden(0, 0, experts_of(dve, 0)[0])
            over_groups(dve, group)

        @block.scalar
        def _(act):
            def x_transposed(t, j):
                wait(act, s.x_t_ps, t + 1)
                nc.scalar.copy(x_t[j % 2][:], x_ps[j % 2][:, 0:P]).then_inc(s.x_t, 1)

            def weights(j, owner):
                nc.scalar.copy(w1[j % GROUP][:], m.w1[:, bass.ds(owner * FF, FF)]).then_inc(s.w1, 1)

            def hidden(t, j, owner):
                if isinstance(t, int) and t == NTILE - 1:
                    act.wait_ge(s.h_ps, NTILE)
                for f in range(FB // 2):
                    ins = nc.scalar.activation(h[j % 2][:, f, :], h_ps[j % 2][0][:, P * (f % 2):P * (f % 2) + P],
                                               ACT.Relu, bias=m.b1[:, bass.ds(owner * FB + f, 1)])
                ins.then_inc(s.h_act, 1)

            def group(q):
                owner = experts_of(act, q)
                for j in range(GROUP):
                    if not ends(q, j + 2):
                        x_transposed(q * GROUP + j + 2, j)
                    if not ends(q, j + 3):
                        weights(j + 3, owner[j + 3])
                    if not ends(q, j + 1):
                        hidden(q * GROUP + j + 1, j + 1, owner[j + 1])

            owner = experts_of(act, 0)
            for t in range(2):
                weights(t, owner[t])
                x_transposed(t, t)
            weights(2, owner[2])
            hidden(0, 0, owner[0])
            over_groups(act, group)


class Gather:

    def __init__(self, ctx, nc, m, rows, ready, prefix):
        def sb(name, *free, dt=F32):
            return ctx.enter_context(nc.sbuf_tensor(prefix + name, [P, *free], dt))

        self.nc, self.m, self.rows, self.ready = nc, m, rows, ready
        self.s = Names()
        self.s.index, self.s.carried, self.s.in0, self.s.in1, self.s.weighed, self.s.both, self.s.sum = \
            semaphores(ctx, nc, prefix, "index carried in0 in1 weighed both sum")
        self.index = [sb(f"index{i}", 4, dt=U32) for i in range(2)]
        self.y = [sb(f"y{i}", 4, D) for i in range(2)]
        self.weighed = sb("weighed", 4, D)
        self.both = sb("both", 2, D)
        self.pool_carrier = sb("pool_carrier", 1)
        self.zeros = m.zero[:, 0:1]
        self.carrier = sb("carrier", 1)

    def arrived(self, par):
        return (self.s.in0, self.s.in1)[par]

    def vector_index(self, dve, n):
        if not isinstance(n.n, int) or n.n > 1:
            wait(dve, self.s.weighed, n.n - 1)
            self.nc.vector.memset(self.carrier[:], 0.0)
        self.nc.vector.tensor_copy(self.index[n.par][:], self.m.slots[:, bass.ds(n.n * 4, 4)]).then_inc(self.s.index, 1)

    def gpsimd(self, pool, n):
        wait(pool, self.s.carried, n.n)
        wait(pool, self.s.index, n.n + 1)
        self.nc.gpsimd.tensor_tensor(self.pool_carrier[:], self.zeros, self.zeros, ALU.add).then_inc(self.s.carried, 1)
        for j in range(4):
            self.nc.gpsimd.indirect_dma_start(
                self.y[n.par][:, j, :], None, self.rows[:, :],
                bass.IndirectOffsetOnAxis(ap=self.index[n.par][:, j:j + 1], axis=0)).then_inc(self.arrived(n.par), 16)

    def vector_sum(self, dve, n, out):
        nc, m, s = self.nc, self.m, self.s
        wait(dve, self.arrived(n.par), (n.half + 1) * 64)
        nc.vector.tensor_tensor(self.weighed[:], self.y[n.par][:],
                                m.gates[:, bass.ds(n.n * 4, 4)].unsqueeze(2).to_broadcast([P, 4, D]),
                                ALU.mult).then_inc(s.weighed, 1)
        wait(dve, s.weighed, n.n + 1)
        w = self.weighed[:].rearrange("p (u k) d -> p u k d", k=2)
        nc.vector.tensor_tensor(self.both[:], w[:, :, 0, :], w[:, :, 1, :], ALU.add).then_inc(s.both, 1)
        wait(dve, s.both, n.n + 1)
        nc.vector.tensor_tensor(out, self.both[:].rearrange("p u d -> p (u d)"), m.x[:, bass.ds(n.n * 2 * D, 2 * D)],
                                ALU.add).then_inc(s.sum, 1)


def space_and_route(nc, m, a, dram):
    with ExitStack() as ctx:
        def sb(name, *free, dt=F32):
            return ctx.enter_context(nc.sbuf_tensor("sp_" + name, [P, *free], dt))

        s = Names()
        s.const_ready, s.stats, s.mv, s.var_eps, s.rstd, s.xn, s.x_t_ps = \
            semaphores(ctx, nc, "sp_", "const_ready stats mv var_eps rstd xn x_t_ps")
        s.x_t, s.in_ps, s.in_cos, s.in_sin, s.turned, s.state, s.back_cos = \
            semaphores(ctx, nc, "sp_", "x_t in_ps in_cos in_sin turned state back_cos")
        s.back_sin, s.out_ps, s.x3, s.next_slot = \
            semaphores(ctx, nc, "sp_", "back_sin out_ps x3 next_slot")
        r = Route(ctx, nc, m, a, dram, "rb_")
        g = Gather(ctx, nc, m, dram.results[0], s.const_ready, "ga_")
        r.bank, r.ready, r.x_written = m.bank[7], s.const_ready, s.x3
        ln = Norm(sb, "ln")
        x2 = sb("x2", 2, D)
        xn = sb("xn", 2, D)
        x_t = [sb(f"x_t{i}", 2, P) for i in range(2)]
        in_cos = sb("in_cos", B, 2, C)
        in_sin = sb("in_sin", B, 2, C)
        turned = sb("turned", B, 2 * C)
        state = [sb(f"state{i}", B, 2 * C) for i in range(2)]
        back_cos = sb("back_cos", 2, B, C)
        back_sin = sb("back_sin", 2, B, C)
        minus_half = sb("minus_half", 2, H)
        t_ps, in_ps, out_ps = m.bank[0], m.bank[1], m.bank[2]

        block = ctx.enter_context(nc.Block())

        @block.tensor
        def _(pe):
            def body(n):
                wait(pe, s.xn, n.n + 1)
                for u in range(2):
                    mm = pe.transpose(t_ps[:, P * u:P * u + P], xn[:, u, :], m.c["ident"])
                mm.then_inc(s.x_t_ps, 1)
                wait(pe, s.x_t, n.n + 1)
                wait(pe, s.in_sin, n.n)
                x_all = x_t[n.par][:].rearrange("p u t -> p (u t)")
                pe.matmul(in_ps[:, 0:256], m.b_in_t[:], x_all, start=True, stop=True)
                pe.matmul(in_ps[:, 256:512], m.b_in_swap[:], x_all, start=True, stop=True).then_inc(s.in_ps, 1)
                if not is_first(n):
                    r.tensor(pe, n.step(-1))
                wait(pe, s.back_sin, n.n + 1)
                wait(pe, s.x3, n.n)
                for u in range(2):
                    out = out_ps[:, D * u:D * u + D]
                    pe.matmul(out, back_cos[:, u].rearrange("s b t -> s (b t)"), m.out_cos[:], start=True, stop=False)
                    pe.matmul(out, back_sin[:, u].rearrange("s b t -> s (b t)"), m.out_sin[:], start=False, stop=False)
                    pe.matmul(out, x_t[n.par][:, u, :], m.out_x[:], start=False, stop=False)
                    mm = pe.matmul(out, m.c["ones"][0:1, :], m.b_out[0:1, :], start=False, stop=True)
                mm.then_inc(s.out_ps, 1)

            over_pairs(pe, body)
            r.tensor(pe, LAST)

        @block.vector
        def _(dve):
            def table(t, n):
                return (t[:, bass.ds(n.n * 2 * C, 2 * C)].rearrange("s (u t) -> s u t", u=2)
                        .unsqueeze(2).to_broadcast([P, 2, B, C]))

            def start(n):
                g.vector_sum(dve, n, x2[:].rearrange("p u d -> p (u d)"))
                wait(dve, g.s.sum, n.n + 1)
                nc.vector.memset(ln.carrier[:], 0.0)
                for u in range(2):
                    ins = nc.vector.bn_stats(ln.stats[:, u, :], x2[:, u, :])
                ins.then_inc(s.stats, 1)
                wait(dve, s.stats, n.n + 1)
                nc.vector.memset(ln.carrier[:], 0.0)
                for u in range(2):
                    ins = nc.vector.bn_aggr(ln.mv[:, u, :], ln.stats[:, u, :])
                ins.then_inc(s.mv, 1)
                wait(dve, s.mv, n.n + 1)
                nc.vector.tensor_scalar(ln.ve[:], ln.mv[:, :, 1], EPS, None, ALU.add).then_inc(s.var_eps, 1)
                wait(dve, s.rstd, n.n + 1)
                for u in range(2):
                    ins = nc.vector.tensor_scalar(xn[:, u, :], x2[:, u, :], ln.mv[:, u, 0:1], ln.rstd[:, u:u + 1],
                                                  ALU.subtract, ALU.mult)
                ins.then_inc(s.xn, 1)

            def recur(n):
                wait(dve, s.in_ps, n.n + 1)
                nc.vector.tensor_tensor(in_cos[:].rearrange("s b u t -> s u b t"),
                                        in_ps[:, 0:256].rearrange("s (u b t) -> s u b t", u=2, b=B),
                                        table(m.cos, n), ALU.mult).then_inc(s.in_cos, 1)
                nc.vector.tensor_tensor(in_sin[:].rearrange("s b u t -> s u b t"),
                                        in_ps[:, 256:512].rearrange("s (u b t) -> s u b t", u=2, b=B),
                                        table(m.sin, n), ALU.mult).then_inc(s.in_sin, 1)
                wait(dve, s.in_sin, n.n + 1)
                nc.vector.tensor_tensor(turned[:].rearrange("s b t -> s (b t)"), in_cos[:].rearrange("s b u t -> s (b u t)"),
                                        in_sin[:].rearrange("s b u t -> s (b u t)"), ALU.add).then_inc(s.turned, 1)
                wait(dve, s.turned, n.n + 1)
                for b in range(B):
                    before = 0.0 if is_first(n) else state[1 - n.par][:, b, 2 * C - 1:2 * C]
                    ins = nc.vector.tensor_tensor_scan(state[n.par][:, b, :], m.mag[:], turned[:, b, :], before,
                                                       ALU.mult, ALU.add)
                ins.then_inc(s.state, 1)
                wait(dve, s.state, n.n + 1)
                wait(dve, s.out_ps, n.n)
                for t, out, done in ((m.cos, back_cos, s.back_cos), (m.sin, back_sin, s.back_sin)):
                    nc.vector.tensor_tensor(out[:], state[n.par][:].rearrange("s b (u t) -> s u b t", u=2),
                                            table(t, n), ALU.mult).then_inc(done, 1)

            def end(n):
                wait(dve, s.out_ps, n.n + 1)
                nc.vector.tensor_tensor(m.x[:, bass.ds(n.n * 2 * D, 2 * D)], out_ps[:, 0:256],
                                        x2[:].rearrange("p u d -> p (u d)"), ALU.add).then_inc(s.x3, 1)

            def body(n):
                if not is_last(n):
                    g.vector_index(dve, n.step(1))
                start(n)
                if not is_first(n):
                    r.vector_norm(dve, n.step(-1))
                    r.vector_normed(dve, n.step(-1))
                recur(n)
                if not is_first(n):
                    r.vector_choose(dve, n.step(-1))
                    r.vector_place(dve, n.step(-1))
                end(n)

            nc.vector.tensor_copy(m.next_slot[:], m.c["base"]).then_inc(s.next_slot, 1)
            dve.wait_ge(s.next_slot, 1)
            nc.vector.memset(minus_half[:], -0.5).then_inc(s.const_ready, 1)
            g.vector_index(dve, FIRST)
            over_pairs(dve, body)
            r.vector_norm(dve, LAST)
            r.vector_normed(dve, LAST)
            r.vector_choose(dve, LAST)
            r.vector_place(dve, LAST)
            r.vector_plan(dve)

        @block.scalar
        def _(act):
            def body(n):
                wait(act, s.x_t_ps, n.n + 1)
                wait(act, s.out_ps, n.n - 1)
                nc.scalar.copy(x_t[n.par][:].rearrange("p u t -> p (u t)"), t_ps[:, 0:256]).then_inc(s.x_t, 1)
                if not is_first(n):
                    r.scalar(act, n.step(-1))

            over_pairs(act, body)
            r.scalar(act, LAST)

        @block.gpsimd
        def _(pool):
            def body(n):
                if not is_last(n):
                    g.gpsimd(pool, n.step(1))
                wait(pool, s.var_eps, n.n + 1)
                wait(pool, s.xn, n.n)
                nc.gpsimd.tensor_tensor(ln.rstd[:], ln.ve[:], minus_half[:, 0, 0:2], ALU.pow).then_inc(s.rstd, 1)
                if not is_first(n):
                    r.gpsimd_norm(pool, n.step(-1), minus_half)
                    r.gpsimd_scatter(pool, n.step(-1))

            pool.wait_ge(s.const_ready, 1)
            g.gpsimd(pool, FIRST)
            over_pairs(pool, body)
            r.gpsimd_norm(pool, LAST, minus_half)
            r.gpsimd_scatter(pool, LAST)
            r.gpsimd_wait(pool)
            pool.wait_ge(g.s.carried, NPAIR)

        @block.sync
        def _(sp):
            r.sync_tails(sp)


def gather_and_store(nc, m, rows, out):
    with ExitStack() as ctx:
        s = Names()
        s.const_ready, s.out0, s.out1 = \
            semaphores(ctx, nc, "go_", "const_ready out0 out1")
        stored = [s.out0, s.out1]
        g = Gather(ctx, nc, m, rows, s.const_ready, "gb_")
        x4 = [ctx.enter_context(nc.sbuf_tensor(f"go_x4_{i}", [P, 2, D], F32)) for i in range(2)]
        block = ctx.enter_context(nc.Block())

        @block.vector
        def _(dve):
            def body(n):
                if not is_last(n):
                    g.vector_index(dve, n.step(1))
                wait(dve, stored[n.par], n.half * 32)
                g.vector_sum(dve, n, x4[n.par][:].rearrange("p u d -> p (u d)"))

            nc.vector.memset(g.both[:], 0.0).then_inc(s.const_ready, 1)
            dve.wait_ge(s.const_ready, 1)
            g.vector_index(dve, FIRST)
            over_pairs(dve, body)

        @block.gpsimd
        def _(pool):
            def body(n):
                if not is_last(n):
                    g.gpsimd(pool, n.step(1))

            pool.wait_ge(s.const_ready, 1)
            g.gpsimd(pool, FIRST)
            over_pairs(pool, body)
            pool.wait_ge(g.s.carried, NPAIR)

        @block.sync
        def _(sp):
            def body(n):
                wait(sp, g.s.sum, n.n + 1)
                for b in range(B):
                    sp.dma_start(out[b, bass.ds(n.n * 2 * C, 2 * C), :].rearrange("(u t) d -> t u d", u=2),
                                 x4[n.par][C * b:C * b + C]).then_inc(stored[n.par], 16)

            over_pairs(sp, body)
            for par in range(2):
                sp.wait_ge(stored[par], 32 * (NPAIR // 2))


def program(nc, a, out):
    with ExitStack() as ctx:
        m = memory(ctx, nc)

        def rows(name, count):
            return [nc.dram_tensor(f"{name}{i}", (count, D), F32, kind="Internal").ap() for i in range(2)]

        dram = Names()
        dram.inputs, dram.results = rows("expert_inputs", ROWS), rows("expert_results", NTILE * P)
        setup(nc, m, a, dram)
        nc.all_engine_barrier()
        attention_and_route(nc, m, a, dram)
        nc.all_engine_barrier()
        experts(nc, m, dram.inputs[0], dram.results[0], "ea_")
        nc.all_engine_barrier()
        space_and_route(nc, m, a, dram)
        nc.all_engine_barrier()
        experts(nc, m, dram.inputs[1], dram.results[1], "eb_")
        nc.all_engine_barrier()
        gather_and_store(nc, m, dram.results[1], out)


def kernel(**inputs):
    import concourse.bacc as bacc
    from concourse.bass_utils import run_bass_kernel_spmd

    nc = bacc.Bacc("TRN2", target_bir_lowering=False, num_devices=1)
    arrays, args = {}, {}
    for name in [*_INS, "constants"]:
        x = constants()[0] if name == "constants" else np.ascontiguousarray(inputs[name])
        arrays[f"in_{name}_dram"] = x
        args[name] = nc.dram_tensor(f"in_{name}_dram", x.shape, mybir.dt.from_np(x.dtype), kind="ExternalInput").ap()
    out = nc.dram_tensor("out_dram", (B, T, D), F32, kind="ExternalOutput").ap()
    program(nc, args, out)
    r = run_bass_kernel_spmd(nc, [arrays], core_ids=[0])
    return r.results[0]["out_dram"]
```

```python
from contextlib import ExitStack

import numpy as np

import concourse.bass as bass
from concourse import mybir

F32 = mybir.dt.float32
U32 = mybir.dt.uint32
I32 = mybir.dt.int32
ALU = mybir.AluOpType
ACT = mybir.ActivationFunctionType
AX_X = mybir.AxisListType.X

P = 128
B = 2
T = 1024
D = 128
H = 4
K = D // H
M = 64
C = 64
NCHUNK = T // C
NPAIR = NCHUNK // 2
GATE_NORM = 8.0
EPS = 1e-5
E = 8
FF = 512
FB = FF // P
N = 64
NTILE = B * T * 2 // P + E
GROUP = 4
NGROUP = NTILE // GROUP
REGION = B * T + P
SPARE = E * REGION - (NTILE - E) * P
ROWS = E * REGION + E * P
LN_MAX = float(2 ** 60)
TWO_PI_1 = 6.28125
TWO_PI_2 = round((2 * np.pi - TWO_PI_1) * 2 ** 20) / 2 ** 20
TWO_PI_3 = 2 * np.pi - TWO_PI_1 - TWO_PI_2
ROUND = 12582912.0
LEVELS = 10
ANGLES_AT = 14
LATE = 4 + 3 + 1 + E + 2 + 2 * E


class Names:
    pass


def constants():
    p = np.arange(P)
    b, t = p // C, p % C
    same = b[:, None] == b[None, :]
    mid = t <= C // 2 - 1
    cols = {
        "ident": np.eye(P),
        "cum": -1 / GATE_NORM * same * ((t[:, None] <= t[None, :]) * 1.0 - mid[:, None] * 1.0),
        "causal": (t[:, None] <= np.arange(C)[None, :]) * 1.0,
        "spans": -1 / GATE_NORM * np.stack([(b == 0) & ~mid, (b == 0) & mid, (b == 1) & ~mid, (b == 1) & mid], 1),
        "earlier": (p[:, None] < p[None, :]) * 1.0,
        "ones": np.ones((P, P)),
        "experts": np.tile(np.arange(E), (P, 1)),
        "base": np.tile(np.arange(E) * REGION, (P, 1)),
        "tiles": np.tile(np.arange(NTILE), (P, 1)),
        "tile_rows": np.tile(np.arange(NTILE) * P, (P, 1)),
        "digits": np.tile(float(E) ** (np.arange(NTILE + GROUP) % GROUP), (P, 1)),
        "powers": np.tile(2.0 ** np.arange(LEVELS), (P, 1)),
        "sign": np.where(p < N, 1.0, -1.0)[:, None],
    }
    at, where = 0, {}
    for name, a in cols.items():
        where[name] = (at, at + a.shape[1])
        at += a.shape[1]
    return np.concatenate(list(cols.values()), 1).astype(np.float32), where


def wait(eng, sem, count):
    if isinstance(count, int) and count <= 0:
        return
    eng.wait_ge(sem, count)


def wait_apart(eng, sem, count, reached):
    eng.wait_ge(reached, 1)
    wait(eng, sem, count)


class Pair:

    def __init__(self, n, half, par):
        self.n, self.half, self.par = n, half, par

    def step(self, k):
        return Pair(self.n + k, self.half + (self.par + k) // 2, (self.par + k) % 2)


def over_pairs(eng, body):
    for n in range(3):
        body(Pair(n, n // 2, n % 2))
    with eng.Fori(1, NPAIR // 2 - 1) as i:
        body(Pair(i * 2 + 1, i, 1))
        body(Pair(i * 2 + 2, i + 1, 0))
    body(Pair(NPAIR - 1, (NPAIR - 1) // 2, (NPAIR - 1) % 2))


FIRST, LAST = Pair(0, 0, 0), Pair(NPAIR - 1, (NPAIR - 1) // 2, (NPAIR - 1) % 2)


def is_first(pair):
    return isinstance(pair.n, int) and pair.n == 0


def is_last(pair):
    return isinstance(pair.n, int) and pair.n == NPAIR - 1


def semaphores(ctx, nc, prefix, names):
    sems = [nc.alloc_semaphore(name=prefix + n) for n in names.split()]
    ctx.callback(nc.clear_and_free_semaphores, sems)
    return sems


def memory(ctx, nc):
    def sb(name, *free, dt=F32):
        return ctx.enter_context(nc.sbuf_tensor(name, [P, *free], dt))

    _, where = constants()
    width = max(b for _, b in where.values())
    m = Names()
    m.const = sb("const", width)
    m.c = {name: m.const[:, a:b] for name, (a, b) in where.items()}
    m.psum = ctx.enter_context(nc.psum_tensor("banks", [P, 8, 512], F32))
    m.bank = [m.psum[:, i, :] for i in range(8)]
    m.bank12 = m.psum[:, 1:3, :]

    m.x = sb("x_rows", NCHUNK * D)
    m.moments = sb("moments", NCHUNK, 2)
    m.rstd = sb("input_rstd", NCHUNK)

    m.w_zkv = sb("w_zkv", 512)
    m.w_q = sb("w_q", D)
    m.w_qk = sb("w_qk", 2, 2, 2 * K)
    m.w_o = sb("w_o", D)
    m.g_norm = sb("g_norm", 1)
    m.w_router = sb("w_router", E)
    m.b_router = sb("b_router", E)
    m.w1 = sb("w1", E * FF)
    m.b1_rows = sb("b1_rows", P)
    m.b1 = sb("b1", E * FB)
    m.b2 = sb("b2_all", E * D)
    m.w2 = sb("w2", E * FB * D)
    m.b_in = sb("b_in", D)
    m.b_in_t = sb("b_in_t", P)
    m.b_in_swap = sb("b_in_swap", P)
    m.c_mats = sb("c_mats", 2 * P)
    m.w_out = sb("w_out", D)
    m.w_out_t = sb("w_out_t", D)
    m.out_cos = sb("out_cos", D)
    m.out_sin = sb("out_sin", D)
    m.out_x = sb("out_x", D)
    m.d_col = sb("d_col", 1)
    m.b_out = sb("b_out_rows", D)
    m.lam = sb("lam", 4)
    m.mag = sb("mag", P)
    m.turn_cos = sb("turn_cos", LEVELS)
    m.turn_sin = sb("turn_sin", LEVELS)
    m.cos = sb("cos_table", T)
    m.sin = sb("sin_table", T)
    m.gates = sb("gates", NPAIR * 4)
    m.chosen = sb("chosen", NPAIR * 4)
    m.slot_of = sb("slot_of", NPAIR * 4)
    m.slots = sb("slots", NPAIR * 4, dt=U32)
    m.next_slot = sb("next_slot", E)
    m.plan = sb("plan", NTILE + NGROUP + E, dt=I32)
    m.zero = sb("zero_rows", D)
    return m


def zero_padded_operands(ctx, nc):
    def sb2(name, *free):
        return [ctx.enter_context(nc.sbuf_tensor(f"{name}{i}", [P, *free], F32)) for i in range(2)]

    z = Names()
    z.kv = sb2("kv", 2, H, 2, B, K)
    z.q_t = sb2("q_t", 2, 2, 2, P)
    z.pt = ctx.enter_context(nc.sbuf_tensor("weights_t", [P, 2, 2, 2, P], F32))
    return z


def setup(nc, m, a, dram, z, loads):
    with ExitStack() as ctx:
        s = Names()
        s.dve, s.act = semaphores(ctx, nc, "su_", "dve act")
        s.memory_zero, s.stats, s.moments, s.rstd = semaphores(ctx, nc, "su_", "memory_zero stats moments rstd")
        th = ctx.enter_context(nc.sbuf_tensor("su_theta", [P, 2], F32))
        ang = ctx.enter_context(nc.sbuf_tensor("su_angles", [P, LEVELS], F32))
        turns = ctx.enter_context(nc.sbuf_tensor("su_turns", [P, LEVELS], F32))
        half = ctx.enter_context(nc.sbuf_tensor("su_half_sine", [P, LEVELS], F32))
        eL = ctx.enter_context(nc.sbuf_tensor("su_decay_rate", [P, 2], F32))
        stats = ctx.enter_context(nc.sbuf_tensor("su_stats", [P, NCHUNK, 6], F32))

        block = ctx.enter_context(nc.Block())

        @block.sync
        def _(sp):
            for w, (lo, hi) in (("Wf", (0, 256)), ("Wk", (256, 384)), ("Wv", (384, 512))):
                sp.dma_start(m.w_zkv[:, lo:hi], a["L0_attn_a_" + w]).then_inc(loads.attn, 16)
            sp.dma_start(m.w_q[:], a["L0_attn_a_Wq"]).then_inc(loads.attn, 16)
            sp.dma_start(m.w_o[:], a["L0_attn_a_Wo"]).then_inc(loads.attn, 16)
            g = a["L0_attn_a_g_norm_w"].rearrange("(v o) -> v o", o=1)
            for h in range(H):
                sp.dma_start(m.g_norm[K * h:K * h + K, :], g).then_inc(loads.attn, 16)
            sp.dma_start(m.w_router[:], a["L0_ffn_router_w"]).then_inc(loads.attn, 16)
            sp.dma_start(m.b_router[:], a["L0_ffn_router_b"].partition_broadcast(P)).then_inc(loads.attn, 16)

        @block.vector
        def _(dve):
            count = [0]

            def own(ins):
                count[0] += 1
                ins.then_inc(s.dve, 1)
                dve.wait_ge(s.dve, count[0])

            nc.vector.memset(m.zero[:], 0.0)
            own(nc.vector.memset(m.mag[:], 1.0))
            dve.wait_ge(loads.rates, 16 * 5)
            dve.wait_ge(s.act, 1)
            own(nc.vector.tensor_tensor(th[:, 0:1], m.lam[:, 1:2], m.lam[:, 3:4], ALU.mult))

            def within_half_turn(x, k):
                own(nc.vector.tensor_scalar(k, x, float(1 / (2 * np.pi)), ROUND, ALU.mult, ALU.add))
                own(nc.vector.tensor_scalar(k, k, -ROUND, None, ALU.add))
                for part in (TWO_PI_1, TWO_PI_2, TWO_PI_3):
                    own(nc.vector.scalar_tensor_tensor(x, k, -part, x, ALU.mult, ALU.add))

            within_half_turn(th[:, 0:1], th[:, 1:2])
            dve.wait_ge(loads.const, 16)
            own(nc.vector.tensor_scalar(ang[:], m.c["powers"], th[:, 0:1], None, ALU.mult))
            within_half_turn(ang[:], turns[:])
            own(nc.vector.tensor_scalar(ang[:], ang[:], 3.1415925, -3.1415925, ALU.min, ALU.max))
            assert count[0] == ANGLES_AT
            dve.wait_ge(loads.x, 16 * B)
            for c in range(NCHUNK):
                ins = nc.vector.bn_stats(stats[:, c, :], m.x[:, c * D:(c + 1) * D])
            ins.then_inc(s.stats, 1)
            dve.wait_ge(s.stats, 1)
            for c in range(NCHUNK):
                ins = nc.vector.bn_aggr(m.moments[:, c, :], stats[:, c, :])
            ins.then_inc(s.moments, 1)
            dve.wait_ge(s.moments, 1)
            nc.vector.tensor_scalar(m.rstd[:], m.moments[:, :, 1], EPS, None, ALU.add).then_inc(s.moments, 1)
            dve.wait_ge(loads.attn, 16 * (7 + H))
            own(nc.vector.tensor_scalar(m.w_o[:], m.w_o[:], m.g_norm[:], None, ALU.mult))
            for kind, w in enumerate((m.w_q[:], m.w_zkv[:, 256:384])):
                for e in range(2):
                    nc.vector.tensor_copy(m.w_qk[:, kind, e, :].rearrange("d (p k) -> d p k", p=2),
                                          w.rearrange("d (p e k) -> d p e k", p=2, e=2)[:, :, e, :])
            own(nc.vector.tensor_copy(m.next_slot[:], m.c["base"]))
            dve.wait_ge(s.act, 6)
            own(nc.vector.tensor_tensor(m.turn_cos[:], half[:], half[:], ALU.mult))
            own(nc.vector.tensor_scalar(m.turn_cos[:], m.turn_cos[:], -2.0, 1.0, ALU.mult, ALU.add))
            own(nc.vector.tensor_scalar(m.mag[:], m.mag[:], eL[:, 1:2], None, ALU.mult))

        @block.scalar
        def _(act):
            for i in range(2):
                half_ = slice(N * i, N * i + N)
                for col, name in ((0, "log_Lam_real"), (1, "Lam_imag")):
                    act.dma_start(m.lam[half_, col:col + 1],
                                  a["L0_attn_b_" + name].rearrange("(n o) -> n o", o=1)).then_inc(loads.rates, 16)
            act.dma_start(m.lam[:, 2:3], a["L0_attn_b_log_dt"].partition_broadcast(P)).then_inc(loads.rates, 16)
            act.dma_start(m.const[:], a["constants"]).then_inc(loads.const, 16)
            for b in range(B):
                act.dma_start(m.x[C * b:C * b + C, :].rearrange("p (c d) -> p c d", d=D),
                              a["L0_attn_a_x"][b].rearrange("(c t) d -> t c d", t=C)).then_inc(loads.x, 16)
            act.wait_ge(loads.rates, 16 * 5)
            nc.scalar.activation(m.lam[:, 3:4], m.lam[:, 2:3], ACT.Exp).then_inc(s.act, 1)
            nc.scalar.activation(eL[:, 0:1], m.lam[:, 0:1], ACT.Exp).then_inc(s.act, 1)
            act.wait_ge(s.act, 2)
            nc.scalar.mul(eL[:, 0:1], eL[:, 0:1], m.lam[:, 3:4]).then_inc(s.act, 1)
            act.wait_ge(s.act, 3)
            nc.scalar.activation(eL[:, 1:2], eL[:, 0:1], ACT.Exp, scale=-1.0).then_inc(s.act, 1)
            act.wait_ge(s.dve, ANGLES_AT)
            nc.scalar.activation(m.turn_sin[:], ang[:], ACT.Sin).then_inc(s.act, 1)
            nc.scalar.activation(half[:], ang[:], ACT.Sin, scale=0.5).then_inc(s.act, 1)
            nc.scalar.preload_act_table_set("natural_log_exp_and_others")
            act.wait_ge(s.moments, 2)
            nc.scalar.activation(m.rstd[:], m.rstd[:], ACT.Ln).then_inc(s.rstd, 1)
            act.wait_ge(s.rstd, 1)
            nc.scalar.activation(m.rstd[:], m.rstd[:], ACT.Exp, scale=-0.5).then_inc(s.rstd, 1)
            act.wait_ge(s.rstd, 2)

        @block.gpsimd
        def _(pool):
            for zeros in (*z.kv, *z.q_t, z.pt):
                ins = nc.gpsimd.memset(zeros[:], 0.0)
            ins.then_inc(s.memory_zero, 1)
            pool.wait_ge(s.memory_zero, 1)


def rotation_tables(nc, pool, m, s, product, product2):
    count = [0]

    def own(ins):
        count[0] += 1
        ins.then_inc(s.table, 1)
        pool.wait_ge(s.table, count[0])

    v = nc.gpsimd
    v.memset(m.cos[:, 0:1], 1.0)
    own(v.memset(m.sin[:, 0:1], 0.0))
    for k in range(LEVELS):
        n = 2 ** k
        old, new = slice(0, n), slice(n, 2 * n)
        c, d = m.turn_cos[:, k:k + 1], m.turn_sin[:, k:k + 1]
        v.tensor_scalar(product[:, old], m.sin[:, old], d, None, ALU.mult)
        v.tensor_scalar(product2[:, old], m.cos[:, old], d, None, ALU.mult)
        v.tensor_scalar(m.cos[:, new], m.cos[:, old], c, None, ALU.mult)
        own(v.tensor_scalar(m.sin[:, new], m.sin[:, old], c, None, ALU.mult))
        v.tensor_tensor(m.cos[:, new], m.cos[:, new], product[:, old], ALU.subtract)
        own(v.tensor_tensor(m.sin[:, new], m.sin[:, new], product2[:, old], ALU.add))
    own(v.tensor_scalar(m.sin[:], m.sin[:], m.c["sign"], None, ALU.mult))


def late_setup(nc, m, loads):
    with ExitStack() as ctx:
        s = Names()
        s.dve, s.pe = semaphores(ctx, nc, "sl_", "dve pe")
        block = ctx.enter_context(nc.Block())

        @block.sync
        def _(sp):
            sp.wait_ge(loads.late, 16 * LATE)

        @block.vector
        def _(dve):
            dve.wait_ge(loads.late, 16 * LATE)
            nc.vector.tensor_scalar(m.b_in[:], m.b_in[:], m.lam[:, 3:4], None, ALU.mult).then_inc(s.dve, 1)
            nc.vector.tensor_copy(m.c_mats[:, 192:256], m.c_mats[:, 0:64])
            nc.vector.tensor_scalar(m.c_mats[:, 128:192], m.c_mats[:, 64:128], -1.0, None, ALU.mult).then_inc(s.dve, 1)
            dve.wait_ge(s.dve, 2)
            nc.vector.tensor_scalar(m.c_mats[:, 64:128], m.c_mats[:, 64:128], -1.0, None, ALU.mult).then_inc(s.dve, 1)
            dve.wait_ge(s.pe, 1)
            nc.vector.tensor_copy(m.b_in_t[:], m.bank[0][:, 0:128])
            nc.vector.tensor_copy(m.b_in_swap[:, 0:64], m.bank[0][:, 64:128])
            nc.vector.tensor_copy(m.b_in_swap[:, 64:128], m.bank[0][:, 0:64])
            nc.vector.tensor_copy(m.w_out_t[:], m.bank[0][:, 128:256]).then_inc(s.dve, 1)
            dve.wait_ge(s.dve, 4)
            nc.vector.tensor_scalar(m.out_x[:], m.w_out_t[:], m.d_col[:], None, ALU.mult)
            nc.vector.tensor_copy(m.b1[:], m.bank[2][:, 0:E * FB])
            dve.wait_ge(s.pe, 2)
            nc.vector.tensor_copy(m.out_cos[:], m.bank[1][:, 0:128])
            nc.vector.tensor_copy(m.out_sin[:], m.bank[1][:, 128:256])

        @block.tensor
        def _(pe):
            pe.wait_ge(loads.late, 16 * LATE)
            pe.transpose(m.bank[2][:, 0:E * FB], m.b1_rows[0:E * FB, :], m.c["ident"][0:E * FB, 0:E * FB])
            pe.wait_ge(s.dve, 1)
            pe.transpose(m.bank[0][:, 0:128], m.b_in[:], m.c["ident"])
            pe.transpose(m.bank[0][:, 128:256], m.w_out[:], m.c["ident"]).then_inc(s.pe, 1)
            pe.wait_ge(s.dve, 4)
            pe.matmul(m.bank[1][:, 0:128], m.c_mats[:, 0:128], m.w_out_t[:], start=True, stop=True)
            pe.matmul(m.bank[1][:, 128:256], m.c_mats[:, 128:256], m.w_out_t[:], start=True, stop=True).then_inc(s.pe, 1)


def chunk_rows(m, n, u):
    return m.x[:, bass.ds((n.n * 2 + u) * D, D)]


class Norm:

    def __init__(self, sb, name):
        self.stats = sb(name + "_stats", 2, 6)
        self.mv = sb(name + "_mv", 2, 2)
        self.ve = sb(name + "_var_eps", 2)
        self.rstd = sb(name + "_rstd", 2)
        self.carrier = sb(name + "_carrier", 1)


class Route:

    def __init__(self, ctx, nc, m, a, dram, prefix):
        def sb(name, *free, dt=F32):
            return ctx.enter_context(nc.sbuf_tensor(prefix + name, [P, *free], dt))

        self.nc, self.m = nc, m
        self.rows_out = dram.inputs[0] if prefix == "ra_" else dram.inputs[1]
        self.s = Names()
        self.s.stats, self.s.mv, self.s.var_eps, self.s.rstd, self.s.xn, self.s.x_t_ps, self.s.x_t = \
            semaphores(ctx, nc, prefix, "stats mv var_eps rstd xn x_t_ps x_t")
        self.s.logits_ps, self.s.logits, self.s.top, self.s.index, self.s.index_f, self.s.picks, self.s.marked = \
            semaphores(ctx, nc, prefix, "logits_ps logits top index index_f picks marked")
        self.s.margin, self.s.exp_margin, self.s.gate_sum, self.s.gate1, self.s.gates = \
            semaphores(ctx, nc, prefix, "margin exp_margin gate_sum gate1 gates")
        self.s.rank_ps, self.s.place, self.s.moved, self.s.picked, self.s.slot_f, self.s.slots = \
            semaphores(ctx, nc, prefix, "rank_ps place moved picked slot_f slots")
        self.s.scattered0, self.s.scattered1, self.s.plan = \
            semaphores(ctx, nc, prefix, "scattered0 scattered1 plan")
        self.s.marks, = semaphores(ctx, nc, prefix, "marks")
        self.s.planned, self.s.tails_out = \
            semaphores(ctx, nc, prefix, "planned tails_out")
        self.ln = Norm(sb, "ln")
        self.xn = [sb(f"xn{i}", 2, D) for i in range(2)]
        self.x_t = sb("x_t", 2, P)
        self.logits = sb("logits", 2, E)
        self.top = sb("top", 2, 8)
        self.index = sb("index", 2, 8, dt=U32)
        self.index_f = sb("index_f", 2, 2)
        self.picks = sb("picks", 2, 2, E)
        self.marked = sb("marked", 2, E)
        self.before = sb("before", 3, E)
        self.margin = sb("margin", 2)
        self.e_margin = sb("exp_margin", 2)
        self.gate_sum = sb("gate_sum", 2)
        self.gates = sb("gates", 2, 2)
        self.place = sb("place", 2, E)
        self.picked = sb("picked", 2, 2, E)
        self.carrier = sb("carrier", 1)
        self.slot_f = sb("slot_f", 4)
        self.slots = [sb(f"slots{i}", 4, dt=U32) for i in range(2)]
        self.count = sb("count", E)
        self.tiles = sb("expert_tiles", E)
        self.tiles_to = sb("tiles_up_to", E)
        self.cmp = sb("compare", NTILE, E)
        self.cmp_row = sb("compare_row", NPAIR * 4, E)
        self.lead = sb("lead", NPAIR * 4)
        self.owner = sb("owner", NTILE)
        self.digits = sb("digits", NTILE + GROUP)
        self.four = sb("four_digits", NGROUP + 1)
        self.three = sb("three_digits", NGROUP + 1)
        self.row = sb("row", NTILE)
        self.spare = sb("spare", NTILE)

    def scattered(self, par):
        return (self.s.scattered0, self.s.scattered1)[par]

    def vector_norm(self, dve, n):
        nc, s, ln = self.nc, self.s, self.ln
        wait(dve, self.x_written, n.n + 1)
        nc.vector.memset(ln.carrier[:], 0.0)
        for u in range(2):
            ins = nc.vector.bn_stats(ln.stats[:, u, :], chunk_rows(self.m, n, u))
        ins.then_inc(s.stats, 1)
        wait(dve, s.stats, n.n + 1)
        nc.vector.memset(ln.carrier[:], 0.0)
        for u in range(2):
            nc.vector.bn_aggr(ln.mv[:, u, :], ln.stats[:, u, :]).then_inc(s.mv, 1)
        wait(dve, s.mv, (n.n + 1) * 2)
        nc.vector.tensor_scalar(ln.ve[:], ln.mv[:, :, 1], EPS, None, ALU.add).then_inc(s.var_eps, 1)

    def gpsimd_norm(self, pool, n, minus_half):
        wait(pool, self.s.var_eps, n.n + 1)
        wait(pool, self.s.xn, n.n)
        self.nc.gpsimd.tensor_tensor(self.ln.rstd[:], self.ln.ve[:], minus_half[:, 0, 0:2], ALU.pow).then_inc(self.s.rstd, 1)

    def vector_normed(self, dve, n):
        wait(dve, self.s.rstd, n.n + 1)
        wait(dve, self.scattered(n.par), n.half * 64)
        for u in range(2):
            ins = self.nc.vector.tensor_scalar(self.xn[n.par][:, u, :], chunk_rows(self.m, n, u),
                                               self.ln.mv[:, u, 0:1], self.ln.rstd[:, u:u + 1], ALU.subtract, ALU.mult)
        ins.then_inc(self.s.xn, 1)

    def tensor_transposed(self, pe, n):
        m, s = self.m, self.s
        wait(pe, s.xn, n.n + 1)
        wait(pe, s.moved, n.n)
        for u in range(2):
            mm = pe.transpose(self.bank[:, P * u:P * u + P], self.xn[n.par][:, u, :], m.c["ident"])
        mm.then_inc(s.x_t_ps, 1)

    def tensor_logits(self, pe, n):
        m, s, bank = self.m, self.s, self.bank
        wait(pe, s.x_t, n.n + 1)
        for u in range(2):
            mm = pe.matmul(bank[:, E * u:E * u + E], self.x_t[:, u, :], m.w_router[:], start=True, stop=True)
        mm.then_inc(s.logits_ps, 1)

    def tensor_ranks(self, pe, n):
        m, s, bank = self.m, self.s, self.bank
        wait(pe, s.marked, n.n + 1)
        pe.matmul(bank[:, 0:3 * E], m.c["ones"], self.before[:].rearrange("p k e -> p (k e)"), start=True, stop=False,
                  skip_group_check=True)
        pe.matmul(bank[:, 0:2 * E], m.c["earlier"], self.marked[:].rearrange("p u e -> p (u e)"), start=False, stop=True,
                  skip_group_check=True).then_inc(s.rank_ps, 1)

    def tensor(self, pe, n):
        self.tensor_transposed(pe, n)
        self.tensor_logits(pe, n)
        self.tensor_ranks(pe, n)

    def scalar_transposed(self, act, n):
        wait(act, self.s.x_t_ps, n.n + 1)
        wait(act, self.s.logits_ps, n.n)
        self.nc.scalar.copy(self.x_t[:].rearrange("p u t -> p (u t)"), self.bank[:, 0:256]).then_inc(self.s.x_t, 1)

    def scalar_margin(self, act, n):
        wait(act, self.s.margin, n.n + 1)
        wait(act, self.s.gates, n.n)
        self.nc.scalar.activation(self.e_margin[:], self.margin[:], ACT.Exp).then_inc(self.s.exp_margin, 1)

    def scalar(self, act, n):
        self.scalar_transposed(act, n)
        self.scalar_margin(act, n)

    def vector_choose(self, dve, n):
        nc, m, s = self.nc, self.m, self.s
        wait(dve, s.logits_ps, n.n + 1)
        nc.vector.tensor_tensor(self.logits[:], self.bank[:, 0:2 * E].rearrange("p (u e) -> p u e", u=2),
                                m.b_router[:].unsqueeze(1).to_broadcast([P, 2, E]), ALU.add).then_inc(s.logits, 1)
        wait_apart(dve, s.logits, n.n + 1, self.ready)
        for u in range(2):
            nc.vector.max(self.top[:, u, :], self.logits[:, u, :]).then_inc(s.top, 1)
        wait(dve, s.top, (n.n + 1) * 2)
        nc.vector.tensor_tensor(self.margin[:], self.top[:, :, 1], self.top[:, :, 0], ALU.subtract).then_inc(s.margin, 1)
        for u in range(2):
            nc.vector.max_index(self.index[:, u, :], self.top[:, u, :], self.logits[:, u, :]).then_inc(s.index, 1)
        wait(dve, s.index, (n.n + 1) * 2)
        nc.vector.tensor_copy(self.index_f[:], self.index[:, :, 0:2]).then_inc(s.index_f, 1)
        wait(dve, s.index_f, n.n + 1)
        nc.vector.tensor_tensor(self.picks[:].rearrange("p u k e -> p (u k) e"),
                                m.c["experts"].unsqueeze(1).to_broadcast([P, 4, E]),
                                self.index_f[:].rearrange("p u k -> p (u k)").unsqueeze(2).to_broadcast([P, 4, E]),
                                ALU.is_equal).then_inc(s.picks, 1)
        nc.vector.tensor_copy(m.chosen[:, bass.ds(n.n * 4, 4)], self.index_f[:].rearrange("p u k -> p (u k)"))
        wait(dve, s.picks, n.n + 1)
        nc.vector.tensor_tensor(self.marked[:], self.picks[:, :, 0, :], self.picks[:, :, 1, :], ALU.add).then_inc(s.marks, 1)
        nc.vector.tensor_tensor(self.before[:, 1, :], self.picks[:, 0, 0, :], self.picks[:, 0, 1, :], ALU.add)
        wait(dve, s.marks, n.n + 1)
        nc.vector.tensor_tensor(self.before[:, 2, :], self.marked[:, 0, :], self.marked[:, 1, :], ALU.add).then_inc(s.marked, 1)
        wait(dve, s.exp_margin, n.n + 1)
        nc.vector.tensor_scalar(self.gate_sum[:], self.e_margin[:], 1.0, None, ALU.add).then_inc(s.gate_sum, 1)
        wait(dve, s.gate_sum, n.n + 1)
        nc.vector.reciprocal(self.gates[:, :, 0], self.gate_sum[:]).then_inc(s.gate1, 1)
        wait(dve, s.gate1, n.n + 1)
        nc.vector.tensor_tensor(self.gates[:, :, 1], self.gates[:, :, 0], self.e_margin[:], ALU.mult).then_inc(s.gates, 1)
        wait(dve, s.gates, n.n + 1)
        nc.vector.memset(self.carrier[:], 0.0)
        nc.vector.tensor_copy(m.gates[:, bass.ds(n.n * 4, 4)], self.gates[:].rearrange("p u k -> p (u k)"))

    def vector_place(self, dve, n):
        nc, m, s = self.nc, self.m, self.s
        wait(dve, s.rank_ps, n.n + 1)
        nc.vector.tensor_tensor(self.place[:], self.bank[:, 0:2 * E].rearrange("p (u e) -> p u e", u=2),
                                m.next_slot[:].unsqueeze(1).to_broadcast([P, 2, E]), ALU.add).then_inc(s.place, 1)
        wait(dve, s.place, n.n + 1)
        nc.vector.tensor_tensor(m.next_slot[:], m.next_slot[:], self.bank[:, 2 * E:3 * E], ALU.add).then_inc(s.moved, 1)
        wait(dve, s.place, n.n + 1)
        for u in range(2):
            ins = nc.vector.tensor_tensor(self.picked[:, u], self.picks[:, u],
                                          self.place[:, u, :].unsqueeze(1).to_broadcast([P, 2, E]), ALU.mult)
        ins.then_inc(s.picked, 1)
        wait(dve, s.picked, n.n + 1)
        nc.vector.tensor_reduce(self.slot_f[:], self.picked[:].rearrange("p u k e -> p (u k) e"), AX_X,
                                ALU.add).then_inc(s.slot_f, 1)
        wait(dve, s.slot_f, n.n + 1)
        nc.vector.tensor_copy(self.slots[n.par][:], self.slot_f[:]).then_inc(s.slots, 1)
        nc.vector.tensor_copy(m.slot_of[:, bass.ds(n.n * 4, 4)], self.slot_f[:])

    def gpsimd_scatter(self, pool, n):
        wait_apart(pool, self.s.slots, n.n + 1, self.ready)
        for u in range(2):
            for k in range(2):
                self.nc.gpsimd.indirect_dma_start(
                    self.rows_out[:, :], bass.IndirectOffsetOnAxis(ap=self.slots[n.par][:, 2 * u + k:2 * u + k + 1], axis=0),
                    self.xn[n.par][:, u, :], None).then_inc(self.scattered(n.par), 16)

    def gpsimd_wait(self, pool):
        for par in range(2):
            pool.wait_ge(self.scattered(par), 64 * (NPAIR // 2))

    def vector_plan(self, dve):
        nc, m, s = self.nc, self.m, self.s
        steps = [0]

        def own(ins):
            steps[0] += 1
            ins.then_inc(s.plan, 1)
            dve.wait_ge(s.plan, steps[0])

        dve.wait_ge(s.moved, NPAIR)
        own(nc.vector.tensor_tensor(self.count[:], m.next_slot[:], m.c["base"], ALU.subtract))
        own(nc.vector.tensor_scalar(self.tiles[:], self.count[:], 1.0 / P, 0.5 - 0.5 / P, ALU.mult, ALU.add))
        own(nc.vector.tensor_scalar(self.tiles[:], self.tiles[:], ROUND, None, ALU.add))
        own(nc.vector.tensor_scalar(self.tiles[:], self.tiles[:], -ROUND, None, ALU.add))
        own(nc.vector.tensor_tensor_scan(self.tiles_to[:], m.c["ones"][:, 0:E], self.tiles[:], 0.0, ALU.mult, ALU.add))
        by_tile = [P, NTILE, E]
        own(nc.vector.tensor_tensor(self.cmp[:], self.tiles_to[:].unsqueeze(1).to_broadcast(by_tile),
                                    m.c["tiles"].unsqueeze(2).to_broadcast(by_tile), ALU.is_le))
        own(nc.vector.tensor_reduce(self.owner[:], self.cmp[:], AX_X, ALU.add))
        own(nc.vector.tensor_tensor(self.tiles[:], self.tiles[:], self.tiles_to[:], ALU.subtract))
        own(nc.vector.scalar_tensor_tensor(self.tiles[:], self.tiles[:], float(P), m.c["base"], ALU.mult, ALU.add))
        own(nc.vector.tensor_tensor(self.cmp[:], self.owner[:].unsqueeze(2).to_broadcast(by_tile),
                                    m.c["experts"].unsqueeze(1).to_broadcast(by_tile), ALU.is_equal))
        own(nc.vector.tensor_tensor(self.cmp[:], self.cmp[:], self.tiles[:].unsqueeze(1).to_broadcast(by_tile), ALU.mult))
        own(nc.vector.tensor_reduce(self.row[:], self.cmp[:], AX_X, ALU.add))
        own(nc.vector.tensor_tensor(self.row[:], self.row[:], m.c["tile_rows"], ALU.add))
        own(nc.vector.tensor_scalar(self.spare[:], self.owner[:], float(E), float(SPARE), ALU.is_equal, ALU.mult))
        own(nc.vector.tensor_tensor(self.row[:], self.row[:], self.spare[:], ALU.add))
        by_row = [P, NPAIR * 4, E]
        own(nc.vector.tensor_tensor(self.cmp_row[:], m.chosen[:].unsqueeze(2).to_broadcast(by_row),
                                    m.c["experts"].unsqueeze(1).to_broadcast(by_row), ALU.is_equal))
        own(nc.vector.tensor_tensor(self.cmp_row[:], self.cmp_row[:], self.tiles[:].unsqueeze(1).to_broadcast(by_row), ALU.mult))
        own(nc.vector.tensor_reduce(self.lead[:], self.cmp_row[:], AX_X, ALU.add))
        nc.vector.tensor_tensor(m.slots[:], m.slot_of[:], self.lead[:], ALU.subtract)
        nc.vector.tensor_copy(m.plan[:, 0:NTILE], self.row[:])
        own(nc.vector.memset(self.digits[:], 0.0))
        own(nc.vector.scalar_tensor_tensor(self.digits[:, 0:NTILE], self.owner[:], float(E - 1), m.c["digits"][:, 0:NTILE],
                                           ALU.min, ALU.mult))
        by_group = self.digits[:].rearrange("p (q k) -> p q k", k=GROUP)
        own(nc.vector.tensor_reduce(self.four[:], by_group, AX_X, ALU.add))
        own(nc.vector.tensor_reduce(self.three[:], by_group[:, :, 0:3], AX_X, ALU.add))
        nc.vector.scalar_tensor_tensor(m.plan[:, NTILE:NTILE + NGROUP], self.three[:, 1:], float(E ** GROUP),
                                       self.four[:, 0:NGROUP], ALU.mult, ALU.add)
        nc.vector.tensor_copy(m.plan[:, NTILE + NGROUP:], m.next_slot[:]).then_inc(s.planned, 1)

    def sync_tails(self, sp):
        sp.wait_ge(self.s.planned, 1)
        for e in range(E):
            row = sp.value_load(self.m.plan[0:1, NTILE + NGROUP + e:NTILE + NGROUP + e + 1], min_val=e * REGION,
                                max_val=e * REGION + B * T)
            sp.dma_start(self.rows_out[bass.ds(row, P), :], self.m.zero[:]).then_inc(self.s.tails_out, 16)
        sp.wait_ge(self.s.tails_out, 16 * E)


def attention_and_route(nc, m, a, dram, z, loads):
    with ExitStack() as ctx:
        def sb(name, *free, dt=F32):
            return ctx.enter_context(nc.sbuf_tensor("at_" + name, [P, *free], dt))

        def sb2(name, *free, dt=F32):
            return [sb(f"{name}{i}", *free, dt=dt) for i in range(2)]

        s = Names()
        s.xn, s.x_t_ps, s.x_t = semaphores(ctx, nc, "at_", "xn x_t_ps x_t")
        s.z_ps, s.qk_ps, s.exp_z, s.exp_kqk, s.capped, s.log1, s.soft = \
            semaphores(ctx, nc, "at_", "z_ps qk_ps exp_z exp_kqk capped log1 soft")
        s.ge_ready, s.v_ready, s.sig_sum, s.sig, s.k_ready, s.q_ready, s.kt_ready = \
            semaphores(ctx, nc, "at_", "ge_ready v_ready sig_sum sig k_ready q_ready kt_ready")
        s.g_ps, s.d_ps, s.d_sb, s.decays, s.s_ready, s.a_ps, s.a_sb = \
            semaphores(ctx, nc, "at_", "g_ps d_ps d_sb decays s_ready a_ps a_sb")
        s.st_ps, s.st_sb, s.u_ps, s.t0, s.st1, s.t1, s.d01 = \
            semaphores(ctx, nc, "at_", "st_ps st_sb u_ps t0 st1 t1 d01")
        s.st0, s.sk_ps, s.sk_sb, s.r_ps, s.logits, s.maxes, s.shifted = \
            semaphores(ctx, nc, "at_", "st0 sk_ps sk_sb r_ps logits maxes shifted")
        s.probs, s.sums, s.pw, s.pt_ps, s.pt_sb, s.b_ps, s.b_sb = \
            semaphores(ctx, nc, "at_", "probs sums pw pt_ps pt_sb b_ps b_sb")
        s.o_ps, s.sq, s.ms, s.s2, s.oe, s.o_rstd, s.on = \
            semaphores(ctx, nc, "at_", "o_ps sq ms s2 oe o_rstd on")
        s.ot_ps, s.ot_sb, s.y_ps, s.x1, s.d10, s.const_ready, s.q_spread = \
            semaphores(ctx, nc, "at_", "ot_ps ot_sb y_ps x1 d10 const_ready q_spread")
        s.sig_log, s.o_log, s.table = semaphores(ctx, nc, "at_", "sig_log o_log table")
        table_product, table_product2 = sb("table_product", T), sb("table_product2", T)
        r = Route(ctx, nc, m, a, dram, "ra_")
        ln = Norm(sb, "ln")
        xn = sb("xn", 2, D)
        x_t = sb("x_t", 2, P)
        exp_z = sb("exp_z", 2, 256)
        exp_kqk = sb("exp_kqk", 768)
        sig = sb("sigmoid", 768)
        soft = sb("softplus", 2, 256)
        ge = sb("ge", 2, 256)
        e_minus = sb("e_minus", 2, 256)
        e_plus = sb2("e_plus", 2, 256)
        slot = sb2("slot", 2, 256)
        kv, q_t, pt_sb = z.kv, z.q_t, z.pt
        q_raw = sb("q_raw", 2, 2, C)
        k_t = sb2("k_t", 2, 2, C)
        d_sb = sb2("span_decays", 2, 2, 2, 2)
        a_sb = sb("a_masked", 2, 2, 2, C)
        st_sb = sb("slot_t", 2, 2, P)
        st0, st1 = sb("state_even", 2, 2, 2, K), sb("state_odd", 2, 2, 2, K)
        t0, t1 = sb("sum_even", 2, 2, 2, K), sb("sum_odd", 2, 2, 2, K)
        d01 = sb("decay_even", 2, 2)
        d10 = sb("decay_odd", 2, 2)
        sk_sb = sb2("state_k_t", P)
        logits = sb("logits", 2, H, M)
        maxes = sb("maxes", 2, H)
        probs = sb("probs", 2, H, M)
        sums = sb("sums", 2, H)
        pw = sb("weights", 2, H * M)
        b_sb = sb("b_masked", 2, H, C)
        sq = sb("squares", 2, H, K)
        ms = sb("mean_squares", 2, H)
        s2 = sb("sums_squared", 2, H)
        o_rstd = sb("o_rstd", 2, H)
        minus_half = sb("minus_half", 2, H)
        on = sb("o_normed", 2, D)
        ot_sb = sb("o_t", 2, P)

        r.bank, r.ready, r.x_written = m.bank[7], s.const_ready, s.x1
        xt_ps = m.bank[0]
        z_ps = m.bank12
        y_ps, ot_ps = m.bank[1], m.bank[2]
        qk_ps = m.bank[3]
        e_ps = m.bank[4]
        f_ps = m.bank[5]
        g_ps = m.bank[6]
        h_ps = m.bank[7]

        block = ctx.enter_context(nc.Block())

        @block.tensor
        def _(pe):
            def x_transposed(n):
                wait(pe, s.xn, n.n + 1)
                wait(pe, s.decays, n.n)
                for u in range(2):
                    mm = pe.transpose(xt_ps[:, P * u:P * u + P], xn[:, u, :], m.c["ident"])
                mm.then_inc(s.x_t_ps, 1)

            def project(n):
                wait(pe, s.x_t, n.n + 1)
                wait(pe, s.soft, n.n)
                wait(pe, s.k_ready, n.n)
                wait(pe, s.x1, n.n - 1)
                for u in range(2):
                    mm = pe.matmul(z_ps[:, u, :], x_t[:, u, :], m.w_zkv[:], start=True, stop=True)
                mm.then_inc(s.z_ps, 1)

            def project_transposed(n):
                wait(pe, s.a_sb, n.n)
                for kind in range(2):
                    for e in range(2):
                        for b in range(B):
                            mm = pe.matmul(qk_ps[64 * b:64 * b + 64, 256 * kind + 128 * e:256 * kind + 128 * e + 128]
                                           .rearrange("p (u t) -> p u t", u=2),
                                           m.w_qk[:, kind, e, :],
                                           x_t[:, :, C * b:C * b + C], start=True, stop=True)
                mm.then_inc(s.qk_ps, 1)

            def gate_sums(n):
                wait(pe, s.soft, n.n + 1)
                wait(pe, s.x_t, n.n + 1)
                for u in range(2):
                    mm = pe.matmul(xt_ps[:, 256 * u:256 * u + 256], m.c["cum"], soft[:, u, :], start=True, stop=True)
                mm.then_inc(s.g_ps, 1)

            def span_sums(n):
                wait(pe, s.soft, n.n + 1)
                for u in range(2):
                    for p in range(2):
                        mm = pe.matmul(h_ps[:, 8 * u:8 * u + 8].rearrange("s (b k p) -> s b k p", b=2, k=2)[:, :, :, p],
                                       soft[:, u, P * p:P * p + P], m.c["spans"], start=True, stop=True)
                mm.then_inc(s.d_ps, 1)

            def attend(n):
                wait(pe, s.kt_ready, n.n + 1)
                wait(pe, s.q_spread, n.n + 1)
                for u in range(2):
                    for e in range(2):
                        for b in range(B):
                            at = 256 * u + 128 * e
                            mm = pe.matmul(qk_ps[64 * b:64 * b + 64, at:at + 128].rearrange("j (p t) -> j p t", p=2),
                                           k_t[n.par][:, e, u, :], q_t[n.par][:, u, e, :, C * b:C * b + C],
                                           start=True, stop=True)
                mm.then_inc(s.a_ps, 1)

            def state_transposed(n, u):
                state = (st0, st1)[u]
                if u == 0:
                    wait(pe, s.st0, n.n + 1)
                    wait(pe, r.s.moved, n.n - 1)
                else:
                    wait(pe, s.st1, n.n + 1)
                    wait(pe, s.sk_sb, n.n * 2 + 1)
                pe.transpose(h_ps[:, 0:P], state[:, 0].rearrange("p b h k -> p (b h k)"), m.c["ident"]).then_inc(s.sk_ps, 1)

            def slots_transposed(n):
                wait(pe, s.s_ready, n.n + 1)
                wait(pe, s.pt_sb, n.n)
                for u in range(2):
                    for p in range(2):
                        at = 256 * u + P * p
                        mm = pe.transpose(f_ps[:, at:at + P], slot[n.par][:, u, P * p:P * p + P], m.c["ident"])
                mm.then_inc(s.st_ps, 1)

            def updates(n):
                wait(pe, s.k_ready, n.n + 1)
                wait(pe, s.v_ready, n.n + 1)
                wait(pe, s.b_sb, n.n)
                for u in range(2):
                    for h in range(H):
                        out = (g_ps[64 * (h % 2):64 * (h % 2) + 64, 256 * u:256 * u + 256]
                               .rearrange("s (c b p k) -> s c b p k", c=2, b=2, p=2)[:, :, :, h // 2, :])
                        mm = pe.matmul(out, slot[n.par][:, u, M * h:M * h + M], kv[n.par][:, u, h], start=True, stop=True)
                mm.then_inc(s.u_ps, 1)

            def raw_logits(n, u):
                if u == 0:
                    wait(pe, s.sq, n.n)
                    wait(pe, s.on, n.n)
                    wait(pe, s.a_sb, n.n + 1)
                wait(pe, s.sk_sb, n.n * 2 + u + 1)
                for h in range(H):
                    at, e = 256 * u + M * h, h % 2
                    pe.matmul(e_ps[:, at:at + M], q_t[n.par][:, u, e, h // 2, :], sk_sb[u][:, M * e:M * e + M],
                              start=(u == 0 and h == 0), stop=False, skip_group_check=True)
                for b in range(B):
                    for h in range(H):
                        rows, at = slice(64 * b, 64 * b + 64), 256 * u + M * h
                        mm = pe.matmul(e_ps[rows, at:at + M], a_sb[rows, u, h % 2, h // 2, :],
                                       slot[n.par][rows, u, M * h:M * h + M], start=False, stop=True,
                                       skip_group_check=True)
                if u == 1:
                    mm.then_inc(s.r_ps, 1)

            def weights_transposed(n):
                wait(pe, s.pw, n.n + 1)
                wait(pe, s.st_sb, n.n + 1)
                for u in range(2):
                    for p in range(2):
                        at = 256 * u + P * p
                        mm = pe.transpose(f_ps[:, at:at + P], pw[:, u, P * p:P * p + P], m.c["ident"])
                mm.then_inc(s.pt_ps, 1)

            def weights_by_slots(n):
                wait(pe, s.pt_sb, n.n + 1)
                wait(pe, s.t1, n.n + 1)
                for u in range(2):
                    for p in range(2):
                        for b in range(B):
                            at = 256 * u + 128 * p
                            mm = pe.matmul(g_ps[64 * b:64 * b + 64, at:at + 128].rearrange("j (e t) -> j e t", e=2),
                                           st_sb[:, u, p, C * b:C * b + C], pt_sb[:, u, p, :, C * b:C * b + C],
                                           start=True, stop=True)
                mm.then_inc(s.b_ps, 1)

            parts = [(u, b, h) for u in range(2) for b in range(B) for h in range(H)]

            def outputs_of_states(n, some):
                for u, b, h in some:
                    pe.matmul(e_ps[64 * b:64 * b + 64, D * u + K * h:D * u + K * h + K],
                              pt_sb[:, u, h // 2, h % 2, C * b:C * b + C], (st0, st1)[u][:, 1, b, h // 2, :],
                              start=(u == 0 and h == 0), stop=False, skip_group_check=True)

            def outputs_of_pair(n):
                wait(pe, s.b_sb, n.n + 1)
                outputs_of_states(n, parts[-1:])
                for u, b, h in parts:
                    rows = slice(64 * b, 64 * b + 64)
                    mm = pe.matmul(e_ps[rows, D * u + K * h:D * u + K * h + K], b_sb[rows, u, h, :],
                                   kv[n.par][rows, u, h, 1, b, :], start=False, stop=True, skip_group_check=True)
                mm.then_inc(s.o_ps, 1)

            def o_transposed(n):
                if not is_last(n):
                    wait(pe, s.soft, n.n + 2)
                    wait(pe, s.k_ready, n.n + 2)
                wait(pe, s.on, n.n + 1)
                for u in range(2):
                    mm = pe.transpose(ot_ps[:, P * u:P * u + P], on[:, u, :], m.c["ident"])
                mm.then_inc(s.ot_ps, 1)

            def project_out(n):
                wait(pe, s.ot_sb, n.n + 1)
                for u in range(2):
                    mm = pe.matmul(y_ps[:, D * u:D * u + D], ot_sb[:, u, :], m.w_o[:], start=True, stop=True)
                mm.then_inc(s.y_ps, 1)

            def body(n):
                state_transposed(n, 0)
                if not is_last(n):
                    x_transposed(n.step(1))
                raw_logits(n, 0)
                state_transposed(n, 1)
                if not is_last(n):
                    project(n.step(1))
                raw_logits(n, 1)
                if not is_last(n):
                    project_transposed(n.step(1))
                weights_transposed(n)
                if not is_last(n):
                    gate_sums(n.step(1))
                weights_by_slots(n)
                outputs_of_states(n, parts[:-1])
                wait(pe, s.sk_sb, n.n * 2 + 2)
                if not is_last(n):
                    span_sums(n.step(1))
                outputs_of_pair(n)
                if not is_first(n):
                    wait(pe, s.d_sb, n.n + 2 if not is_last(n) else NPAIR)
                    r.tensor_transposed(pe, n.step(-1))
                if not is_last(n):
                    attend(n.step(1))
                if not is_first(n):
                    r.tensor_logits(pe, n.step(-1))
                if not is_last(n):
                    slots_transposed(n.step(1))
                o_transposed(n)
                if not is_last(n):
                    updates(n.step(1))
                project_out(n)
                if not is_first(n):
                    r.tensor_ranks(pe, n.step(-1))

            x_transposed(FIRST)
            project(FIRST)
            project_transposed(FIRST)
            gate_sums(FIRST)
            span_sums(FIRST)
            attend(FIRST)
            slots_transposed(FIRST)
            updates(FIRST)
            pe.wait_ge(s.d_sb, 1)
            over_pairs(pe, body)
            r.tensor(pe, LAST)

        @block.vector
        def _(dve):
            def normed(n):
                wait(dve, s.x_t_ps, n.n)
                for u in range(2):
                    c = n.n * 2 + u
                    at = slice(c, c + 1) if isinstance(c, int) else bass.ds(c, 1)
                    ins = nc.vector.tensor_scalar(xn[:, u, :], chunk_rows(m, n, u), m.moments[:, at, 0], m.rstd[:, at],
                                                  ALU.subtract, ALU.mult)
                ins.then_inc(s.xn, 1)

            def gates_and_values(n):
                wait(dve, s.exp_z, n.n + 1)
                nc.vector.tensor_scalar(exp_z[:], exp_z[:], LN_MAX, None, ALU.min).then_inc(s.capped, 1)
                wait(dve, s.o_ps, n.n - 1)
                for b in range(B):
                    rows = slice(64 * b, 64 * b + 64)
                    ins = nc.vector.tensor_copy(kv[n.par][rows, :, :, 1, b, :],
                                                z_ps[rows, :, 384:512].rearrange("p u (h k) -> p u h k", h=H))
                ins.then_inc(s.v_ready, 1)

            def cap_sigmoids(n):
                wait(dve, s.exp_kqk, n.n + 1)
                nc.vector.tensor_scalar(exp_kqk[:], exp_kqk[:], LN_MAX, None, ALU.min).then_inc(s.sig_sum, 1)

            def gated(n):
                wait(dve, s.sig, n.n + 1)
                for b in range(B):
                    rows = slice(64 * b, 64 * b + 64)
                    ins = nc.vector.tensor_tensor(kv[n.par][rows, :, :, 0, b, :],
                                                  z_ps[rows, :, 256:384].rearrange("p u (h k) -> p u h k", h=H),
                                                  sig[rows, 0:256].rearrange("p (u h k) -> p u h k", u=2, h=H), ALU.mult)
                ins.then_inc(s.k_ready, 1)
                wait(dve, s.q_spread, n.n)
                nc.vector.scalar_tensor_tensor(q_raw[:].rearrange("p e u t -> p (e u t)"), qk_ps[:, 0:256],
                                               float(K) ** -0.5, sig[:, 256:512], ALU.mult, ALU.mult).then_inc(s.q_ready, 1)
                nc.vector.tensor_tensor(k_t[n.par][:].rearrange("p e u t -> p (e u t)"), qk_ps[:, 256:512],
                                        sig[:, 512:768], ALU.mult).then_inc(s.kt_ready, 1)

            def softplus(n):
                wait(dve, s.log1, n.n + 1)
                nc.vector.scalar_tensor_tensor(soft[:], z_ps[:, :, 0:256], -1.0, exp_z[:], ALU.mult, ALU.max).then_inc(s.soft, 1)

            def slots(n):
                wait(dve, s.decays, n.n + 1)
                wait(dve, s.r_ps, n.n - 1)
                nc.vector.scalar_tensor_tensor(slot[n.par][:], ge[:], 1.0, e_minus[:], ALU.subtract, ALU.mult,
                                               reverse0=True).then_inc(s.s_ready, 1)

            def causal():
                return m.c["causal"].unsqueeze(1).to_broadcast([P, 2 * H, C])

            def mask_a(n):
                wait(dve, s.a_ps, n.n + 1)
                wait(dve, s.r_ps, n.n)
                nc.vector.tensor_tensor(a_sb[:].rearrange("j u e p t -> j (u e p) t"),
                                        qk_ps.rearrange("p (a t) -> p a t", t=C), causal(), ALU.mult).then_inc(s.a_sb, 1)

            def new_states(n):
                wait(dve, s.d_sb, n.n + 1)
                wait(dve, s.st0, n.n + 1)
                wait(dve, s.u_ps, n.n + 1)
                nc.vector.tensor_tensor(t0[:].rearrange("p c b h k -> p (c b h k)"), st0[:].rearrange("p c b h k -> p (c b h k)"),
                                        g_ps[:, 0:256], ALU.add).then_inc(s.t0, 1)
                nc.vector.tensor_tensor(d01[:], d_sb[n.par][:, 0, :, 0, :], d_sb[n.par][:, 1, :, 1, :],
                                        ALU.mult).then_inc(s.d01, 1)
                wait(dve, s.d01, n.n + 1)
                nc.vector.tensor_tensor(st1[:].rearrange("p c b h k -> p c (b h) k"), t0[:].rearrange("p c b h k -> p c (b h) k"),
                                        d01[:].rearrange("p b h -> p (b h)").unsqueeze(2).unsqueeze(1).to_broadcast([P, 2, 4, K]),
                                        ALU.mult).then_inc(s.st1, 1)
                wait(dve, s.st1, n.n + 1)
                nc.vector.tensor_tensor(t1[:].rearrange("p c b h k -> p (c b h k)"), st1[:].rearrange("p c b h k -> p (c b h k)"),
                                        g_ps[:, 256:512], ALU.add).then_inc(s.t1, 1)

            def carry_state(n):
                wait(dve, s.d_sb, n.n + 2)
                nc.vector.tensor_tensor(d10[:], d_sb[n.par][:, 1, :, 0, :], d_sb[1 - n.par][:, 0, :, 1, :],
                                        ALU.mult).then_inc(s.d10, 1)
                wait(dve, s.d10, n.n + 1)
                wait(dve, s.o_ps, n.n + 1)
                nc.vector.tensor_tensor(st0[:].rearrange("p c b h k -> p c (b h) k"), t1[:].rearrange("p c b h k -> p c (b h) k"),
                                        d10[:].rearrange("p b h -> p (b h)").unsqueeze(2).unsqueeze(1).to_broadcast([P, 2, 4, K]),
                                        ALU.mult).then_inc(s.st0, 1)

            def flat(x):
                return x[:].rearrange("p u h m -> p (u h) m")

            def softmax_in(n):
                wait(dve, s.r_ps, n.n + 1)
                nc.vector.tensor_tensor(logits[:].rearrange("p u h m -> p (u h m)"), e_ps,
                                        e_plus[n.par][:].rearrange("p u m -> p (u m)"), ALU.mult).then_inc(s.logits, 1)
                wait(dve, s.logits, n.n + 1)
                nc.vector.tensor_reduce(maxes[:].rearrange("p u h -> p (u h)"), flat(logits), AX_X, ALU.max).then_inc(s.maxes, 1)
                wait(dve, s.maxes, n.n + 1)
                nc.vector.tensor_tensor(flat(logits), flat(logits),
                                        maxes[:].rearrange("p u h -> p (u h)").unsqueeze(2).to_broadcast([P, 2 * H, M]),
                                        ALU.subtract).then_inc(s.shifted, 1)

            def softmax_out(n):
                wait(dve, s.probs, n.n + 1)
                nc.vector.tensor_tensor(pw[:].rearrange("p u m -> p (u m)"), probs[:].rearrange("p u h m -> p (u h m)"),
                                        e_plus[n.par][:].rearrange("p u m -> p (u m)"), ALU.mult).then_inc(s.pw, 1)
                nc.vector.tensor_reduce(sums[:].rearrange("p u h -> p (u h)"), flat(probs), AX_X, ALU.add).then_inc(s.sums, 1)

            def mask_b(n):
                wait(dve, s.b_ps, n.n + 1)
                nc.vector.tensor_tensor(b_sb[:].rearrange("p u h t -> p (u h) t"),
                                        g_ps.rearrange("p (a t) -> p a t", t=C), causal(), ALU.mult).then_inc(s.b_sb, 1)

            def out_norm_start(n):
                wait(dve, s.sums, n.n + 1)
                nc.vector.tensor_tensor(s2[:], sums[:], sums[:], ALU.mult).then_inc(s.s2, 1)
                wait(dve, s.sq, n.n + 1)
                nc.vector.tensor_reduce(ms[:].rearrange("p u h -> p (u h)"), flat(sq), AX_X, ALU.add).then_inc(s.ms, 1)
                wait(dve, s.ms, n.n + 1)
                nc.vector.scalar_tensor_tensor(ms[:], s2[:], EPS, ms[:], ALU.mult, ALU.add).then_inc(s.oe, 1)

            def out_norm(n):
                wait(dve, s.o_rstd, n.n + 1)
                nc.vector.tensor_tensor(on[:].rearrange("p u (h k) -> p (u h) k", h=H),
                                        e_ps[:, 0:256].rearrange("p (a k) -> p a k", k=K),
                                        o_rstd[:].rearrange("p u h -> p (u h)").unsqueeze(2).to_broadcast([P, 2 * H, K]),
                                        ALU.mult).then_inc(s.on, 1)

            def residual(n):
                wait(dve, s.y_ps, n.n + 1)
                x = m.x[:, bass.ds(n.n * 2 * D, 2 * D)]
                nc.vector.tensor_tensor(x, y_ps[:, 0:256], x, ALU.add).then_inc(s.x1, 1)

            def body(n):
                mask_a(n)
                if not is_last(n):
                    normed(n.step(1))
                if not is_first(n) and not is_first(n.step(-1)):
                    r.vector_choose(dve, n.step(-2))
                if not is_first(n):
                    residual(n.step(-1))
                if not is_first(n) and not is_first(n.step(-1)):
                    r.vector_place(dve, n.step(-2))
                new_states(n)
                if not is_first(n):
                    r.vector_norm(dve, n.step(-1))
                if not is_last(n):
                    gates_and_values(n.step(1))
                softmax_in(n)
                if not is_last(n):
                    cap_sigmoids(n.step(1))
                softmax_out(n)
                if not is_last(n):
                    softplus(n.step(1))
                    gated(n.step(1))
                if not is_first(n):
                    r.vector_normed(dve, n.step(-1))
                mask_b(n)
                if not is_last(n):
                    slots(n.step(1))
                out_norm_start(n)
                if not is_last(n):
                    carry_state(n)
                out_norm(n)

            nc.vector.memset(st0[:], 0.0).then_inc(s.st0, 1)
            nc.vector.memset(r.before[:, 0, :], 0.0)
            nc.vector.memset(minus_half[:], -0.5).then_inc(s.const_ready, 1)
            normed(FIRST)
            gates_and_values(FIRST)
            cap_sigmoids(FIRST)
            softplus(FIRST)
            gated(FIRST)
            slots(FIRST)
            over_pairs(dve, body)
            r.vector_choose(dve, LAST.step(-1))
            residual(LAST)
            r.vector_place(dve, LAST.step(-1))
            r.vector_norm(dve, LAST)
            r.vector_normed(dve, LAST)
            r.vector_choose(dve, LAST)
            r.vector_place(dve, LAST)
            r.vector_plan(dve)

        @block.scalar
        def _(act):
            def x_transposed(n):
                wait(act, s.x_t_ps, n.n + 1)
                wait(act, s.qk_ps, n.n)
                nc.scalar.copy(x_t[:].rearrange("p u t -> p (u t)"), xt_ps[:, 0:256]).then_inc(s.x_t, 1)

            def exps(n):
                wait(act, s.z_ps, n.n + 1)
                wait(act, s.sig, n.n)
                nc.scalar.activation(exp_kqk[:, 0:256].rearrange("p (u d) -> p u d", u=2), z_ps[:, :, 256:384], ACT.Exp,
                                     scale=-1.0)
                wait(act, s.soft, n.n)
                nc.scalar.activation(exp_z[:], z_ps[:, :, 0:256], ACT.Exp, scale=-1.0).then_inc(s.exp_z, 1)
                wait(act, s.qk_ps, n.n + 1)
                nc.scalar.activation(exp_kqk[:, 256:768], qk_ps, ACT.Exp, scale=-1.0).then_inc(s.exp_kqk, 1)

            def spread_q(n):
                wait(act, s.q_ready, n.n + 1)
                wait(act, s.r_ps, n.n - 1)
                for b in range(B):
                    for p in range(2):
                        rows = slice(64 * b + 32 * p, 64 * b + 32 * p + 32)
                        ins = nc.scalar.copy(q_t[n.par][rows, :, :, p, C * b:C * b + C],
                                             q_raw[rows].rearrange("k e u t -> k u e t"))
                ins.then_inc(s.q_spread, 1)

            def sigmoids(n):
                wait(act, s.sig_sum, n.n + 1)
                wait(act, s.kt_ready, n.n)
                nc.scalar.activation(sig[:], exp_kqk[:], ACT.Ln, bias=1.0).then_inc(s.sig_log, 1)
                wait(act, s.sig_log, n.n + 1)
                nc.scalar.activation(sig[:], sig[:], ACT.Exp, scale=-1.0).then_inc(s.sig, 1)

            def log1(n):
                wait(act, s.capped, n.n + 1)
                nc.scalar.activation(exp_z[:], exp_z[:], ACT.Ln, bias=1.0).then_inc(s.log1, 1)

            def decays(n):
                wait(act, s.soft, n.n + 1)
                wait(act, s.s_ready, n.n)
                nc.scalar.activation(ge[:], soft[:], ACT.Exp, scale=-1 / GATE_NORM).then_inc(s.ge_ready, 1)
                wait(act, s.g_ps, n.n + 1)
                wait(act, s.pw, n.n - 1)
                nc.scalar.activation(e_plus[n.par][:].rearrange("p u m -> p (u m)"), xt_ps, ACT.Exp)
                nc.scalar.activation(e_minus[:].rearrange("p u m -> p (u m)"), xt_ps, ACT.Exp, scale=-1.0).then_inc(s.decays, 1)
                wait(act, s.d_ps, n.n + 1)
                wait(act, s.d10, n.n - 1)
                nc.scalar.activation(d_sb[n.par][:].rearrange("s u b k p -> s (u b k p)"), h_ps[:, 0:16],
                                     ACT.Exp).then_inc(s.d_sb, 1)

            def state_transposed(n, u):
                wait(act, s.sk_ps, n.n * 2 + u + 1)
                wait(act, s.r_ps, n.n)
                nc.scalar.copy(sk_sb[u][:], h_ps[:, 0:P]).then_inc(s.sk_sb, 1)

            def slots_transposed(n):
                wait(act, s.st_ps, n.n + 1)
                wait(act, s.b_ps, n.n)
                nc.scalar.copy(st_sb[:].rearrange("p u h t -> p (u h t)"), f_ps).then_inc(s.st_sb, 1)

            def probabilities(n):
                wait(act, s.shifted, n.n + 1)
                wait(act, s.pw, n.n)
                nc.scalar.activation(probs[:], logits[:], ACT.Exp).then_inc(s.probs, 1)

            def weights_transposed(n):
                wait(act, s.pt_ps, n.n + 1)
                wait(act, s.o_ps, n.n)
                for e in range(2):
                    rows = slice(64 * e, 64 * e + 64)
                    ins = nc.scalar.copy(pt_sb[rows, :, :, e, :], f_ps[rows, :].rearrange("s (u p t) -> s u p t", u=2, p=2))
                ins.then_inc(s.pt_sb, 1)

            def squares(n):
                wait(act, s.o_ps, n.n + 1)
                wait(act, s.ms, n.n)
                nc.scalar.activation(sq[:].rearrange("p u h k -> p (u h k)"), e_ps[:, 0:256], ACT.Square,
                                     scale=float(K) ** -0.5).then_inc(s.sq, 1)

            def o_transposed(n):
                wait(act, s.ot_ps, n.n + 1)
                wait(act, s.y_ps, n.n)
                nc.scalar.copy(ot_sb[:].rearrange("p u t -> p (u t)"), ot_ps[:, 0:256]).then_inc(s.ot_sb, 1)

            def output_rstd(n):
                wait(act, s.oe, n.n + 1)
                wait(act, s.on, n.n)
                nc.scalar.activation(o_rstd[:], ms[:], ACT.Ln).then_inc(s.o_log, 1)
                wait(act, s.o_log, n.n + 1)
                nc.scalar.activation(o_rstd[:], o_rstd[:], ACT.Exp, scale=-0.5).then_inc(s.o_rstd, 1)

            def body(n):
                state_transposed(n, 0)
                if not is_last(n):
                    x_transposed(n.step(1))
                state_transposed(n, 1)
                if not is_last(n):
                    exps(n.step(1))
                    log1(n.step(1))
                probabilities(n)
                if not is_last(n):
                    sigmoids(n.step(1))
                weights_transposed(n)
                if not is_last(n):
                    decays(n.step(1))
                    spread_q(n.step(1))
                squares(n)
                output_rstd(n)
                if not is_first(n):
                    r.scalar_transposed(act, n.step(-1))
                if not is_last(n):
                    slots_transposed(n.step(1))
                o_transposed(n)
                if not is_first(n):
                    r.scalar_margin(act, n.step(-1))

            nc.scalar.preload_act_table_set("natural_log_exp_and_others")
            x_transposed(FIRST)
            exps(FIRST)
            log1(FIRST)
            sigmoids(FIRST)
            spread_q(FIRST)
            decays(FIRST)
            slots_transposed(FIRST)
            over_pairs(act, body)
            r.scalar(act, LAST)

        @block.gpsimd
        def _(pool):
            def body(n):
                if not is_first(n):
                    r.gpsimd_norm(pool, n.step(-1), minus_half)
                    r.gpsimd_scatter(pool, n.step(-1))

            rotation_tables(nc, pool, m, s, table_product, table_product2)
            pool.wait_ge(s.const_ready, 1)
            over_pairs(pool, body)
            r.gpsimd_norm(pool, LAST, minus_half)
            r.gpsimd_scatter(pool, LAST)
            r.gpsimd_wait(pool)

        @block.sync
        def _(sp):
            for i, side in enumerate(("real", "imag")):
                half_ = slice(N * i, N * i + N)
                sp.dma_start(m.b_in[half_, :], a["L0_attn_b_B_" + side]).then_inc(loads.late, 16)
                sp.dma_start(m.c_mats[:, half_], a["L0_attn_b_C_" + side]).then_inc(loads.late, 16)
            sp.dma_start(m.w_out[:], a["L0_attn_b_W_out"]).then_inc(loads.late, 16)
            sp.dma_start(m.d_col[:], a["L0_attn_b_D"].rearrange("(h o) -> h o", o=1)).then_inc(loads.late, 16)
            sp.dma_start(m.b_out[:], a["L0_attn_b_b_out"].partition_broadcast(P)).then_inc(loads.late, 16)
            sp.dma_start(m.w1[:].rearrange("p (e f) -> p e f", e=E),
                         a["L0_ffn_W1"].rearrange("e d f -> d e f")).then_inc(loads.late, 16)
            for e in range(E):
                sp.dma_start(m.w2[:, e * FF:(e + 1) * FF].rearrange("f (k d) -> f k d", k=FB),
                             a["L0_ffn_W2"][e].rearrange("(k f) d -> f k d", f=P)).then_inc(loads.late, 16)
            sp.dma_start(m.b1_rows[0:E * FB, :], a["L0_ffn_b1"].rearrange("e (k f) -> (e k) f", f=P)).then_inc(loads.late, 16)
            sp.dma_start(m.b2[:], a["L0_ffn_b2"].rearrange("e d -> (e d)").partition_broadcast(P)).then_inc(loads.late, 16)
            for rows in dram.inputs:
                for i in range(E):
                    sp.dma_start(rows[E * REGION + i * P:E * REGION + (i + 1) * P, :], m.zero[:]).then_inc(loads.late, 16)
            r.sync_tails(sp)


_INS = """L0_attn_a_x L0_attn_a_Wq L0_attn_a_Wk L0_attn_a_Wv L0_attn_a_Wf L0_attn_a_g_norm_w L0_attn_a_Wo
L0_attn_b_log_Lam_real L0_attn_b_Lam_imag L0_attn_b_B_real L0_attn_b_B_imag L0_attn_b_C_real L0_attn_b_C_imag
L0_attn_b_D L0_attn_b_log_dt L0_attn_b_W_out L0_attn_b_b_out L0_ffn_router_w L0_ffn_router_b L0_ffn_W1 L0_ffn_b1
L0_ffn_W2 L0_ffn_b2""".split()


def experts(nc, m, rows_in, rows_out, prefix):
    with ExitStack() as ctx:
        def sb(name, *free, dt=F32):
            return ctx.enter_context(nc.sbuf_tensor(prefix + name, [P, *free], dt))

        s = Names()
        s.x_t_ps, s.x_t, s.w1, s.h_ps, s.h_act, s.h_dve, s.y_ps, s.y = \
            semaphores(ctx, nc, prefix, "x_t_ps x_t w1 h_ps h_act h_dve y_ps y")
        loaded = semaphores(ctx, nc, prefix, "rows_in0 rows_in1 rows_in2 rows_in3")
        stored = semaphores(ctx, nc, prefix, "rows_out0 rows_out1 rows_out2 rows_out3")
        x_in = [sb(f"x_in{j}", D) for j in range(GROUP)]
        x_t = [sb(f"x_t{j}", P) for j in range(2)]
        w1 = [sb(f"w1_of_tile{j}", FF) for j in range(GROUP)]
        h = [sb(f"h{j}", FB, P) for j in range(2)]
        y = [sb(f"y{j}", D) for j in range(GROUP)]
        x_ps, h_ps, y_ps = m.bank[0:2], (m.bank[2:4], m.bank[4:6]), m.bank[6:8]

        block = ctx.enter_context(nc.Block())

        LASTQ = NGROUP - 1

        def ends(q, j):
            return isinstance(q, int) and q * GROUP + j >= NTILE

        def plan_value(eng, at, most):
            at = slice(at, at + 1) if isinstance(at, int) else bass.ds(at, 1)
            return eng.value_load(m.plan[0:1, at], min_val=0, max_val=most)

        def experts_of(eng, q):
            digits = plan_value(eng, q + NTILE, E ** (GROUP + 3) - 1)
            return [(digits >> (3 * k)) & (E - 1) for k in range(GROUP + 3)]

        def over_groups(eng, group):
            group(0)
            with eng.Fori(1, LASTQ) as q:
                group(q)
            group(LASTQ)

        @block.sync
        def _(sp):
            def load(t, q, j):
                row = plan_value(sp, t, ROWS - P)
                wait(sp, s.x_t_ps, t - GROUP + 1)
                sp.dma_start(x_in[j][:], rows_in[bass.ds(row, P), :]).then_inc(loaded[j], 16)

            def group(q):
                for j in range(GROUP):
                    load(q * GROUP + (j + GROUP), q + 1, j)

            for j in range(GROUP):
                load(j, 0, j)
            group(0)
            with sp.Fori(1, LASTQ) as q:
                group(q)

        @block.gpsimd
        def _(pool):
            def group(q):
                for j in range(GROUP):
                    t = q * GROUP + j
                    wait(pool, s.y, t + 1)
                    pool.dma_start(rows_out[bass.ds(t * P, P), :], y[j][:]).then_inc(stored[j], 16)

            over_groups(pool, group)
            for j in range(GROUP):
                pool.wait_ge(stored[j], 16 * NGROUP)

        @block.tensor
        def _(pe):
            def transposed(t, q, j):
                wait(pe, loaded[j], (q + 1) * 16)
                wait(pe, s.x_t, t - 1)
                pe.transpose(x_ps[j % 2][:, 0:P], x_in[j][:], m.c["ident"]).then_inc(s.x_t_ps, 1)

            def hidden(t, j):
                wait(pe, s.x_t, t + 1)
                wait(pe, s.w1, t + 1)
                wait(pe, s.h_act, t - 1)
                wait(pe, s.h_dve, t - 1)
                for f in range(FB):
                    mm = pe.matmul(h_ps[j % 2][f // 2][:, P * (f % 2):P * (f % 2) + P],
                                   w1[j % GROUP][:, P * f:P * f + P], x_t[j % 2][:], start=True, stop=True)
                mm.then_inc(s.h_ps, 1)

            def result(t, j, owner):
                wait(pe, s.h_act, t + 1)
                wait(pe, s.h_dve, t + 1)
                wait(pe, s.y, t - 1)
                for f in range(FB):
                    mm = pe.matmul(y_ps[j % 2][:, 0:D], h[j % 2][:, f, :], m.w2[:, bass.ds(owner * FF + D * f, D)],
                                   start=(f == 0), stop=(f == FB - 1))
                mm.then_inc(s.y_ps, 1)

            def group(q):
                owner = experts_of(pe, q)
                for j in range(GROUP):
                    t = q * GROUP + j
                    if not ends(q, j + 1):
                        hidden(t + 1, j + 1)
                    if not ends(q, j + 2):
                        transposed(t + 2, q + (j + 2) // GROUP, (j + 2) % GROUP)
                    result(t, j, owner[j])

            transposed(0, 0, 0)
            hidden(0, 0)
            transposed(1, 0, 1)
            over_groups(pe, group)

        @block.vector
        def _(dve):
            def hidden(t, j, owner):
                wait(dve, s.h_ps, t + 1)
                wait(dve, s.y_ps, t - 1)
                for f in range(FB // 2, FB):
                    ins = nc.vector.tensor_scalar(h[j % 2][:, f, :], h_ps[j % 2][1][:, P * (f % 2):P * (f % 2) + P],
                                                  m.b1[:, bass.ds(owner * FB + f, 1)], 0.0, ALU.add, ALU.max)
                ins.then_inc(s.h_dve, 1)

            def result(t, q, j, owner):
                wait(dve, s.y_ps, t + 1)
                wait(dve, stored[j], q * 16)
                nc.vector.tensor_tensor(y[j][:], y_ps[j % 2][:, 0:D], m.b2[:, bass.ds(owner * D, D)], ALU.add).then_inc(s.y, 1)

            def group(q):
                owner = experts_of(dve, q)
                for j in range(GROUP):
                    if not ends(q, j + 1):
                        hidden(q * GROUP + j + 1, j + 1, owner[j + 1])
                    result(q * GROUP + j, q, j, owner[j])

            hidden(0, 0, experts_of(dve, 0)[0])
            over_groups(dve, group)

        @block.scalar
        def _(act):
            def x_transposed(t, j):
                wait(act, s.x_t_ps, t + 1)
                nc.scalar.copy(x_t[j % 2][:], x_ps[j % 2][:, 0:P]).then_inc(s.x_t, 1)

            def weights(j, owner):
                nc.scalar.copy(w1[j % GROUP][:], m.w1[:, bass.ds(owner * FF, FF)]).then_inc(s.w1, 1)

            def hidden(t, j, owner):
                if isinstance(t, int) and t == NTILE - 1:
                    act.wait_ge(s.h_ps, NTILE)
                for f in range(FB // 2):
                    ins = nc.scalar.activation(h[j % 2][:, f, :], h_ps[j % 2][0][:, P * (f % 2):P * (f % 2) + P],
                                               ACT.Relu, bias=m.b1[:, bass.ds(owner * FB + f, 1)])
                ins.then_inc(s.h_act, 1)

            def group(q):
                owner = experts_of(act, q)
                for j in range(GROUP):
                    if not ends(q, j + 2):
                        x_transposed(q * GROUP + j + 2, j)
                    if not ends(q, j + 3):
                        weights(j + 3, owner[j + 3])
                    if not ends(q, j + 1):
                        hidden(q * GROUP + j + 1, j + 1, owner[j + 1])

            owner = experts_of(act, 0)
            for t in range(2):
                weights(t, owner[t])
                x_transposed(t, t)
            weights(2, owner[2])
            hidden(0, 0, owner[0])
            over_groups(act, group)


class Gather:

    def __init__(self, ctx, nc, m, rows, ready, prefix):
        def sb(name, *free, dt=F32):
            return ctx.enter_context(nc.sbuf_tensor(prefix + name, [P, *free], dt))

        self.nc, self.m, self.rows, self.ready = nc, m, rows, ready
        self.s = Names()
        self.s.index, self.s.carried, self.s.in0, self.s.in1, self.s.weighed, self.s.both, self.s.sum = \
            semaphores(ctx, nc, prefix, "index carried in0 in1 weighed both sum")
        self.index = [sb(f"index{i}", 4, dt=U32) for i in range(2)]
        self.y = [sb(f"y{i}", 4, D) for i in range(2)]
        self.weighed = sb("weighed", 4, D)
        self.both = sb("both", 2, D)
        self.pool_carrier = sb("pool_carrier", 1)
        self.zeros = m.zero[:, 0:1]
        self.carrier = sb("carrier", 1)

    def arrived(self, par):
        return (self.s.in0, self.s.in1)[par]

    def vector_index(self, dve, n):
        if not isinstance(n.n, int) or n.n > 1:
            wait(dve, self.s.weighed, n.n - 1)
            self.nc.vector.memset(self.carrier[:], 0.0)
        self.nc.vector.tensor_copy(self.index[n.par][:], self.m.slots[:, bass.ds(n.n * 4, 4)]).then_inc(self.s.index, 1)

    def gpsimd(self, pool, n):
        wait(pool, self.s.carried, n.n)
        wait(pool, self.s.index, n.n + 1)
        self.nc.gpsimd.tensor_tensor(self.pool_carrier[:], self.zeros, self.zeros, ALU.add).then_inc(self.s.carried, 1)
        for j in range(4):
            self.nc.gpsimd.indirect_dma_start(
                self.y[n.par][:, j, :], None, self.rows[:, :],
                bass.IndirectOffsetOnAxis(ap=self.index[n.par][:, j:j + 1], axis=0)).then_inc(self.arrived(n.par), 16)

    def vector_sum(self, dve, n, out):
        nc, m, s = self.nc, self.m, self.s
        wait(dve, self.arrived(n.par), (n.half + 1) * 64)
        nc.vector.tensor_tensor(self.weighed[:], self.y[n.par][:],
                                m.gates[:, bass.ds(n.n * 4, 4)].unsqueeze(2).to_broadcast([P, 4, D]),
                                ALU.mult).then_inc(s.weighed, 1)
        wait(dve, s.weighed, n.n + 1)
        w = self.weighed[:].rearrange("p (u k) d -> p u k d", k=2)
        nc.vector.tensor_tensor(self.both[:], w[:, :, 0, :], w[:, :, 1, :], ALU.add).then_inc(s.both, 1)
        wait(dve, s.both, n.n + 1)
        nc.vector.tensor_tensor(out, self.both[:].rearrange("p u d -> p (u d)"), m.x[:, bass.ds(n.n * 2 * D, 2 * D)],
                                ALU.add).then_inc(s.sum, 1)


def space_and_route(nc, m, a, dram):
    with ExitStack() as ctx:
        def sb(name, *free, dt=F32):
            return ctx.enter_context(nc.sbuf_tensor("sp_" + name, [P, *free], dt))

        s = Names()
        s.const_ready, s.stats, s.mv, s.var_eps, s.rstd, s.xn, s.x_t_ps = \
            semaphores(ctx, nc, "sp_", "const_ready stats mv var_eps rstd xn x_t_ps")
        s.x_t, s.in_ps, s.in_cos, s.in_sin, s.turned, s.state, s.back_cos = \
            semaphores(ctx, nc, "sp_", "x_t in_ps in_cos in_sin turned state back_cos")
        s.back_sin, s.out_ps, s.x3, s.next_slot = \
            semaphores(ctx, nc, "sp_", "back_sin out_ps x3 next_slot")
        r = Route(ctx, nc, m, a, dram, "rb_")
        g = Gather(ctx, nc, m, dram.results[0], s.const_ready, "ga_")
        r.bank, r.ready, r.x_written = m.bank[7], s.const_ready, s.x3
        ln = Norm(sb, "ln")
        x2 = sb("x2", 2, D)
        xn = sb("xn", 2, D)
        x_t = [sb(f"x_t{i}", 2, P) for i in range(2)]
        in_cos = sb("in_cos", B, 2, C)
        in_sin = sb("in_sin", B, 2, C)
        turned = sb("turned", B, 2 * C)
        state = [sb(f"state{i}", B, 2 * C) for i in range(2)]
        back_cos = sb("back_cos", 2, B, C)
        back_sin = sb("back_sin", 2, B, C)
        minus_half = sb("minus_half", 2, H)
        t_ps, in_ps, out_ps = m.bank[0], m.bank[1], m.bank[2]

        block = ctx.enter_context(nc.Block())

        @block.tensor
        def _(pe):
            def body(n):
                wait(pe, s.xn, n.n + 1)
                for u in range(2):
                    mm = pe.transpose(t_ps[:, P * u:P * u + P], xn[:, u, :], m.c["ident"])
                mm.then_inc(s.x_t_ps, 1)
                wait(pe, s.x_t, n.n + 1)
                wait(pe, s.in_sin, n.n)
                x_all = x_t[n.par][:].rearrange("p u t -> p (u t)")
                pe.matmul(in_ps[:, 0:256], m.b_in_t[:], x_all, start=True, stop=True)
                pe.matmul(in_ps[:, 256:512], m.b_in_swap[:], x_all, start=True, stop=True).then_inc(s.in_ps, 1)
                if not is_first(n):
                    r.tensor(pe, n.step(-1))
                wait(pe, s.back_sin, n.n + 1)
                wait(pe, s.x3, n.n)
                for u in range(2):
                    out = out_ps[:, D * u:D * u + D]
                    pe.matmul(out, back_cos[:, u].rearrange("s b t -> s (b t)"), m.out_cos[:], start=True, stop=False)
                    pe.matmul(out, back_sin[:, u].rearrange("s b t -> s (b t)"), m.out_sin[:], start=False, stop=False)
                    pe.matmul(out, x_t[n.par][:, u, :], m.out_x[:], start=False, stop=False)
                    mm = pe.matmul(out, m.c["ones"][0:1, :], m.b_out[0:1, :], start=False, stop=True)
                mm.then_inc(s.out_ps, 1)

            over_pairs(pe, body)
            r.tensor(pe, LAST)

        @block.vector
        def _(dve):
            def table(t, n):
                return (t[:, bass.ds(n.n * 2 * C, 2 * C)].rearrange("s (u t) -> s u t", u=2)
                        .unsqueeze(2).to_broadcast([P, 2, B, C]))

            def start(n):
                g.vector_sum(dve, n, x2[:].rearrange("p u d -> p (u d)"))
                wait(dve, g.s.sum, n.n + 1)
                nc.vector.memset(ln.carrier[:], 0.0)
                for u in range(2):
                    ins = nc.vector.bn_stats(ln.stats[:, u, :], x2[:, u, :])
                ins.then_inc(s.stats, 1)
                wait(dve, s.stats, n.n + 1)
                nc.vector.memset(ln.carrier[:], 0.0)
                for u in range(2):
                    ins = nc.vector.bn_aggr(ln.mv[:, u, :], ln.stats[:, u, :])
                ins.then_inc(s.mv, 1)
                wait(dve, s.mv, n.n + 1)
                nc.vector.tensor_scalar(ln.ve[:], ln.mv[:, :, 1], EPS, None, ALU.add).then_inc(s.var_eps, 1)
                wait(dve, s.rstd, n.n + 1)
                for u in range(2):
                    ins = nc.vector.tensor_scalar(xn[:, u, :], x2[:, u, :], ln.mv[:, u, 0:1], ln.rstd[:, u:u + 1],
                                                  ALU.subtract, ALU.mult)
                ins.then_inc(s.xn, 1)

            def recur(n):
                wait(dve, s.in_ps, n.n + 1)
                nc.vector.tensor_tensor(in_cos[:].rearrange("s b u t -> s u b t"),
                                        in_ps[:, 0:256].rearrange("s (u b t) -> s u b t", u=2, b=B),
                                        table(m.cos, n), ALU.mult).then_inc(s.in_cos, 1)
                nc.vector.tensor_tensor(in_sin[:].rearrange("s b u t -> s u b t"),
                                        in_ps[:, 256:512].rearrange("s (u b t) -> s u b t", u=2, b=B),
                                        table(m.sin, n), ALU.mult).then_inc(s.in_sin, 1)
                wait(dve, s.in_sin, n.n + 1)
                nc.vector.tensor_tensor(turned[:].rearrange("s b t -> s (b t)"), in_cos[:].rearrange("s b u t -> s (b u t)"),
                                        in_sin[:].rearrange("s b u t -> s (b u t)"), ALU.add).then_inc(s.turned, 1)
                wait(dve, s.turned, n.n + 1)
                for b in range(B):
                    before = 0.0 if is_first(n) else state[1 - n.par][:, b, 2 * C - 1:2 * C]
                    ins = nc.vector.tensor_tensor_scan(state[n.par][:, b, :], m.mag[:], turned[:, b, :], before,
                                                       ALU.mult, ALU.add)
                ins.then_inc(s.state, 1)
                wait(dve, s.state, n.n + 1)
                wait(dve, s.out_ps, n.n)
                for t, out, done in ((m.cos, back_cos, s.back_cos), (m.sin, back_sin, s.back_sin)):
                    nc.vector.tensor_tensor(out[:], state[n.par][:].rearrange("s b (u t) -> s u b t", u=2),
                                            table(t, n), ALU.mult).then_inc(done, 1)

            def end(n):
                wait(dve, s.out_ps, n.n + 1)
                nc.vector.tensor_tensor(m.x[:, bass.ds(n.n * 2 * D, 2 * D)], out_ps[:, 0:256],
                                        x2[:].rearrange("p u d -> p (u d)"), ALU.add).then_inc(s.x3, 1)

            def body(n):
                if not is_last(n):
                    g.vector_index(dve, n.step(1))
                start(n)
                if not is_first(n):
                    r.vector_norm(dve, n.step(-1))
                    r.vector_normed(dve, n.step(-1))
                recur(n)
                if not is_first(n):
                    r.vector_choose(dve, n.step(-1))
                    r.vector_place(dve, n.step(-1))
                end(n)

            nc.vector.tensor_copy(m.next_slot[:], m.c["base"]).then_inc(s.next_slot, 1)
            dve.wait_ge(s.next_slot, 1)
            nc.vector.memset(r.before[:, 0, :], 0.0)
            nc.vector.memset(minus_half[:], -0.5).then_inc(s.const_ready, 1)
            g.vector_index(dve, FIRST)
            over_pairs(dve, body)
            r.vector_norm(dve, LAST)
            r.vector_normed(dve, LAST)
            r.vector_choose(dve, LAST)
            r.vector_place(dve, LAST)
            r.vector_plan(dve)

        @block.scalar
        def _(act):
            def body(n):
                wait(act, s.x_t_ps, n.n + 1)
                wait(act, s.out_ps, n.n - 1)
                nc.scalar.copy(x_t[n.par][:].rearrange("p u t -> p (u t)"), t_ps[:, 0:256]).then_inc(s.x_t, 1)
                if not is_first(n):
                    r.scalar(act, n.step(-1))

            over_pairs(act, body)
            r.scalar(act, LAST)

        @block.gpsimd
        def _(pool):
            def body(n):
                if not is_last(n):
                    g.gpsimd(pool, n.step(1))
                wait(pool, s.var_eps, n.n + 1)
                wait(pool, s.xn, n.n)
                nc.gpsimd.tensor_tensor(ln.rstd[:], ln.ve[:], minus_half[:, 0, 0:2], ALU.pow).then_inc(s.rstd, 1)
                if not is_first(n):
                    r.gpsimd_norm(pool, n.step(-1), minus_half)
                    r.gpsimd_scatter(pool, n.step(-1))

            pool.wait_ge(s.const_ready, 1)
            g.gpsimd(pool, FIRST)
            over_pairs(pool, body)
            r.gpsimd_norm(pool, LAST, minus_half)
            r.gpsimd_scatter(pool, LAST)
            r.gpsimd_wait(pool)
            pool.wait_ge(g.s.carried, NPAIR)

        @block.sync
        def _(sp):
            r.sync_tails(sp)


def gather_and_store(nc, m, rows, out):
    with ExitStack() as ctx:
        s = Names()
        s.const_ready, s.out0, s.out1 = \
            semaphores(ctx, nc, "go_", "const_ready out0 out1")
        stored = [s.out0, s.out1]
        g = Gather(ctx, nc, m, rows, s.const_ready, "gb_")
        x4 = [ctx.enter_context(nc.sbuf_tensor(f"go_x4_{i}", [P, 2, D], F32)) for i in range(2)]
        block = ctx.enter_context(nc.Block())

        @block.vector
        def _(dve):
            def body(n):
                if not is_last(n):
                    g.vector_index(dve, n.step(1))
                wait(dve, stored[n.par], n.half * 32)
                g.vector_sum(dve, n, x4[n.par][:].rearrange("p u d -> p (u d)"))

            nc.vector.memset(g.both[:], 0.0).then_inc(s.const_ready, 1)
            dve.wait_ge(s.const_ready, 1)
            g.vector_index(dve, FIRST)
            over_pairs(dve, body)

        @block.gpsimd
        def _(pool):
            def body(n):
                if not is_last(n):
                    g.gpsimd(pool, n.step(1))

            pool.wait_ge(s.const_ready, 1)
            g.gpsimd(pool, FIRST)
            over_pairs(pool, body)
            pool.wait_ge(g.s.carried, NPAIR)

        @block.sync
        def _(sp):
            def body(n):
                wait(sp, g.s.sum, n.n + 1)
                for b in range(B):
                    sp.dma_start(out[b, bass.ds(n.n * 2 * C, 2 * C), :].rearrange("(u t) d -> t u d", u=2),
                                 x4[n.par][C * b:C * b + C]).then_inc(stored[n.par], 16)

            over_pairs(sp, body)
            for par in range(2):
                sp.wait_ge(stored[par], 32 * (NPAIR // 2))


def program(nc, a, out):
    with ExitStack() as ctx:
        m = memory(ctx, nc)

        def rows(name, count):
            return [nc.dram_tensor(f"{name}{i}", (count, D), F32, kind="Internal").ap() for i in range(2)]

        dram = Names()
        loads = Names()
        loads.const, loads.attn, loads.x, loads.rates, loads.late = semaphores(ctx, nc, "in_", "const attn x rates late")
        dram.inputs, dram.results = rows("expert_inputs", ROWS), rows("expert_results", NTILE * P)
        with ExitStack() as attention:
            z = zero_padded_operands(attention, nc)
            setup(nc, m, a, dram, z, loads)
            nc.all_engine_barrier()
            attention_and_route(nc, m, a, dram, z, loads)
        nc.all_engine_barrier()
        late_setup(nc, m, loads)
        nc.all_engine_barrier()
        experts(nc, m, dram.inputs[0], dram.results[0], "ea_")
        nc.all_engine_barrier()
        space_and_route(nc, m, a, dram)
        nc.all_engine_barrier()
        experts(nc, m, dram.inputs[1], dram.results[1], "eb_")
        nc.all_engine_barrier()
        gather_and_store(nc, m, dram.results[1], out)


def kernel(**inputs):
    import concourse.bacc as bacc
    from concourse.bass_utils import run_bass_kernel_spmd

    nc = bacc.Bacc("TRN2", target_bir_lowering=False, num_devices=1)
    arrays, args = {}, {}
    for name in [*_INS, "constants"]:
        x = constants()[0] if name == "constants" else np.ascontiguousarray(inputs[name])
        arrays[f"in_{name}_dram"] = x
        args[name] = nc.dram_tensor(f"in_{name}_dram", x.shape, mybir.dt.from_np(x.dtype), kind="ExternalInput").ap()
    out = nc.dram_tensor("out_dram", (B, T, D), F32, kind="ExternalOutput").ap()
    program(nc, args, out)
    r = run_bass_kernel_spmd(nc, [arrays], core_ids=[0])
    return r.results[0]["out_dram"]
```

```python
from contextlib import ExitStack

import numpy as np

import concourse.bass as bass
from concourse import mybir

F32 = mybir.dt.float32
U32 = mybir.dt.uint32
I32 = mybir.dt.int32
ALU = mybir.AluOpType
ACT = mybir.ActivationFunctionType
AX_X = mybir.AxisListType.X

P = 128
B = 2
T = 1024
D = 128
H = 4
K = D // H
M = 64
C = 64
NCHUNK = T // C
NPAIR = NCHUNK // 2
GATE_NORM = 8.0
EPS = 1e-5
E = 8
FF = 512
FB = FF // P
N = 64
NTILE = B * T * 2 // P + E - 1
GROUP = 4
NGROUP = -(-NTILE // GROUP)
REGION = B * T + P
SPARE = E * REGION - (NTILE - E) * P
ROWS = E * REGION + E * P
ROW = D + 2
LN_MAX = float(2 ** 60)
TWO_PI_1 = 6.28125
TWO_PI_2 = round((2 * np.pi - TWO_PI_1) * 2 ** 20) / 2 ** 20
TWO_PI_3 = 2 * np.pi - TWO_PI_1 - TWO_PI_2
ROUND = 12582912.0
LEVELS = 10
ANGLES_AT = 19
LATE = 4 + 3 + 1 + E + 2 + 2


class Names:
    pass


def constants():
    p = np.arange(P)
    b, t = p // C, p % C
    same = b[:, None] == b[None, :]
    mid = t <= C // 2 - 1
    cols = {
        "ident": np.eye(P),
        "cum": -1 / GATE_NORM * same * ((t[:, None] <= t[None, :]) * 1.0 - mid[:, None] * 1.0),
        "causal": (t[:, None] <= np.arange(C)[None, :]) * 1.0,
        "spans": -1 / GATE_NORM * np.stack([(b == 0) & ~mid, (b == 0) & mid, (b == 1) & ~mid, (b == 1) & mid], 1),
        "earlier": (p[:, None] < p[None, :]) * 1.0,
        "ones": np.ones((P, P)),
        "experts": np.tile(np.arange(E), (P, 1)),
        "base": np.tile(np.arange(E) * REGION, (P, 1)),
        "ids": (np.arange(2)[None, None, None, :] * B * T + np.arange(NCHUNK).reshape(1, NPAIR, 2, 1) * P
                + p[:, None, None, None]).reshape(P, NPAIR * 4),
        "unread": 2 * B * T + np.arange(2 * E) * P + p[:, None],
        "tiles": np.tile(np.arange(NTILE), (P, 1)),
        "tile_rows": np.tile(np.arange(NTILE) * P, (P, 1)),
        "digits": np.tile(float(E) ** (np.arange(NTILE) % GROUP), (P, 1)),
        "powers": np.tile(2.0 ** np.arange(LEVELS), (P, 1)),
        "sign": np.where(p < N, 1.0, -1.0)[:, None],
    }
    at, where = 0, {}
    for name, a in cols.items():
        where[name] = (at, at + a.shape[1])
        at += a.shape[1]
    return np.concatenate(list(cols.values()), 1).astype(np.float32), where


def wait(eng, sem, count):
    if isinstance(count, int) and count <= 0:
        return
    eng.wait_ge(sem, count)


def wait_apart(eng, sem, count, reached):
    if not isinstance(count, int):
        count = eng.to_reg(count)
    eng.wait_ge(reached, 1)
    wait(eng, sem, count)


class Pair:

    def __init__(self, n, half, par):
        self.n, self.half, self.par = n, half, par

    def step(self, k):
        return Pair(self.n + k, self.half + (self.par + k) // 2, (self.par + k) % 2)


def over_pairs(eng, body):
    for n in range(3):
        body(Pair(n, n // 2, n % 2))
    with eng.Fori(1, NPAIR // 2 - 1) as i:
        body(Pair(i * 2 + 1, i, 1))
        body(Pair(i * 2 + 2, i + 1, 0))
    body(Pair(NPAIR - 1, (NPAIR - 1) // 2, (NPAIR - 1) % 2))


FIRST, LAST = Pair(0, 0, 0), Pair(NPAIR - 1, (NPAIR - 1) // 2, (NPAIR - 1) % 2)


def is_first(pair):
    return isinstance(pair.n, int) and pair.n == 0


def is_last(pair):
    return isinstance(pair.n, int) and pair.n == NPAIR - 1


class Stage(ExitStack):

    def __init__(self, nc):
        super().__init__()
        self.sems = []
        self.callback(nc.clear_and_free_semaphores, self.sems)


def semaphores(stage, nc, prefix, names):
    sems = [nc.alloc_semaphore(name=prefix + n) for n in names.split()]
    stage.sems.extend(sems)
    return sems


def memory(ctx, nc):
    def sb(name, *free, dt=F32):
        return ctx.enter_context(nc.sbuf_tensor(name, [P, *free], dt))

    _, where = constants()
    width = max(b for _, b in where.values())
    m = Names()
    m.const = sb("const", width)
    m.c = {name: m.const[:, a:b] for name, (a, b) in where.items()}
    m.psum = ctx.enter_context(nc.psum_tensor("banks", [P, 8, 512], F32))
    m.bank = [m.psum[:, i, :] for i in range(8)]
    m.bank12 = m.psum[:, 1:3, :]

    m.x = sb("x_rows", NCHUNK * D)
    m.moments = sb("moments", NCHUNK, 2)
    m.rstd = sb("input_rstd", NCHUNK)

    m.w_zkv = sb("w_zkv", 512)
    m.w_q = sb("w_q", D)
    m.w_qk = sb("w_qk", 2, 2, 2 * K)
    m.w_o = sb("w_o", D)
    m.g_norm = sb("g_norm", 1)
    m.w_router = sb("w_router", E)
    m.b_router = sb("b_router", E)
    m.w1 = sb("w1", E * FF)
    m.b1_rows = sb("b1_rows", P)
    m.b1 = sb("b1", E * FB)
    m.b2 = sb("b2_all", E * D)
    m.w2 = sb("w2", E * FB * D)
    m.b_in = sb("b_in", D)
    m.b_in_t = sb("b_in_t", P)
    m.b_in_swap = sb("b_in_swap", P)
    m.c_mats = sb("c_mats", 2 * P)
    m.w_out = sb("w_out", D)
    m.w_out_t = sb("w_out_t", D)
    m.out_cos = sb("out_cos", D)
    m.out_sin = sb("out_sin", D)
    m.out_x = sb("out_x", D)
    m.d_col = sb("d_col", 1)
    m.b_out = sb("b_out_rows", D)
    m.lam = sb("lam", 4)
    m.mag = sb("mag", P)
    m.turn_cos = sb("turn_cos", LEVELS)
    m.turn_sin = sb("turn_sin", LEVELS)
    m.cos = sb("cos_table", T)
    m.sin = sb("sin_table", T)
    m.results = sb("results", 2, NCHUNK, D)
    m.next_slot = sb("next_slot", E)
    m.plan = sb("plan", NTILE + NGROUP + E, dt=I32)
    m.zero = sb("zero_rows", 2 * E, ROW)
    return m


def zero_padded_operands(ctx, nc):
    def sb2(name, *free):
        return [ctx.enter_context(nc.sbuf_tensor(f"{name}{i}", [P, *free], F32)) for i in range(2)]

    z = Names()
    z.kv = sb2("kv", 2, H, 2, B, K)
    z.q_t = sb2("q_t", 2, 2, 2, P)
    z.pt = ctx.enter_context(nc.sbuf_tensor("weights_t", [P, 2, 2, 2, P], F32))
    return z


def setup(nc, m, a, dram, z, loads):
    with Stage(nc) as ctx:
        s = Names()
        s.dve, s.act = semaphores(ctx, nc, "su_", "dve act")
        s.memory_zero, s.stats, s.moments, s.rstd, s.angles = \
            semaphores(ctx, nc, "su_", "memory_zero stats moments rstd angles")
        th = ctx.enter_context(nc.sbuf_tensor("su_theta", [P, 3], F32))
        ang = ctx.enter_context(nc.sbuf_tensor("su_angles", [P, LEVELS], F32))
        turns = ctx.enter_context(nc.sbuf_tensor("su_turns", [P, LEVELS], F32))
        half = ctx.enter_context(nc.sbuf_tensor("su_half_sine", [P, LEVELS], F32))
        eL = ctx.enter_context(nc.sbuf_tensor("su_decay_rate", [P, 2], F32))
        stats = ctx.enter_context(nc.sbuf_tensor("su_stats", [P, NCHUNK, 6], F32))

        block = ctx.enter_context(nc.Block())

        def load_x(eng, b):
            eng.dma_start(m.x[C * b:C * b + C, :].rearrange("p (c d) -> p c d", d=D),
                          a["L0_attn_a_x"][b].rearrange("(c t) d -> t c d", t=C)).then_inc(loads.x, 16)

        @block.sync
        def _(sp):
            load_x(sp, 0)
            sp.dma_start(m.const[:], a["constants"]).then_inc(loads.const, 16)
            for w, (lo, hi) in (("Wf", (0, 256)), ("Wk", (256, 384)), ("Wv", (384, 512))):
                sp.dma_start(m.w_zkv[:, lo:hi], a["L0_attn_a_" + w]).then_inc(loads.attn, 16)
            sp.dma_start(m.w_q[:], a["L0_attn_a_Wq"]).then_inc(loads.attn, 16)
            sp.dma_start(m.w_o[:], a["L0_attn_a_Wo"]).then_inc(loads.attn, 16)
            g = a["L0_attn_a_g_norm_w"].rearrange("(v o) -> v o", o=1)
            for h in range(H):
                sp.dma_start(m.g_norm[K * h:K * h + K, :], g).then_inc(loads.attn, 16)
            sp.dma_start(m.w_router[:], a["L0_ffn_router_w"]).then_inc(loads.attn, 16)
            sp.dma_start(m.b_router[:], a["L0_ffn_router_b"].partition_broadcast(P)).then_inc(loads.attn, 16)

        @block.vector
        def _(dve):
            count = [0]

            def own(ins):
                count[0] += 1
                ins.then_inc(s.dve, 1)
                dve.wait_ge(s.dve, count[0])

            nc.vector.memset(m.zero[:], 0.0)
            own(nc.vector.memset(m.mag[:], 1.0))
            dve.wait_ge(loads.x, 16 * B)
            for c in range(NCHUNK):
                ins = nc.vector.bn_stats(stats[:, c, :], m.x[:, c * D:(c + 1) * D])
            ins.then_inc(s.stats, 1)
            dve.wait_ge(s.stats, 1)
            for c in range(NCHUNK):
                ins = nc.vector.bn_aggr(m.moments[:, c, :], stats[:, c, :])
            ins.then_inc(s.moments, 1)
            dve.wait_ge(s.moments, 1)
            nc.vector.tensor_scalar(m.rstd[:], m.moments[:, :, 1], EPS, None, ALU.add).then_inc(s.moments, 1)
            dve.wait_ge(loads.attn, 16 * (7 + H))
            own(nc.vector.tensor_scalar(m.w_o[:], m.w_o[:], m.g_norm[:], None, ALU.mult))
            for kind, w in enumerate((m.w_q[:], m.w_zkv[:, 256:384])):
                for e in range(2):
                    nc.vector.tensor_copy(m.w_qk[:, kind, e, :].rearrange("d (p k) -> d p k", p=2),
                                          w.rearrange("d (p e k) -> d p e k", p=2, e=2)[:, :, e, :])
            dve.wait_ge(loads.const, 16)
            nc.vector.tensor_copy(m.zero[:, :, D], m.c["unread"])
            own(nc.vector.tensor_copy(m.next_slot[:], m.c["base"]))
            dve.wait_ge(s.act, 4)
            own(nc.vector.tensor_scalar(m.mag[:], m.mag[:], eL[:, 1:2], None, ALU.mult))

        @block.scalar
        def _(act):
            load_x(act, 1)
            for i in range(2):
                half_ = slice(N * i, N * i + N)
                for col, name in ((0, "log_Lam_real"), (1, "Lam_imag")):
                    act.dma_start(m.lam[half_, col:col + 1],
                                  a["L0_attn_b_" + name].rearrange("(n o) -> n o", o=1)).then_inc(loads.rates, 16)
            act.dma_start(m.lam[:, 2:3], a["L0_attn_b_log_dt"].partition_broadcast(P)).then_inc(loads.rates, 16)
            act.wait_ge(loads.rates, 16 * 5)
            nc.scalar.activation(m.lam[:, 3:4], m.lam[:, 2:3], ACT.Exp).then_inc(s.act, 1)
            nc.scalar.activation(eL[:, 0:1], m.lam[:, 0:1], ACT.Exp).then_inc(s.act, 1)
            act.wait_ge(s.act, 2)
            nc.scalar.mul(eL[:, 0:1], eL[:, 0:1], m.lam[:, 3:4]).then_inc(s.act, 1)
            act.wait_ge(s.act, 3)
            nc.scalar.activation(eL[:, 1:2], eL[:, 0:1], ACT.Exp, scale=-1.0).then_inc(s.act, 1)
            act.wait_ge(s.angles, ANGLES_AT)
            nc.scalar.activation(m.turn_sin[:], ang[:], ACT.Sin).then_inc(s.act, 1)
            nc.scalar.activation(half[:], ang[:], ACT.Sin, scale=0.5).then_inc(s.act, 1)
            nc.scalar.preload_act_table_set("natural_log_exp_and_others")
            act.wait_ge(s.moments, 2)
            nc.scalar.activation(m.rstd[:], m.rstd[:], ACT.Ln).then_inc(s.rstd, 1)
            act.wait_ge(s.rstd, 1)
            nc.scalar.activation(m.rstd[:], m.rstd[:], ACT.Exp, scale=-0.5).then_inc(s.rstd, 1)
            act.wait_ge(s.rstd, 2)

        @block.gpsimd
        def _(pool):
            for zeros in (*z.kv, *z.q_t, z.pt):
                ins = nc.gpsimd.memset(zeros[:], 0.0)
            ins.then_inc(s.memory_zero, 1)
            pool.wait_ge(s.memory_zero, 1)
            count = [0]

            def own(ins):
                count[0] += 1
                ins.then_inc(s.angles, 1)
                pool.wait_ge(s.angles, count[0])

            pool.wait_ge(loads.rates, 16 * 5)
            pool.wait_ge(s.act, 1)
            own(nc.gpsimd.tensor_tensor(th[:, 0:1], m.lam[:, 1:2], m.lam[:, 3:4], ALU.mult))

            def within_half_turn(x, k, product):
                own(nc.gpsimd.tensor_scalar(k, x, float(1 / (2 * np.pi)), ROUND, ALU.mult, ALU.add))
                own(nc.gpsimd.tensor_scalar(k, k, -ROUND, None, ALU.add))
                for part in (TWO_PI_1, TWO_PI_2, TWO_PI_3):
                    own(nc.gpsimd.tensor_scalar(product, k, -part, None, ALU.mult))
                    own(nc.gpsimd.tensor_tensor(x, x, product, ALU.add))

            within_half_turn(th[:, 0:1], th[:, 1:2], th[:, 2:3])
            pool.wait_ge(loads.const, 16)
            own(nc.gpsimd.tensor_scalar(ang[:], m.c["powers"], th[:, 0:1], None, ALU.mult))
            within_half_turn(ang[:], turns[:], half[:])
            own(nc.gpsimd.tensor_scalar(ang[:], ang[:], 3.1415925, -3.1415925, ALU.min, ALU.max))
            assert count[0] == ANGLES_AT
            pool.wait_ge(s.act, 6)
            own(nc.gpsimd.tensor_tensor(m.turn_cos[:], half[:], half[:], ALU.mult))
            own(nc.gpsimd.tensor_scalar(m.turn_cos[:], m.turn_cos[:], -2.0, 1.0, ALU.mult, ALU.add))


def rotation_tables(nc, pool, m, s, product, product2):
    count = [0]

    def own(ins):
        count[0] += 1
        ins.then_inc(s.table, 1)
        pool.wait_ge(s.table, count[0])

    v = nc.gpsimd
    v.memset(m.cos[:, 0:1], 1.0)
    own(v.memset(m.sin[:, 0:1], 0.0))
    for k in range(LEVELS):
        n = 2 ** k
        old, new = slice(0, n), slice(n, 2 * n)
        c, d = m.turn_cos[:, k:k + 1], m.turn_sin[:, k:k + 1]
        v.tensor_scalar(product[:, old], m.sin[:, old], d, None, ALU.mult)
        v.tensor_scalar(product2[:, old], m.cos[:, old], d, None, ALU.mult)
        v.tensor_scalar(m.cos[:, new], m.cos[:, old], c, None, ALU.mult)
        own(v.tensor_scalar(m.sin[:, new], m.sin[:, old], c, None, ALU.mult))
        v.tensor_tensor(m.cos[:, new], m.cos[:, new], product[:, old], ALU.subtract)
        own(v.tensor_tensor(m.sin[:, new], m.sin[:, new], product2[:, old], ALU.add))
    own(v.tensor_scalar(m.sin[:], m.sin[:], m.c["sign"], None, ALU.mult))


def tensor_late(pe, m, s, loads):
    pe.wait_ge(loads.late, 16 * LATE)
    pe.wait_ge(s.x1, NPAIR)
    pe.transpose(m.bank[2][:, 0:E * FB], m.b1_rows[0:E * FB, :], m.c["ident"][0:E * FB, 0:E * FB])
    pe.wait_ge(s.late_act, 1)
    pe.transpose(m.bank[0][:, 0:128], m.b_in[:], m.c["ident"])
    pe.transpose(m.bank[0][:, 128:256], m.w_out[:], m.c["ident"]).then_inc(s.late_pe, 1)


def tensor_late_products(pe, m, s):
    pe.wait_ge(s.late_act, 4)
    pe.matmul(m.bank[1][:, 0:128], m.c_mats[:, 0:128], m.w_out_t[:], start=True, stop=True)
    pe.matmul(m.bank[1][:, 128:256], m.c_mats[:, 128:256], m.w_out_t[:], start=True, stop=True).then_inc(s.late_pe, 1)


def scalar_late_maps(nc, act, m, s, loads):
    act.wait_ge(loads.late, 16 * LATE)
    nc.scalar.activation(m.b_in[:], m.b_in[:], ACT.Copy, scale=m.lam[:, 3:4]).then_inc(s.late_act, 1)
    nc.scalar.copy(m.c_mats[:, 192:256], m.c_mats[:, 0:64])
    nc.scalar.activation(m.c_mats[:, 128:192], m.c_mats[:, 64:128], ACT.Copy, scale=-1.0).then_inc(s.late_act, 1)
    act.wait_ge(s.late_act, 2)
    nc.scalar.activation(m.c_mats[:, 64:128], m.c_mats[:, 64:128], ACT.Copy, scale=-1.0).then_inc(s.late_act, 1)


def scalar_late_copies(nc, act, m, s):
    act.wait_ge(s.late_pe, 1)
    nc.scalar.copy(m.w_out_t[:], m.bank[0][:, 128:256]).then_inc(s.late_act, 1)
    nc.scalar.copy(m.b_in_t[:], m.bank[0][:, 0:128])
    nc.scalar.copy(m.b_in_swap[:, 0:64], m.bank[0][:, 64:128])
    nc.scalar.copy(m.b_in_swap[:, 64:128], m.bank[0][:, 0:64])
    act.wait_ge(s.late_act, 4)
    nc.scalar.activation(m.out_x[:], m.w_out_t[:], ACT.Copy, scale=m.d_col[:])
    nc.scalar.copy(m.b1[:], m.bank[2][:, 0:E * FB])
    act.wait_ge(s.late_pe, 2)
    nc.scalar.copy(m.out_cos[:], m.bank[1][:, 0:128])
    nc.scalar.copy(m.out_sin[:], m.bank[1][:, 128:256])


def chunk_rows(m, n, u):
    return m.x[:, bass.ds((n.n * 2 + u) * D, D)]


class Norm:

    def __init__(self, sb, name):
        self.stats = sb(name + "_stats", 2, 6)
        self.mv = sb(name + "_mv", 2, 2)
        self.ve = sb(name + "_var_eps", 2)
        self.rstd = sb(name + "_rstd", 2)
        self.carrier = sb(name + "_carrier", 1)


class Route:

    def __init__(self, ctx, nc, m, a, dram, prefix):
        def sb(name, *free, dt=F32):
            return ctx.enter_context(nc.sbuf_tensor(prefix + name, [P, *free], dt))

        self.nc, self.m = nc, m
        self.rows_out = dram.inputs[0] if prefix == "ra_" else dram.inputs[1]
        self.s = Names()
        self.s.stats, self.s.mv, self.s.var_eps, self.s.rstd, self.s.xn, self.s.x_t_ps, self.s.x_t = \
            semaphores(ctx, nc, prefix, "stats mv var_eps rstd xn x_t_ps x_t")
        self.s.logits_ps, self.s.logits, self.s.top, self.s.index, self.s.index_f, self.s.picks, self.s.marked = \
            semaphores(ctx, nc, prefix, "logits_ps logits top index index_f picks marked")
        self.s.margin, self.s.exp_margin, self.s.gate_sum, self.s.gate1, self.s.gates = \
            semaphores(ctx, nc, prefix, "margin exp_margin gate_sum gate1 gates")
        self.s.rank_ps, self.s.place, self.s.moved, self.s.picked, self.s.slot_f, self.s.slots = \
            semaphores(ctx, nc, prefix, "rank_ps place moved picked slot_f slots")
        self.s.scattered0, self.s.scattered1, self.s.plan = \
            semaphores(ctx, nc, prefix, "scattered0 scattered1 plan")
        self.s.marks, self.s.rstd_log = semaphores(ctx, nc, prefix, "marks rstd_log")
        self.s.tails_at, self.s.tails_out = \
            semaphores(ctx, nc, prefix, "tails_at tails_out")
        self.ln = Norm(sb, "ln")
        self.rows = [sb(f"rows{i}", 2, 2, ROW) for i in range(2)]
        self.x_t = sb("x_t", 2, P)
        self.logits = sb("logits", 2, E)
        self.top = sb("top", 2, 8)
        self.index = sb("index", 2, 8, dt=U32)
        self.index_f = sb("index_f", 2, 2)
        self.picks = sb("picks", 2, 2, E)
        self.marked = sb("marked", 2, E)
        self.before = sb("before", 3, E)
        self.margin = sb("margin", 2)
        self.e_margin = sb("exp_margin", 2)
        self.gate_sum = sb("gate_sum", 2)
        self.gates = sb("gates", 2, 2)
        self.place = sb("place", 2, E)
        self.picked = sb("picked", 2, 2, E)
        self.slot_f = sb("slot_f", 4)
        self.slots = [sb(f"slots{i}", 4, dt=U32) for i in range(2)]
        self.count = sb("count", E)
        self.tiles = sb("expert_tiles", E)
        self.tiles_to = sb("tiles_up_to", E)
        self.cmp = sb("compare", NTILE, E)
        self.owner = sb("owner", NTILE)
        self.digits = sb("digits", (NGROUP + 1) * GROUP)
        self.four = sb("four_digits", NGROUP + 1)
        self.three = sb("three_digits", NGROUP + 1)
        self.row = sb("row", NTILE)
        self.spare = sb("spare", NTILE)

    def scattered(self, par):
        return (self.s.scattered0, self.s.scattered1)[par]

    def vector_norm(self, dve, n):
        nc, s, ln = self.nc, self.s, self.ln
        wait(dve, self.x_written, n.n + 1)
        nc.vector.memset(ln.carrier[:], 0.0)
        for u in range(2):
            ins = nc.vector.bn_stats(ln.stats[:, u, :], chunk_rows(self.m, n, u))
        ins.then_inc(s.stats, 1)
        wait(dve, s.stats, n.n + 1)
        nc.vector.memset(ln.carrier[:], 0.0)
        for u in range(2):
            nc.vector.bn_aggr(ln.mv[:, u, :], ln.stats[:, u, :]).then_inc(s.mv, 1)
        wait(dve, s.mv, (n.n + 1) * 2)
        nc.vector.tensor_scalar(ln.ve[:], ln.mv[:, :, 1], EPS, None, ALU.add).then_inc(s.var_eps, 1)

    def scalar_norm(self, act, n):
        nc, s, ln = self.nc, self.s, self.ln
        wait(act, s.var_eps, n.n + 1)
        wait(act, s.xn, n.n)
        nc.scalar.activation(ln.rstd[:], ln.ve[:], ACT.Ln).then_inc(s.rstd_log, 1)
        wait(act, s.rstd_log, n.n + 1)
        nc.scalar.activation(ln.rstd[:], ln.rstd[:], ACT.Exp, scale=-0.5).then_inc(s.rstd, 1)

    def vector_normed(self, dve, n):
        wait(dve, self.s.rstd, n.n + 1)
        wait(dve, self.scattered(n.par), n.half * 64)
        for u in range(2):
            self.nc.vector.tensor_scalar(self.rows[n.par][:, u, :, 0:D],
                                         chunk_rows(self.m, n, u).unsqueeze(1).to_broadcast([P, 2, D]),
                                         self.ln.mv[:, u, 0:1], self.ln.rstd[:, u:u + 1], ALU.subtract, ALU.mult)
        ids = self.m.c["ids"][:, bass.ds(n.n * 4, 4)].rearrange("p (u k) -> p u k", u=2)
        self.nc.vector.tensor_copy(self.rows[n.par][:, :, :, D], ids).then_inc(self.s.xn, 1)

    def tensor_transposed(self, pe, n):
        m, s = self.m, self.s
        wait(pe, s.xn, n.n + 1)
        wait(pe, s.moved, n.n)
        for u in range(2):
            mm = pe.transpose(self.bank[:, P * u:P * u + P], self.rows[n.par][:, u, 0, 0:D], m.c["ident"])
        mm.then_inc(s.x_t_ps, 1)

    def tensor_logits(self, pe, n):
        m, s, bank = self.m, self.s, self.bank
        wait(pe, s.x_t, n.n + 1)
        for u in range(2):
            mm = pe.matmul(bank[:, E * u:E * u + E], self.x_t[:, u, :], m.w_router[:], start=True, stop=True)
        mm.then_inc(s.logits_ps, 1)

    def tensor_ranks(self, pe, n):
        m, s, bank = self.m, self.s, self.bank
        wait(pe, s.marked, n.n + 1)
        pe.matmul(bank[:, 0:3 * E], m.c["ones"], self.before[:].rearrange("p k e -> p (k e)"), start=True, stop=False,
                  skip_group_check=True)
        pe.matmul(bank[:, 0:2 * E], m.c["earlier"], self.marked[:].rearrange("p u e -> p (u e)"), start=False, stop=True,
                  skip_group_check=True).then_inc(s.rank_ps, 1)

    def tensor(self, pe, n):
        self.tensor_transposed(pe, n)
        self.tensor_logits(pe, n)
        self.tensor_ranks(pe, n)

    def scalar_transposed(self, act, n):
        wait(act, self.s.x_t_ps, n.n + 1)
        wait(act, self.s.logits_ps, n.n)
        self.nc.scalar.copy(self.x_t[:].rearrange("p u t -> p (u t)"), self.bank[:, 0:256]).then_inc(self.s.x_t, 1)

    def scalar_margin(self, act, n):
        wait(act, self.s.margin, n.n + 1)
        wait(act, self.s.gates, n.n)
        self.nc.scalar.activation(self.e_margin[:], self.margin[:], ACT.Exp).then_inc(self.s.exp_margin, 1)

    def scalar(self, act, n):
        self.scalar_transposed(act, n)
        self.scalar_margin(act, n)

    def vector_choose(self, dve, n):
        nc, m, s = self.nc, self.m, self.s
        wait(dve, s.logits_ps, n.n + 1)
        nc.vector.tensor_tensor(self.logits[:], self.bank[:, 0:2 * E].rearrange("p (u e) -> p u e", u=2),
                                m.b_router[:].unsqueeze(1).to_broadcast([P, 2, E]), ALU.add).then_inc(s.logits, 1)
        wait_apart(dve, s.logits, n.n + 1, self.ready)
        for u in range(2):
            nc.vector.max(self.top[:, u, :], self.logits[:, u, :]).then_inc(s.top, 1)
        wait(dve, s.top, (n.n + 1) * 2)
        nc.vector.tensor_tensor(self.margin[:], self.top[:, :, 1], self.top[:, :, 0], ALU.subtract).then_inc(s.margin, 1)
        for u in range(2):
            nc.vector.max_index(self.index[:, u, :], self.top[:, u, :], self.logits[:, u, :]).then_inc(s.index, 1)
        wait(dve, s.index, (n.n + 1) * 2)
        nc.vector.tensor_copy(self.index_f[:], self.index[:, :, 0:2]).then_inc(s.index_f, 1)
        wait(dve, s.index_f, n.n + 1)
        nc.vector.tensor_tensor(self.picks[:].rearrange("p u k e -> p (u k) e"),
                                m.c["experts"].unsqueeze(1).to_broadcast([P, 4, E]),
                                self.index_f[:].rearrange("p u k -> p (u k)").unsqueeze(2).to_broadcast([P, 4, E]),
                                ALU.is_equal).then_inc(s.picks, 1)
        wait(dve, s.picks, n.n + 1)
        nc.vector.tensor_tensor(self.marked[:], self.picks[:, :, 0, :], self.picks[:, :, 1, :], ALU.add).then_inc(s.marks, 1)
        nc.vector.tensor_tensor(self.before[:, 1, :], self.picks[:, 0, 0, :], self.picks[:, 0, 1, :], ALU.add)
        wait(dve, s.marks, n.n + 1)
        nc.vector.tensor_tensor(self.before[:, 2, :], self.marked[:, 0, :], self.marked[:, 1, :], ALU.add).then_inc(s.marked, 1)
        wait(dve, s.exp_margin, n.n + 1)
        nc.vector.tensor_scalar(self.gate_sum[:], self.e_margin[:], 1.0, None, ALU.add).then_inc(s.gate_sum, 1)
        wait(dve, s.gate_sum, n.n + 1)
        nc.vector.reciprocal(self.gates[:, :, 0], self.gate_sum[:]).then_inc(s.gate1, 1)
        wait(dve, s.gate1, n.n + 1)
        nc.vector.tensor_tensor(self.gates[:, :, 1], self.gates[:, :, 0], self.e_margin[:], ALU.mult).then_inc(s.gates, 1)
        wait(dve, s.gates, n.n + 1)
        nc.vector.tensor_copy(self.rows[n.par][:, :, :, D + 1], self.gates[:])

    def vector_place(self, dve, n):
        nc, m, s = self.nc, self.m, self.s
        wait(dve, s.rank_ps, n.n + 1)
        nc.vector.tensor_tensor(self.place[:], self.bank[:, 0:2 * E].rearrange("p (u e) -> p u e", u=2),
                                m.next_slot[:].unsqueeze(1).to_broadcast([P, 2, E]), ALU.add).then_inc(s.place, 1)
        wait(dve, s.place, n.n + 1)
        nc.vector.tensor_tensor(m.next_slot[:], m.next_slot[:], self.bank[:, 2 * E:3 * E], ALU.add).then_inc(s.moved, 1)
        wait(dve, s.place, n.n + 1)
        for u in range(2):
            ins = nc.vector.tensor_tensor(self.picked[:, u], self.picks[:, u],
                                          self.place[:, u, :].unsqueeze(1).to_broadcast([P, 2, E]), ALU.mult)
        ins.then_inc(s.picked, 1)
        wait(dve, s.picked, n.n + 1)
        nc.vector.tensor_reduce(self.slot_f[:], self.picked[:].rearrange("p u k e -> p (u k) e"), AX_X,
                                ALU.add).then_inc(s.slot_f, 1)
        wait(dve, s.slot_f, n.n + 1)
        nc.vector.tensor_copy(self.slots[n.par][:], self.slot_f[:]).then_inc(s.slots, 1)

    def gpsimd_scatter(self, pool, n):
        wait_apart(pool, self.s.slots, n.n + 1, self.ready)
        for u in range(2):
            for k in range(2):
                self.nc.gpsimd.indirect_dma_start(
                    self.rows_out[:, :], bass.IndirectOffsetOnAxis(ap=self.slots[n.par][:, 2 * u + k:2 * u + k + 1], axis=0),
                    self.rows[n.par][:, u, k, :], None).then_inc(self.scattered(n.par), 16)

    def gpsimd_wait(self, pool):
        for par in range(2):
            pool.wait_ge(self.scattered(par), 64 * (NPAIR // 2))

    def vector_plan(self, dve):
        nc, m, s = self.nc, self.m, self.s
        steps = [0]

        def own(ins):
            steps[0] += 1
            ins.then_inc(s.plan, 1)
            dve.wait_ge(s.plan, steps[0])

        dve.wait_ge(s.moved, NPAIR)
        nc.vector.tensor_copy(m.plan[:, NTILE + NGROUP:], m.next_slot[:]).then_inc(s.tails_at, 1)
        own(nc.vector.tensor_tensor(self.count[:], m.next_slot[:], m.c["base"], ALU.subtract))
        own(nc.vector.tensor_scalar(self.tiles[:], self.count[:], 1.0 / P, 0.5 - 0.5 / P, ALU.mult, ALU.add))
        own(nc.vector.tensor_scalar(self.tiles[:], self.tiles[:], ROUND, None, ALU.add))
        own(nc.vector.tensor_scalar(self.tiles[:], self.tiles[:], -ROUND, None, ALU.add))
        own(nc.vector.tensor_tensor_scan(self.tiles_to[:], m.c["ones"][:, 0:E], self.tiles[:], 0.0, ALU.mult, ALU.add))
        by_tile = [P, NTILE, E]
        own(nc.vector.tensor_tensor(self.cmp[:], self.tiles_to[:].unsqueeze(1).to_broadcast(by_tile),
                                    m.c["tiles"].unsqueeze(2).to_broadcast(by_tile), ALU.is_le))
        own(nc.vector.tensor_reduce(self.owner[:], self.cmp[:], AX_X, ALU.add))
        own(nc.vector.tensor_tensor(self.tiles[:], self.tiles[:], self.tiles_to[:], ALU.subtract))
        own(nc.vector.scalar_tensor_tensor(self.tiles[:], self.tiles[:], float(P), m.c["base"], ALU.mult, ALU.add))
        own(nc.vector.tensor_tensor(self.cmp[:], self.owner[:].unsqueeze(2).to_broadcast(by_tile),
                                    m.c["experts"].unsqueeze(1).to_broadcast(by_tile), ALU.is_equal))
        own(nc.vector.tensor_tensor(self.cmp[:], self.cmp[:], self.tiles[:].unsqueeze(1).to_broadcast(by_tile), ALU.mult))
        own(nc.vector.tensor_reduce(self.row[:], self.cmp[:], AX_X, ALU.add))
        own(nc.vector.tensor_tensor(self.row[:], self.row[:], m.c["tile_rows"], ALU.add))
        own(nc.vector.tensor_scalar(self.spare[:], self.owner[:], float(E), float(SPARE), ALU.is_equal, ALU.mult))
        own(nc.vector.tensor_tensor(self.row[:], self.row[:], self.spare[:], ALU.add))
        nc.vector.tensor_copy(m.plan[:, 0:NTILE], self.row[:])
        own(nc.vector.memset(self.digits[:], 0.0))
        own(nc.vector.scalar_tensor_tensor(self.digits[:, 0:NTILE], self.owner[:], float(E - 1), m.c["digits"],
                                           ALU.min, ALU.mult))
        by_group = self.digits[:].rearrange("p (q k) -> p q k", k=GROUP)
        own(nc.vector.tensor_reduce(self.four[:], by_group, AX_X, ALU.add))
        own(nc.vector.tensor_reduce(self.three[:], by_group[:, :, 0:3], AX_X, ALU.add))
        nc.vector.scalar_tensor_tensor(m.plan[:, NTILE:NTILE + NGROUP], self.three[:, 1:], float(E ** GROUP),
                                       self.four[:, 0:NGROUP], ALU.mult, ALU.add)

    def tails(self, eng, half):
        eng.wait_ge(self.s.tails_at, 1)
        for e in range(half, E, 2):
            row = eng.value_load(self.m.plan[0:1, NTILE + NGROUP + e:NTILE + NGROUP + e + 1], min_val=e * REGION,
                                 max_val=e * REGION + B * T)
            eng.dma_start(self.rows_out[bass.ds(row, P), :], self.m.zero[:, e, :]).then_inc(self.s.tails_out, 16)


def attention_and_route(nc, m, a, dram, z, loads):
    with Stage(nc) as ctx:
        def sb(name, *free, dt=F32):
            return ctx.enter_context(nc.sbuf_tensor("at_" + name, [P, *free], dt))

        def sb2(name, *free, dt=F32):
            return [sb(f"{name}{i}", *free, dt=dt) for i in range(2)]

        s = Names()
        s.xn, s.x_t_ps, s.x_t = semaphores(ctx, nc, "at_", "xn x_t_ps x_t")
        s.z_ps, s.qk_ps, s.exp_z, s.exp_kqk, s.capped, s.log1, s.soft = \
            semaphores(ctx, nc, "at_", "z_ps qk_ps exp_z exp_kqk capped log1 soft")
        s.ge_ready, s.v_ready, s.sig_sum, s.sig, s.k_ready, s.q_ready, s.kt_ready = \
            semaphores(ctx, nc, "at_", "ge_ready v_ready sig_sum sig k_ready q_ready kt_ready")
        s.g_ps, s.d_ps, s.d_sb, s.decays, s.s_ready, s.a_ps, s.a_sb = \
            semaphores(ctx, nc, "at_", "g_ps d_ps d_sb decays s_ready a_ps a_sb")
        s.st_ps, s.st_sb, s.u_ps, s.t0, s.st1, s.t1, s.d01 = \
            semaphores(ctx, nc, "at_", "st_ps st_sb u_ps t0 st1 t1 d01")
        s.st0, s.sk_ps, s.sk_sb, s.r_ps, s.logits, s.maxes, s.shifted = \
            semaphores(ctx, nc, "at_", "st0 sk_ps sk_sb r_ps logits maxes shifted")
        s.probs, s.sums, s.pw, s.pt_ps, s.pt_sb, s.b_ps, s.b_sb = \
            semaphores(ctx, nc, "at_", "probs sums pw pt_ps pt_sb b_ps b_sb")
        s.o_ps, s.sq, s.ms, s.s2, s.oe, s.o_rstd, s.on = \
            semaphores(ctx, nc, "at_", "o_ps sq ms s2 oe o_rstd on")
        s.ot_ps, s.ot_sb, s.y_ps, s.x1, s.d10, s.const_ready, s.q_spread = \
            semaphores(ctx, nc, "at_", "ot_ps ot_sb y_ps x1 d10 const_ready q_spread")
        s.sig_log, s.o_log, s.table, s.late_act, s.late_pe = \
            semaphores(ctx, nc, "at_", "sig_log o_log table late_act late_pe")
        table_product, table_product2 = sb("table_product", T), sb("table_product2", T)
        r = Route(ctx, nc, m, a, dram, "ra_")
        ln = Norm(sb, "ln")
        xn = sb("xn", 2, D)
        x_t = sb("x_t", 2, P)
        exp_z = sb("exp_z", 2, 256)
        exp_kqk = sb("exp_kqk", 768)
        sig = sb("sigmoid", 768)
        soft = sb("softplus", 2, 256)
        ge = sb("ge", 2, 256)
        e_minus = sb("e_minus", 2, 256)
        e_plus = sb2("e_plus", 2, 256)
        slot = sb2("slot", 2, 256)
        kv, q_t, pt_sb = z.kv, z.q_t, z.pt
        q_raw = sb("q_raw", 2, 2, C)
        k_t = sb2("k_t", 2, 2, C)
        d_sb = sb2("span_decays", 2, 2, 2, 2)
        a_sb = sb("a_masked", 2, 2, 2, C)
        st_sb = sb("slot_t", 2, 2, P)
        st0, st1 = sb("state_even", 2, 2, 2, K), sb("state_odd", 2, 2, 2, K)
        t0, t1 = sb("sum_even", 2, 2, 2, K), sb("sum_odd", 2, 2, 2, K)
        d01 = sb("decay_even", 2, 2)
        d10 = sb("decay_odd", 2, 2)
        sk_sb = sb2("state_k_t", P)
        logits = sb("logits", 2, H, M)
        maxes = sb("maxes", 2, H)
        probs = sb("probs", 2, H, M)
        sums = sb("sums", 2, H)
        pw = sb("weights", 2, H * M)
        b_sb = sb("b_masked", 2, H, C)
        sq = sb("squares", 2, H, K)
        ms = sb("mean_squares", 2, H)
        s2 = sb("sums_squared", 2, H)
        o_rstd = sb("o_rstd", 2, H)
        ready = sb("ready", 1)
        on = sb("o_normed", 2, D)
        ot_sb = sb("o_t", 2, P)

        r.bank, r.ready, r.x_written = m.bank[7], s.const_ready, s.x1
        xt_ps = m.bank[0]
        z_ps = m.bank12
        y_ps, ot_ps = m.bank[1], m.bank[2]
        qk_ps = m.bank[3]
        e_ps = m.bank[4]
        f_ps = m.bank[5]
        g_ps = m.bank[6]
        h_ps = m.bank[7]

        block = ctx.enter_context(nc.Block())

        @block.tensor
        def _(pe):
            def x_transposed(n):
                wait(pe, s.xn, n.n + 1)
                wait(pe, s.decays, n.n)
                for u in range(2):
                    mm = pe.transpose(xt_ps[:, P * u:P * u + P], xn[:, u, :], m.c["ident"])
                mm.then_inc(s.x_t_ps, 1)

            def project(n):
                wait(pe, s.x_t, n.n + 1)
                wait(pe, s.soft, n.n)
                wait(pe, s.k_ready, n.n)
                wait(pe, s.x1, n.n - 1)
                for u in range(2):
                    mm = pe.matmul(z_ps[:, u, :], x_t[:, u, :], m.w_zkv[:], start=True, stop=True)
                mm.then_inc(s.z_ps, 1)

            def project_transposed(n):
                wait(pe, s.a_sb, n.n)
                for kind in range(2):
                    for e in range(2):
                        for b in range(B):
                            mm = pe.matmul(qk_ps[64 * b:64 * b + 64, 256 * kind + 128 * e:256 * kind + 128 * e + 128]
                                           .rearrange("p (u t) -> p u t", u=2),
                                           m.w_qk[:, kind, e, :],
                                           x_t[:, :, C * b:C * b + C], start=True, stop=True)
                mm.then_inc(s.qk_ps, 1)

            def gate_sums(n):
                wait(pe, s.soft, n.n + 1)
                wait(pe, s.x_t, n.n + 1)
                for u in range(2):
                    mm = pe.matmul(xt_ps[:, 256 * u:256 * u + 256], m.c["cum"], soft[:, u, :], start=True, stop=True)
                mm.then_inc(s.g_ps, 1)

            def span_sums(n):
                wait(pe, s.soft, n.n + 1)
                for u in range(2):
                    for p in range(2):
                        mm = pe.matmul(h_ps[:, 8 * u:8 * u + 8].rearrange("s (b k p) -> s b k p", b=2, k=2)[:, :, :, p],
                                       soft[:, u, P * p:P * p + P], m.c["spans"], start=True, stop=True)
                mm.then_inc(s.d_ps, 1)

            def attend(n):
                wait(pe, s.kt_ready, n.n + 1)
                wait(pe, s.q_spread, n.n + 1)
                for u in range(2):
                    for e in range(2):
                        for b in range(B):
                            at = 256 * u + 128 * e
                            mm = pe.matmul(qk_ps[64 * b:64 * b + 64, at:at + 128].rearrange("j (p t) -> j p t", p=2),
                                           k_t[n.par][:, e, u, :], q_t[n.par][:, u, e, :, C * b:C * b + C],
                                           start=True, stop=True)
                mm.then_inc(s.a_ps, 1)

            def state_transposed(n, u):
                state = (st0, st1)[u]
                if u == 0:
                    wait(pe, s.st0, n.n + 1)
                    wait(pe, s.d_sb, n.n + 1)
                else:
                    wait(pe, s.st1, n.n + 1)
                    wait(pe, s.sk_sb, n.n * 2 + 1)
                pe.transpose(h_ps[:, 0:P], state[:, 0].rearrange("p b h k -> p (b h k)"), m.c["ident"]).then_inc(s.sk_ps, 1)

            def slots_transposed(n):
                wait(pe, s.s_ready, n.n + 1)
                wait(pe, s.pt_sb, n.n)
                for u in range(2):
                    for p in range(2):
                        at = 256 * u + P * p
                        mm = pe.transpose(f_ps[:, at:at + P], slot[n.par][:, u, P * p:P * p + P], m.c["ident"])
                mm.then_inc(s.st_ps, 1)

            def updates(n):
                wait(pe, s.k_ready, n.n + 1)
                wait(pe, s.v_ready, n.n + 1)
                wait(pe, s.b_sb, n.n)
                for u in range(2):
                    for h in range(H):
                        out = (g_ps[64 * (h % 2):64 * (h % 2) + 64, 256 * u:256 * u + 256]
                               .rearrange("s (c b p k) -> s c b p k", c=2, b=2, p=2)[:, :, :, h // 2, :])
                        mm = pe.matmul(out, slot[n.par][:, u, M * h:M * h + M], kv[n.par][:, u, h], start=True, stop=True)
                mm.then_inc(s.u_ps, 1)

            def raw_logits(n, u):
                if u == 0:
                    wait(pe, s.sq, n.n)
                    wait(pe, s.on, n.n)
                    wait(pe, s.a_sb, n.n + 1)
                wait(pe, s.sk_sb, n.n * 2 + u + 1)
                for h in range(H):
                    at, e = 256 * u + M * h, h % 2
                    pe.matmul(e_ps[:, at:at + M], q_t[n.par][:, u, e, h // 2, :], sk_sb[u][:, M * e:M * e + M],
                              start=(u == 0 and h == 0), stop=False, skip_group_check=True)
                for b in range(B):
                    for h in range(H):
                        rows, at = slice(64 * b, 64 * b + 64), 256 * u + M * h
                        mm = pe.matmul(e_ps[rows, at:at + M], a_sb[rows, u, h % 2, h // 2, :],
                                       slot[n.par][rows, u, M * h:M * h + M], start=False, stop=True,
                                       skip_group_check=True)
                if u == 1:
                    mm.then_inc(s.r_ps, 1)

            def weights_transposed(n):
                wait(pe, s.pw, n.n + 1)
                wait(pe, s.st_sb, n.n + 1)
                for u in range(2):
                    for p in range(2):
                        at = 256 * u + P * p
                        mm = pe.transpose(f_ps[:, at:at + P], pw[:, u, P * p:P * p + P], m.c["ident"])
                mm.then_inc(s.pt_ps, 1)

            def weights_by_slots(n):
                wait(pe, s.pt_sb, n.n + 1)
                wait(pe, s.t1, n.n + 1)
                for u in range(2):
                    for p in range(2):
                        for b in range(B):
                            at = 256 * u + 128 * p
                            mm = pe.matmul(g_ps[64 * b:64 * b + 64, at:at + 128].rearrange("j (e t) -> j e t", e=2),
                                           st_sb[:, u, p, C * b:C * b + C], pt_sb[:, u, p, :, C * b:C * b + C],
                                           start=True, stop=True)
                mm.then_inc(s.b_ps, 1)

            parts = [(u, b, h) for u in range(2) for b in range(B) for h in range(H)]

            def outputs_of_states(n, some):
                for u, b, h in some:
                    pe.matmul(e_ps[64 * b:64 * b + 64, D * u + K * h:D * u + K * h + K],
                              pt_sb[:, u, h // 2, h % 2, C * b:C * b + C], (st0, st1)[u][:, 1, b, h // 2, :],
                              start=(u == 0 and h == 0), stop=False, skip_group_check=True)

            def outputs_of_pair(n):
                wait(pe, s.b_sb, n.n + 1)
                outputs_of_states(n, parts[-1:])
                for u, b, h in parts:
                    rows = slice(64 * b, 64 * b + 64)
                    mm = pe.matmul(e_ps[rows, D * u + K * h:D * u + K * h + K], b_sb[rows, u, h, :],
                                   kv[n.par][rows, u, h, 1, b, :], start=False, stop=True, skip_group_check=True)
                mm.then_inc(s.o_ps, 1)

            def o_transposed(n):
                if not is_last(n):
                    wait(pe, s.soft, n.n + 2)
                    wait(pe, s.k_ready, n.n + 2)
                wait(pe, s.on, n.n + 1)
                for u in range(2):
                    mm = pe.transpose(ot_ps[:, P * u:P * u + P], on[:, u, :], m.c["ident"])
                mm.then_inc(s.ot_ps, 1)

            def project_out(n):
                wait(pe, s.ot_sb, n.n + 1)
                for u in range(2):
                    mm = pe.matmul(y_ps[:, D * u:D * u + D], ot_sb[:, u, :], m.w_o[:], start=True, stop=True)
                mm.then_inc(s.y_ps, 1)

            def body(n):
                state_transposed(n, 0)
                if not is_last(n):
                    x_transposed(n.step(1))
                raw_logits(n, 0)
                state_transposed(n, 1)
                if not is_last(n):
                    project(n.step(1))
                raw_logits(n, 1)
                wait(pe, s.sk_sb, n.n * 2 + 2)
                if not is_first(n):
                    r.tensor_transposed(pe, n.step(-1))
                if not is_last(n):
                    project_transposed(n.step(1))
                if not is_first(n):
                    r.tensor_logits(pe, n.step(-1))
                weights_transposed(n)
                if not is_last(n):
                    gate_sums(n.step(1))
                weights_by_slots(n)
                if not is_first(n):
                    r.tensor_ranks(pe, n.step(-1))
                outputs_of_states(n, parts[:-1])
                if not is_last(n):
                    wait(pe, r.s.moved, n.n)
                    span_sums(n.step(1))
                outputs_of_pair(n)
                if not is_last(n):
                    slots_transposed(n.step(1))
                    attend(n.step(1))
                o_transposed(n)
                if not is_last(n):
                    updates(n.step(1))
                project_out(n)

            x_transposed(FIRST)
            project(FIRST)
            project_transposed(FIRST)
            gate_sums(FIRST)
            span_sums(FIRST)
            attend(FIRST)
            slots_transposed(FIRST)
            updates(FIRST)
            over_pairs(pe, body)
            tensor_late(pe, m, s, loads)
            r.tensor(pe, LAST)
            tensor_late_products(pe, m, s)

        @block.vector
        def _(dve):
            def normed(n):
                wait(dve, s.x_t_ps, n.n)
                for u in range(2):
                    c = n.n * 2 + u
                    at = slice(c, c + 1) if isinstance(c, int) else bass.ds(c, 1)
                    ins = nc.vector.tensor_scalar(xn[:, u, :], chunk_rows(m, n, u), m.moments[:, at, 0], m.rstd[:, at],
                                                  ALU.subtract, ALU.mult)
                ins.then_inc(s.xn, 1)

            def gates_and_values(n):
                wait(dve, s.exp_z, n.n + 1)
                nc.vector.tensor_scalar(exp_z[:], exp_z[:], LN_MAX, None, ALU.min).then_inc(s.capped, 1)
                wait(dve, s.o_ps, n.n - 1)
                for b in range(B):
                    rows = slice(64 * b, 64 * b + 64)
                    ins = nc.vector.tensor_copy(kv[n.par][rows, :, :, 1, b, :],
                                                z_ps[rows, :, 384:512].rearrange("p u (h k) -> p u h k", h=H))
                ins.then_inc(s.v_ready, 1)

            def cap_sigmoids(n):
                wait(dve, s.exp_kqk, n.n + 1)
                nc.vector.tensor_scalar(exp_kqk[:], exp_kqk[:], LN_MAX, None, ALU.min).then_inc(s.sig_sum, 1)

            def gated(n):
                wait(dve, s.sig, n.n + 1)
                for b in range(B):
                    rows = slice(64 * b, 64 * b + 64)
                    ins = nc.vector.tensor_tensor(kv[n.par][rows, :, :, 0, b, :],
                                                  z_ps[rows, :, 256:384].rearrange("p u (h k) -> p u h k", h=H),
                                                  sig[rows, 0:256].rearrange("p (u h k) -> p u h k", u=2, h=H), ALU.mult)
                ins.then_inc(s.k_ready, 1)
                wait(dve, s.q_spread, n.n)
                nc.vector.scalar_tensor_tensor(q_raw[:].rearrange("p e u t -> p (e u t)"), qk_ps[:, 0:256],
                                               float(K) ** -0.5, sig[:, 256:512], ALU.mult, ALU.mult).then_inc(s.q_ready, 1)
                nc.vector.tensor_tensor(k_t[n.par][:].rearrange("p e u t -> p (e u t)"), qk_ps[:, 256:512],
                                        sig[:, 512:768], ALU.mult).then_inc(s.kt_ready, 1)

            def softplus(n):
                wait(dve, s.log1, n.n + 1)
                nc.vector.scalar_tensor_tensor(soft[:], z_ps[:, :, 0:256], -1.0, exp_z[:], ALU.mult, ALU.max).then_inc(s.soft, 1)

            def slots(n):
                wait(dve, s.decays, n.n + 1)
                wait(dve, s.r_ps, n.n - 1)
                nc.vector.scalar_tensor_tensor(slot[n.par][:], ge[:], 1.0, e_minus[:], ALU.subtract, ALU.mult,
                                               reverse0=True).then_inc(s.s_ready, 1)

            def causal():
                return m.c["causal"].unsqueeze(1).to_broadcast([P, 2 * H, C])

            def mask_a(n):
                wait(dve, s.a_ps, n.n + 1)
                wait(dve, s.r_ps, n.n)
                nc.vector.tensor_tensor(a_sb[:].rearrange("j u e p t -> j (u e p) t"),
                                        qk_ps.rearrange("p (a t) -> p a t", t=C), causal(), ALU.mult).then_inc(s.a_sb, 1)

            def new_states(n):
                wait(dve, s.d_sb, n.n + 1)
                wait(dve, s.st0, n.n + 1)
                wait(dve, s.u_ps, n.n + 1)
                nc.vector.tensor_tensor(t0[:].rearrange("p c b h k -> p (c b h k)"), st0[:].rearrange("p c b h k -> p (c b h k)"),
                                        g_ps[:, 0:256], ALU.add).then_inc(s.t0, 1)
                nc.vector.tensor_tensor(d01[:], d_sb[n.par][:, 0, :, 0, :], d_sb[n.par][:, 1, :, 1, :],
                                        ALU.mult).then_inc(s.d01, 1)
                wait(dve, s.d01, n.n + 1)
                nc.vector.tensor_tensor(st1[:].rearrange("p c b h k -> p c (b h) k"), t0[:].rearrange("p c b h k -> p c (b h) k"),
                                        d01[:].rearrange("p b h -> p (b h)").unsqueeze(2).unsqueeze(1).to_broadcast([P, 2, 4, K]),
                                        ALU.mult).then_inc(s.st1, 1)
                wait(dve, s.st1, n.n + 1)
                nc.vector.tensor_tensor(t1[:].rearrange("p c b h k -> p (c b h k)"), st1[:].rearrange("p c b h k -> p (c b h k)"),
                                        g_ps[:, 256:512], ALU.add).then_inc(s.t1, 1)

            def carry_state(n):
                wait(dve, s.d_sb, n.n + 2)
                nc.vector.tensor_tensor(d10[:], d_sb[n.par][:, 1, :, 0, :], d_sb[1 - n.par][:, 0, :, 1, :],
                                        ALU.mult).then_inc(s.d10, 1)
                wait(dve, s.d10, n.n + 1)
                wait(dve, s.o_ps, n.n + 1)
                nc.vector.tensor_tensor(st0[:].rearrange("p c b h k -> p c (b h) k"), t1[:].rearrange("p c b h k -> p c (b h) k"),
                                        d10[:].rearrange("p b h -> p (b h)").unsqueeze(2).unsqueeze(1).to_broadcast([P, 2, 4, K]),
                                        ALU.mult).then_inc(s.st0, 1)

            def flat(x):
                return x[:].rearrange("p u h m -> p (u h) m")

            def softmax_in(n):
                wait(dve, s.r_ps, n.n + 1)
                nc.vector.tensor_tensor(logits[:].rearrange("p u h m -> p (u h m)"), e_ps,
                                        e_plus[n.par][:].rearrange("p u m -> p (u m)"), ALU.mult).then_inc(s.logits, 1)
                wait(dve, s.logits, n.n + 1)
                nc.vector.tensor_reduce(maxes[:].rearrange("p u h -> p (u h)"), flat(logits), AX_X, ALU.max).then_inc(s.maxes, 1)
                wait(dve, s.maxes, n.n + 1)
                nc.vector.tensor_tensor(flat(logits), flat(logits),
                                        maxes[:].rearrange("p u h -> p (u h)").unsqueeze(2).to_broadcast([P, 2 * H, M]),
                                        ALU.subtract).then_inc(s.shifted, 1)

            def softmax_out(n):
                wait(dve, s.probs, n.n + 1)
                nc.vector.tensor_tensor(pw[:].rearrange("p u m -> p (u m)"), probs[:].rearrange("p u h m -> p (u h m)"),
                                        e_plus[n.par][:].rearrange("p u m -> p (u m)"), ALU.mult).then_inc(s.pw, 1)
                nc.vector.tensor_reduce(sums[:].rearrange("p u h -> p (u h)"), flat(probs), AX_X, ALU.add).then_inc(s.sums, 1)

            def mask_b(n):
                wait(dve, s.b_ps, n.n + 1)
                nc.vector.tensor_tensor(b_sb[:].rearrange("p u h t -> p (u h) t"),
                                        g_ps.rearrange("p (a t) -> p a t", t=C), causal(), ALU.mult).then_inc(s.b_sb, 1)

            def out_norm_start(n):
                wait(dve, s.sums, n.n + 1)
                nc.vector.tensor_tensor(s2[:], sums[:], sums[:], ALU.mult).then_inc(s.s2, 1)
                wait(dve, s.sq, n.n + 1)
                nc.vector.tensor_reduce(ms[:].rearrange("p u h -> p (u h)"), flat(sq), AX_X, ALU.add).then_inc(s.ms, 1)
                wait(dve, s.ms, n.n + 1)
                nc.vector.scalar_tensor_tensor(ms[:], s2[:], EPS, ms[:], ALU.mult, ALU.add).then_inc(s.oe, 1)

            def out_norm(n):
                wait(dve, s.o_rstd, n.n + 1)
                nc.vector.tensor_tensor(on[:].rearrange("p u (h k) -> p (u h) k", h=H),
                                        e_ps[:, 0:256].rearrange("p (a k) -> p a k", k=K),
                                        o_rstd[:].rearrange("p u h -> p (u h)").unsqueeze(2).to_broadcast([P, 2 * H, K]),
                                        ALU.mult).then_inc(s.on, 1)

            def residual(n):
                wait(dve, s.y_ps, n.n + 1)
                x = m.x[:, bass.ds(n.n * 2 * D, 2 * D)]
                nc.vector.tensor_tensor(x, y_ps[:, 0:256], x, ALU.add).then_inc(s.x1, 1)

            def body(n):
                mask_a(n)
                if not is_last(n):
                    normed(n.step(1))
                new_states(n)
                if not is_first(n):
                    residual(n.step(-1))
                    r.vector_norm(dve, n.step(-1))
                    r.vector_normed(dve, n.step(-1))
                if not is_last(n):
                    gates_and_values(n.step(1))
                softmax_in(n)
                if not is_last(n):
                    softplus(n.step(1))
                    cap_sigmoids(n.step(1))
                softmax_out(n)
                if not is_last(n):
                    gated(n.step(1))
                if not is_first(n):
                    r.vector_choose(dve, n.step(-1))
                mask_b(n)
                if not is_first(n):
                    r.vector_place(dve, n.step(-1))
                if not is_last(n):
                    slots(n.step(1))
                out_norm_start(n)
                if not is_last(n):
                    carry_state(n)
                out_norm(n)

            nc.vector.memset(st0[:], 0.0).then_inc(s.st0, 1)
            nc.vector.memset(r.before[:, 0, :], 0.0)
            nc.vector.memset(ready[:], 0.0).then_inc(s.const_ready, 1)
            normed(FIRST)
            gates_and_values(FIRST)
            cap_sigmoids(FIRST)
            softplus(FIRST)
            gated(FIRST)
            slots(FIRST)
            over_pairs(dve, body)
            residual(LAST)
            r.vector_norm(dve, LAST)
            r.vector_normed(dve, LAST)
            r.vector_choose(dve, LAST)
            r.vector_place(dve, LAST)
            r.vector_plan(dve)

        @block.scalar
        def _(act):
            def x_transposed(n):
                wait(act, s.x_t_ps, n.n + 1)
                wait(act, s.qk_ps, n.n)
                nc.scalar.copy(x_t[:].rearrange("p u t -> p (u t)"), xt_ps[:, 0:256]).then_inc(s.x_t, 1)

            def exps(n):
                wait(act, s.z_ps, n.n + 1)
                wait(act, s.sig, n.n)
                nc.scalar.activation(exp_kqk[:, 0:256].rearrange("p (u d) -> p u d", u=2), z_ps[:, :, 256:384], ACT.Exp,
                                     scale=-1.0)
                wait(act, s.soft, n.n)
                nc.scalar.activation(exp_z[:], z_ps[:, :, 0:256], ACT.Exp, scale=-1.0).then_inc(s.exp_z, 1)

            def exps_transposed(n):
                wait(act, s.qk_ps, n.n + 1)
                nc.scalar.activation(exp_kqk[:, 256:768], qk_ps, ACT.Exp, scale=-1.0).then_inc(s.exp_kqk, 1)

            def spread_q(n):
                wait(act, s.q_ready, n.n + 1)
                wait(act, s.r_ps, n.n - 1)
                for b in range(B):
                    for p in range(2):
                        rows = slice(64 * b + 32 * p, 64 * b + 32 * p + 32)
                        ins = nc.scalar.copy(q_t[n.par][rows, :, :, p, C * b:C * b + C],
                                             q_raw[rows].rearrange("k e u t -> k u e t"))
                ins.then_inc(s.q_spread, 1)

            def sigmoids(n):
                wait(act, s.sig_sum, n.n + 1)
                wait(act, s.kt_ready, n.n)
                nc.scalar.activation(sig[:], exp_kqk[:], ACT.Ln, bias=1.0).then_inc(s.sig_log, 1)
                wait(act, s.sig_log, n.n + 1)
                nc.scalar.activation(sig[:], sig[:], ACT.Exp, scale=-1.0).then_inc(s.sig, 1)

            def log1(n):
                wait(act, s.capped, n.n + 1)
                nc.scalar.activation(exp_z[:], exp_z[:], ACT.Ln, bias=1.0).then_inc(s.log1, 1)

            def decays(n):
                wait(act, s.soft, n.n + 1)
                wait(act, s.s_ready, n.n)
                nc.scalar.activation(ge[:], soft[:], ACT.Exp, scale=-1 / GATE_NORM).then_inc(s.ge_ready, 1)
                wait(act, s.g_ps, n.n + 1)
                wait(act, s.pw, n.n - 1)
                nc.scalar.activation(e_plus[n.par][:].rearrange("p u m -> p (u m)"), xt_ps, ACT.Exp)
                nc.scalar.activation(e_minus[:].rearrange("p u m -> p (u m)"), xt_ps, ACT.Exp, scale=-1.0).then_inc(s.decays, 1)

            def span_decays(n):
                wait(act, s.d_ps, n.n + 1)
                wait(act, s.d10, n.n - 1)
                nc.scalar.activation(d_sb[n.par][:].rearrange("s u b k p -> s (u b k p)"), h_ps[:, 0:16],
                                     ACT.Exp).then_inc(s.d_sb, 1)

            def state_transposed(n, u):
                wait(act, s.sk_ps, n.n * 2 + u + 1)
                wait(act, s.r_ps, n.n)
                nc.scalar.copy(sk_sb[u][:], h_ps[:, 0:P]).then_inc(s.sk_sb, 1)

            def slots_transposed(n):
                wait(act, s.st_ps, n.n + 1)
                wait(act, s.b_ps, n.n)
                nc.scalar.copy(st_sb[:].rearrange("p u h t -> p (u h t)"), f_ps).then_inc(s.st_sb, 1)

            def probabilities(n):
                wait(act, s.shifted, n.n + 1)
                wait(act, s.pw, n.n)
                nc.scalar.activation(probs[:], logits[:], ACT.Exp).then_inc(s.probs, 1)

            def weights_transposed(n):
                wait(act, s.pt_ps, n.n + 1)
                wait(act, s.o_ps, n.n)
                for e in range(2):
                    rows = slice(64 * e, 64 * e + 64)
                    ins = nc.scalar.copy(pt_sb[rows, :, :, e, :], f_ps[rows, :].rearrange("s (u p t) -> s u p t", u=2, p=2))
                ins.then_inc(s.pt_sb, 1)

            def squares(n):
                wait(act, s.o_ps, n.n + 1)
                wait(act, s.ms, n.n)
                nc.scalar.activation(sq[:].rearrange("p u h k -> p (u h k)"), e_ps[:, 0:256], ACT.Square,
                                     scale=float(K) ** -0.5).then_inc(s.sq, 1)

            def o_transposed(n):
                wait(act, s.ot_ps, n.n + 1)
                wait(act, s.y_ps, n.n)
                nc.scalar.copy(ot_sb[:].rearrange("p u t -> p (u t)"), ot_ps[:, 0:256]).then_inc(s.ot_sb, 1)

            def output_rstd(n):
                wait(act, s.oe, n.n + 1)
                wait(act, s.on, n.n)
                nc.scalar.activation(o_rstd[:], ms[:], ACT.Ln).then_inc(s.o_log, 1)
                wait(act, s.o_log, n.n + 1)
                nc.scalar.activation(o_rstd[:], o_rstd[:], ACT.Exp, scale=-0.5).then_inc(s.o_rstd, 1)

            def body(n):
                state_transposed(n, 0)
                if not is_last(n):
                    x_transposed(n.step(1))
                state_transposed(n, 1)
                if not is_first(n):
                    r.scalar_norm(act, n.step(-1))
                if not is_last(n):
                    exps(n.step(1))
                if not is_first(n):
                    r.scalar_transposed(act, n.step(-1))
                if not is_last(n):
                    exps_transposed(n.step(1))
                    log1(n.step(1))
                probabilities(n)
                if not is_last(n):
                    sigmoids(n.step(1))
                weights_transposed(n)
                if not is_last(n):
                    decays(n.step(1))
                if not is_first(n):
                    r.scalar_margin(act, n.step(-1))
                if not is_last(n):
                    span_decays(n.step(1))
                    spread_q(n.step(1))
                squares(n)
                output_rstd(n)
                if not is_last(n):
                    slots_transposed(n.step(1))
                o_transposed(n)

            nc.scalar.preload_act_table_set("natural_log_exp_and_others")
            x_transposed(FIRST)
            exps(FIRST)
            exps_transposed(FIRST)
            log1(FIRST)
            sigmoids(FIRST)
            spread_q(FIRST)
            decays(FIRST)
            span_decays(FIRST)
            slots_transposed(FIRST)
            over_pairs(act, body)
            scalar_late_maps(nc, act, m, s, loads)
            r.scalar_norm(act, LAST)
            r.scalar(act, LAST)
            scalar_late_copies(nc, act, m, s)
            r.tails(act, 1)

        @block.gpsimd
        def _(pool):
            def body(n):
                if not is_first(n):
                    r.gpsimd_scatter(pool, n.step(-1))

            rotation_tables(nc, pool, m, s, table_product, table_product2)
            pool.wait_ge(s.const_ready, 1)
            over_pairs(pool, body)
            r.gpsimd_scatter(pool, LAST)
            r.gpsimd_wait(pool)

        @block.sync
        def _(sp):
            for i, side in enumerate(("real", "imag")):
                half_ = slice(N * i, N * i + N)
                sp.dma_start(m.b_in[half_, :], a["L0_attn_b_B_" + side]).then_inc(loads.late, 16)
                sp.dma_start(m.c_mats[:, half_], a["L0_attn_b_C_" + side]).then_inc(loads.late, 16)
            sp.dma_start(m.w_out[:], a["L0_attn_b_W_out"]).then_inc(loads.late, 16)
            sp.dma_start(m.d_col[:], a["L0_attn_b_D"].rearrange("(h o) -> h o", o=1)).then_inc(loads.late, 16)
            sp.dma_start(m.b_out[:], a["L0_attn_b_b_out"].partition_broadcast(P)).then_inc(loads.late, 16)
            sp.dma_start(m.w1[:].rearrange("p (e f) -> p e f", e=E),
                         a["L0_ffn_W1"].rearrange("e d f -> d e f")).then_inc(loads.late, 16)
            for e in range(E):
                sp.dma_start(m.w2[:, e * FF:(e + 1) * FF].rearrange("f (k d) -> f k d", k=FB),
                             a["L0_ffn_W2"][e].rearrange("(k f) d -> f k d", f=P)).then_inc(loads.late, 16)
            sp.dma_start(m.b1_rows[0:E * FB, :], a["L0_ffn_b1"].rearrange("e (k f) -> (e k) f", f=P)).then_inc(loads.late, 16)
            sp.dma_start(m.b2[:], a["L0_ffn_b2"].rearrange("e d -> (e d)").partition_broadcast(P)).then_inc(loads.late, 16)
            for rows in dram.inputs:
                sp.dma_start(rows[E * REGION:, :].rearrange("(i p) d -> p i d", p=P), m.zero[:, E:, :]).then_inc(loads.late, 16)
            sp.wait_ge(loads.late, 16 * LATE)
            r.tails(sp, 0)
            sp.wait_ge(r.s.tails_out, 16 * E)


_INS = """L0_attn_a_x L0_attn_a_Wq L0_attn_a_Wk L0_attn_a_Wv L0_attn_a_Wf L0_attn_a_g_norm_w L0_attn_a_Wo
L0_attn_b_log_Lam_real L0_attn_b_Lam_imag L0_attn_b_B_real L0_attn_b_B_imag L0_attn_b_C_real L0_attn_b_C_imag
L0_attn_b_D L0_attn_b_log_dt L0_attn_b_W_out L0_attn_b_b_out L0_ffn_router_w L0_ffn_router_b L0_ffn_W1 L0_ffn_b1
L0_ffn_W2 L0_ffn_b2""".split()


def experts(nc, m, rows_in, rows_out, prefix):
    with Stage(nc) as ctx:
        def sb(name, *free, dt=F32):
            return ctx.enter_context(nc.sbuf_tensor(prefix + name, [P, *free], dt))

        s = Names()
        s.x_t_ps, s.x_t, s.w1, s.h_ps, s.h_act, s.h_dve, s.y_ps, s.y = \
            semaphores(ctx, nc, prefix, "x_t_ps x_t w1 h_ps h_act h_dve y_ps y")
        s.where, s.w2 = semaphores(ctx, nc, prefix, "where w2")
        begun = sb("begun", 1)
        s.y_raw, s.begun = semaphores(ctx, nc, prefix, "y_raw begun")
        loaded = semaphores(ctx, nc, prefix, "rows_in0 rows_in1 rows_in2 rows_in3")
        stored = semaphores(ctx, nc, prefix, "rows_out0 rows_out1 rows_out2 rows_out3")
        x_in = [sb(f"x_in{j}", ROW) for j in range(GROUP)]
        to = [sb(f"to{j}", 1, dt=U32) for j in range(GROUP)]
        where = [sb(f"where{j}", ROW - D) for j in range(GROUP)]
        x_t = [sb(f"x_t{j}", P) for j in range(2)]
        w2 = [sb(f"w2_of_tile{j}", FF) for j in range(GROUP)]
        w1 = [sb(f"w1_of_tile{j}", FF) for j in range(GROUP)]
        h = [sb(f"h{j}", FB, P) for j in range(2)]
        y_raw = [sb(f"y_raw{j}", D) for j in range(GROUP)]
        y = [sb(f"y{j}", D) for j in range(GROUP)]
        x_ps, h_ps, y_ps = m.bank[0:2], (m.bank[2:4], m.bank[4:6]), m.bank[6:8]

        block = ctx.enter_context(nc.Block())

        LASTQ = NGROUP - 1

        def ends(q, j):
            return isinstance(q, int) and q * GROUP + j >= NTILE

        def plan_value(eng, at, most):
            at = slice(at, at + 1) if isinstance(at, int) else bass.ds(at, 1)
            return eng.value_load(m.plan[0:1, at], min_val=0, max_val=most)

        def experts_of(eng, q):
            digits = plan_value(eng, q + NTILE, E ** (GROUP + 3) - 1)
            return [(digits >> (3 * k)) & (E - 1) for k in range(GROUP + 3)]

        def over_groups(eng, group):
            group(0)
            with eng.Fori(1, LASTQ) as q:
                group(q)
            group(LASTQ)

        @block.sync
        def _(sp):
            def load(t, q, j):
                row = plan_value(sp, t, ROWS - P)
                wait(sp, s.where, t - GROUP + 1)
                sp.dma_start(x_in[j][:], rows_in[bass.ds(row, P), :]).then_inc(loaded[j], 16)

            def group(q):
                for j in range(GROUP):
                    if not ends(q, j + GROUP):
                        load(q * GROUP + (j + GROUP), q + 1, j)

            for j in range(GROUP):
                load(j, 0, j)
            group(0)
            with sp.Fori(1, LASTQ - 1) as q:
                group(q)
            group(LASTQ - 1)

        @block.gpsimd
        def _(pool):
            def group(q):
                for j in range(GROUP):
                    if ends(q, j):
                        break
                    t = q * GROUP + j
                    wait_apart(pool, s.y, t + 1, s.begun)
                    nc.gpsimd.indirect_dma_start(rows_out[:, :], bass.IndirectOffsetOnAxis(ap=to[j][:], axis=0),
                                                 y[j][:], None).then_inc(stored[j], 16)

            over_groups(pool, group)
            for j in range(GROUP):
                pool.wait_ge(stored[j], 16 * len(range(j, NTILE, GROUP)))

        @block.tensor
        def _(pe):
            def transposed(t, q, j):
                wait(pe, loaded[j], (q + 1) * 16)
                wait(pe, s.x_t, t - 1)
                pe.transpose(x_ps[j % 2][:, 0:P], x_in[j][:, 0:D], m.c["ident"]).then_inc(s.x_t_ps, 1)

            def hidden(t, j):
                wait(pe, s.x_t, t + 1)
                wait(pe, s.w1, t + 1)
                wait(pe, s.h_act, t - 1)
                wait(pe, s.h_dve, t - 1)
                for f in range(FB):
                    mm = pe.matmul(h_ps[j % 2][f // 2][:, P * (f % 2):P * (f % 2) + P],
                                   w1[j % GROUP][:, P * f:P * f + P], x_t[j % 2][:], start=True, stop=True)
                mm.then_inc(s.h_ps, 1)

            def result(t, j):
                wait(pe, s.w2, t + 1)
                wait(pe, s.h_act, t + 1)
                wait(pe, s.h_dve, t + 1)
                wait(pe, s.y_raw, t - 1)
                for f in range(FB):
                    mm = pe.matmul(y_ps[j % 2][:, 0:D], h[j % 2][:, f, :], w2[j][:, D * f:D * f + D],
                                   start=(f == 0), stop=(f == FB - 1))
                mm.then_inc(s.y_ps, 1)

            def group(q):
                for j in range(GROUP):
                    if ends(q, j):
                        break
                    t = q * GROUP + j
                    if not ends(q, j + 1):
                        hidden(t + 1, j + 1)
                    if not ends(q, j + 2):
                        transposed(t + 2, q + (j + 2) // GROUP, (j + 2) % GROUP)
                    result(t, j)

            transposed(0, 0, 0)
            hidden(0, 0)
            transposed(1, 0, 1)
            over_groups(pe, group)

        @block.vector
        def _(dve):
            def hidden(t, j, owner):
                wait(dve, s.h_ps, t + 1)
                wait(dve, s.y_ps, t - 1)
                for f in range(FB // 2, FB):
                    ins = nc.vector.tensor_scalar(h[j % 2][:, f, :], h_ps[j % 2][1][:, P * (f % 2):P * (f % 2) + P],
                                                  m.b1[:, bass.ds(owner * FB + f, 1)], 0.0, ALU.add, ALU.max)
                ins.then_inc(s.h_dve, 1)

            def destinations(t, j):
                wait(dve, s.x_t_ps, t + 1)
                nc.vector.tensor_copy(where[j][:], x_in[j][:, D:]).then_inc(s.where, 1)

            def weights(j, owner):
                nc.vector.tensor_copy(w2[j % GROUP][:], m.w2[:, bass.ds(owner * FF, FF)]).then_inc(s.w2, 1)

            def result(t, q, j, owner):
                wait(dve, stored[j], q * 16)
                wait(dve, s.y_ps, t + 1)
                nc.vector.tensor_tensor(y_raw[j][:], y_ps[j % 2][:, 0:D], m.b2[:, bass.ds(owner * D, D)], ALU.add).then_inc(s.y_raw, 1)
                nc.vector.tensor_copy(to[j][:], where[j][:, 0:1])
                wait(dve, s.y_raw, t + 1)
                nc.vector.tensor_scalar(y[j][:], y_raw[j][:], where[j][:, 1:2], None, ALU.mult).then_inc(s.y, 1)

            def group(q):
                owner = experts_of(dve, q)
                for j in range(GROUP):
                    if ends(q, j):
                        break
                    if not ends(q, j + 2):
                        destinations(q * GROUP + j + 2, (j + 2) % GROUP)
                    result(q * GROUP + j, q, j, owner[j])
                    if not ends(q, j + 2):
                        weights(j + 2, owner[j + 2])
                        hidden(q * GROUP + j + 2, j + 2, owner[j + 2])

            nc.vector.memset(begun[:], 0.0).then_inc(s.begun, 1)
            owner = experts_of(dve, 0)
            for t in range(2):
                weights(t, owner[t])
                destinations(t, t)
                hidden(t, t, owner[t])
            over_groups(dve, group)

        @block.scalar
        def _(act):
            def x_transposed(t, j):
                wait(act, s.x_t_ps, t + 1)
                nc.scalar.copy(x_t[j % 2][:], x_ps[j % 2][:, 0:P]).then_inc(s.x_t, 1)

            def weights(j, owner):
                nc.scalar.copy(w1[j % GROUP][:], m.w1[:, bass.ds(owner * FF, FF)]).then_inc(s.w1, 1)

            def hidden(t, j, owner):
                if isinstance(t, int) and t == NTILE - 1:
                    act.wait_ge(s.h_ps, NTILE)
                for f in range(FB // 2):
                    ins = nc.scalar.activation(h[j % 2][:, f, :], h_ps[j % 2][0][:, P * (f % 2):P * (f % 2) + P],
                                               ACT.Relu, bias=m.b1[:, bass.ds(owner * FB + f, 1)])
                ins.then_inc(s.h_act, 1)

            def group(q):
                owner = experts_of(act, q)
                for j in range(GROUP):
                    if ends(q, j):
                        break
                    if not ends(q, j + 2):
                        x_transposed(q * GROUP + j + 2, j)
                    if not ends(q, j + 3):
                        weights(j + 3, owner[j + 3])
                    if not ends(q, j + 1):
                        hidden(q * GROUP + j + 1, j + 1, owner[j + 1])

            owner = experts_of(act, 0)
            for t in range(2):
                weights(t, owner[t])
                x_transposed(t, t)
            weights(2, owner[2])
            hidden(0, 0, owner[0])
            over_groups(act, group)


PARTS = 4
PART = NCHUNK // PARTS


def load_results(eng, m, rows, choice, chunks, arrived):
    at = choice * B * T + chunks.start * P
    eng.dma_start(m.results[:, choice, chunks.start:chunks.stop, :],
                  rows[at:at + len(chunks) * P, :].rearrange("(c p) d -> p c d", p=P)).then_inc(arrived, 16)


def space_and_route(nc, m, a, dram):
    with Stage(nc) as ctx:
        def sb(name, *free, dt=F32):
            return ctx.enter_context(nc.sbuf_tensor("sp_" + name, [P, *free], dt))

        s = Names()
        s.const_ready, s.stats, s.mv, s.var_eps, s.rstd_log, s.rstd, s.xn, s.x_t_ps = \
            semaphores(ctx, nc, "sp_", "const_ready stats mv var_eps rstd_log rstd xn x_t_ps")
        s.x_t, s.in_ps, s.in_cos, s.in_sin, s.turned, s.state, s.back_cos = \
            semaphores(ctx, nc, "sp_", "x_t in_ps in_cos in_sin turned state back_cos")
        s.back_sin, s.out_ps, s.x3, s.next_slot, s.both, s.sum = \
            semaphores(ctx, nc, "sp_", "back_sin out_ps x3 next_slot both sum")
        arrived = semaphores(ctx, nc, "sp_", "results0 results1 results2 results3")
        parts = range(0, 2), range(2, 4), range(4, 8), range(8, NCHUNK)
        r = Route(ctx, nc, m, a, dram, "rb_")
        r.bank, r.ready, r.x_written = m.bank[7], s.const_ready, s.x3
        ln = Norm(sb, "ln")
        both = sb("both", 2, D)
        xn = sb("xn", 2, D)
        x_t = [sb(f"x_t{i}", 2, P) for i in range(2)]
        in_cos = sb("in_cos", B, 2, C)
        in_sin = sb("in_sin", B, 2, C)
        turned = sb("turned", B, 2 * C)
        state = [sb(f"state{i}", B, 2 * C) for i in range(2)]
        back_cos = sb("back_cos", 2, B, C)
        back_sin = sb("back_sin", 2, B, C)
        t_ps, in_ps, out_ps = m.bank[0], m.bank[1], m.bank[2]

        block = ctx.enter_context(nc.Block())

        @block.sync
        def _(sp):
            load_results(sp, m, dram.results[0], 0, parts[0], arrived[0])
            for chunks, sem in zip(parts[1:], arrived[1:]):
                for choice in range(2):
                    load_results(sp, m, dram.results[0], choice, chunks, sem)
            r.tails(sp, 0)
            sp.wait_ge(r.s.tails_out, 16 * E)

        @block.tensor
        def _(pe):
            def out(n):
                wait(pe, s.x3, n.n)
                wait(pe, s.back_sin, n.n + 1)
                for u in range(2):
                    to = out_ps[:, D * u:D * u + D]
                    pe.matmul(to, x_t[n.par][:, u, :], m.out_x[:], start=True, stop=False)
                    pe.matmul(to, m.c["ones"][0:1, :], m.b_out[0:1, :], start=False, stop=False)
                    pe.matmul(to, back_cos[:, u].rearrange("s b t -> s (b t)"), m.out_cos[:], start=False, stop=False)
                    mm = pe.matmul(to, back_sin[:, u].rearrange("s b t -> s (b t)"), m.out_sin[:], start=False, stop=True)
                mm.then_inc(s.out_ps, 1)

            def x_transposed(n):
                wait(pe, s.x_t, n.n)
                wait(pe, s.xn, n.n + 1)
                for u in range(2):
                    mm = pe.transpose(t_ps[:, P * u:P * u + P], xn[:, u, :], m.c["ident"])
                mm.then_inc(s.x_t_ps, 1)

            def into(n):
                wait(pe, s.in_sin, n.n)
                wait(pe, s.x_t, n.n + 1)
                x_all = x_t[n.par][:].rearrange("p u t -> p (u t)")
                pe.matmul(in_ps[:, 0:256], m.b_in_t[:], x_all, start=True, stop=True)
                pe.matmul(in_ps[:, 256:512], m.b_in_swap[:], x_all, start=True, stop=True).then_inc(s.in_ps, 1)

            def body(n):
                if not is_first(n):
                    out(n.step(-1))
                x_transposed(n)
                if not is_first(n) and not is_first(n.step(-1)):
                    r.tensor_ranks(pe, n.step(-2))
                into(n)
                if not is_first(n):
                    r.tensor_transposed(pe, n.step(-1))
                    r.tensor_logits(pe, n.step(-1))

            over_pairs(pe, body)
            out(LAST)
            r.tensor_ranks(pe, LAST.step(-1))
            r.tensor(pe, LAST)

        @block.vector
        def _(dve):
            def table(t, n):
                return (t[:, bass.ds(n.n * 2 * C, 2 * C)].rearrange("s (u t) -> s u t", u=2)
                        .unsqueeze(2).to_broadcast([P, 2, B, C]))

            def residual(n):
                if isinstance(n.n, int) and n.n < 2:
                    dve.wait_ge(arrived[n.n], 32)
                elif isinstance(n.n, int) and n.n == 2:
                    for later in arrived[2:]:
                        dve.wait_ge(later, 32)
                wait(dve, s.sum, n.n)
                nc.vector.tensor_tensor(both[:], m.results[:, 0, bass.ds(n.n * 2, 2), :],
                                        m.results[:, 1, bass.ds(n.n * 2, 2), :], ALU.add).then_inc(s.both, 1)
                wait(dve, s.both, n.n + 1)
                x = m.x[:, bass.ds(n.n * 2 * D, 2 * D)]
                nc.vector.tensor_tensor(x, both[:].rearrange("p u d -> p (u d)"), x, ALU.add).then_inc(s.sum, 1)
                wait(dve, s.sum, n.n + 1)
                nc.vector.memset(ln.carrier[:], 0.0)
                for u in range(2):
                    ins = nc.vector.bn_stats(ln.stats[:, u, :], chunk_rows(m, n, u))
                ins.then_inc(s.stats, 1)
                wait(dve, s.stats, n.n + 1)
                nc.vector.memset(ln.carrier[:], 0.0)
                for u in range(2):
                    ins = nc.vector.bn_aggr(ln.mv[:, u, :], ln.stats[:, u, :])
                ins.then_inc(s.mv, 1)
                wait(dve, s.mv, n.n + 1)
                nc.vector.tensor_scalar(ln.ve[:], ln.mv[:, :, 1], EPS, None, ALU.add).then_inc(s.var_eps, 1)

            def normed(n):
                wait(dve, s.x_t_ps, n.n)
                wait(dve, s.rstd, n.n + 1)
                for u in range(2):
                    ins = nc.vector.tensor_scalar(xn[:, u, :], chunk_rows(m, n, u), ln.mv[:, u, 0:1], ln.rstd[:, u:u + 1],
                                                  ALU.subtract, ALU.mult)
                ins.then_inc(s.xn, 1)

            def recur(n):
                wait(dve, s.in_ps, n.n + 1)
                nc.vector.tensor_tensor(in_cos[:].rearrange("s b u t -> s u b t"),
                                        in_ps[:, 0:256].rearrange("s (u b t) -> s u b t", u=2, b=B),
                                        table(m.cos, n), ALU.mult).then_inc(s.in_cos, 1)
                nc.vector.tensor_tensor(in_sin[:].rearrange("s b u t -> s u b t"),
                                        in_ps[:, 256:512].rearrange("s (u b t) -> s u b t", u=2, b=B),
                                        table(m.sin, n), ALU.mult).then_inc(s.in_sin, 1)
                wait(dve, s.in_sin, n.n + 1)
                nc.vector.tensor_tensor(turned[:].rearrange("s b t -> s (b t)"), in_cos[:].rearrange("s b u t -> s (b u t)"),
                                        in_sin[:].rearrange("s b u t -> s (b u t)"), ALU.add).then_inc(s.turned, 1)
                wait(dve, s.turned, n.n + 1)
                for b in range(B):
                    before = 0.0 if is_first(n) else state[1 - n.par][:, b, 2 * C - 1:2 * C]
                    ins = nc.vector.tensor_tensor_scan(state[n.par][:, b, :], m.mag[:], turned[:, b, :], before,
                                                       ALU.mult, ALU.add)
                ins.then_inc(s.state, 1)
                wait(dve, s.state, n.n + 1)
                wait(dve, s.out_ps, n.n)
                for t, out, done in ((m.cos, back_cos, s.back_cos), (m.sin, back_sin, s.back_sin)):
                    nc.vector.tensor_tensor(out[:], state[n.par][:].rearrange("s b (u t) -> s u b t", u=2),
                                            table(t, n), ALU.mult).then_inc(done, 1)

            def end(n):
                wait(dve, s.out_ps, n.n + 1)
                x = m.x[:, bass.ds(n.n * 2 * D, 2 * D)]
                nc.vector.tensor_tensor(x, out_ps[:, 0:256], x, ALU.add).then_inc(s.x3, 1)

            def body(n):
                if not is_last(n):
                    residual(n.step(1))
                if not is_first(n):
                    end(n.step(-1))
                    r.vector_norm(dve, n.step(-1))
                if not is_first(n):
                    if not is_first(n.step(-1)):
                        r.vector_place(dve, n.step(-2))
                    r.vector_normed(dve, n.step(-1))
                recur(n)
                if not is_last(n):
                    normed(n.step(1))
                if not is_first(n):
                    r.vector_choose(dve, n.step(-1))

            nc.vector.tensor_copy(m.next_slot[:], m.c["base"]).then_inc(s.next_slot, 1)
            dve.wait_ge(s.next_slot, 1)
            nc.vector.memset(r.before[:, 0, :], 0.0).then_inc(s.const_ready, 1)
            residual(FIRST)
            normed(FIRST)
            over_pairs(dve, body)
            r.vector_place(dve, LAST.step(-1))
            end(LAST)
            r.vector_norm(dve, LAST)
            r.vector_normed(dve, LAST)
            r.vector_choose(dve, LAST)
            r.vector_place(dve, LAST)
            r.vector_plan(dve)

        @block.scalar
        def _(act):
            def input_norm(n):
                wait(act, s.var_eps, n.n + 1)
                wait(act, s.xn, n.n)
                nc.scalar.activation(ln.rstd[:], ln.ve[:], ACT.Ln).then_inc(s.rstd_log, 1)
                wait(act, s.rstd_log, n.n + 1)
                nc.scalar.activation(ln.rstd[:], ln.rstd[:], ACT.Exp, scale=-0.5).then_inc(s.rstd, 1)

            def body(n):
                wait(act, s.out_ps, n.n - 1)
                wait(act, s.x_t_ps, n.n + 1)
                nc.scalar.copy(x_t[n.par][:].rearrange("p u t -> p (u t)"), t_ps[:, 0:256]).then_inc(s.x_t, 1)
                if not is_first(n):
                    r.scalar_norm(act, n.step(-1))
                if not is_last(n):
                    input_norm(n.step(1))
                if not is_first(n):
                    r.scalar_transposed(act, n.step(-1))
                    r.scalar_margin(act, n.step(-1))

            load_results(act, m, dram.results[0], 1, parts[0], arrived[0])
            nc.scalar.preload_act_table_set("natural_log_exp_and_others")
            input_norm(FIRST)
            over_pairs(act, body)
            r.scalar_norm(act, LAST)
            r.scalar(act, LAST)
            r.tails(act, 1)

        @block.gpsimd
        def _(pool):
            def body(n):
                if not is_first(n) and not is_first(n.step(-1)):
                    r.gpsimd_scatter(pool, n.step(-2))

            pool.wait_ge(s.const_ready, 1)
            over_pairs(pool, body)
            r.gpsimd_scatter(pool, LAST.step(-1))
            r.gpsimd_scatter(pool, LAST)
            r.gpsimd_wait(pool)


def add_and_store(nc, m, rows, out):
    with Stage(nc) as ctx:
        s = Names()
        s.both, s.sum, s.out = semaphores(ctx, nc, "go_", "both sum out")
        arrived = semaphores(ctx, nc, "go_", "results0 results1 results2 results3")
        block = ctx.enter_context(nc.Block())

        def store(eng, part, b):
            chunks = slice(part * PART * D, (part + 1) * PART * D)
            at = part * PART * C
            eng.dma_start(out[b, at:at + PART * C, :].rearrange("(c t) d -> t c d", t=C),
                          m.x[C * b:C * b + C, chunks].rearrange("p (c d) -> p c d", d=D)).then_inc(s.out, 16)

        @block.vector
        def _(dve):
            for part in range(PARTS):
                here = slice(part * PART, (part + 1) * PART)
                best, second = m.results[:, 0, here, :], m.results[:, 1, here, :]
                dve.wait_ge(arrived[part], 32)
                nc.vector.tensor_tensor(best, best, second, ALU.add).then_inc(s.both, 1)
                x = m.x[:, part * PART * D:(part + 1) * PART * D].rearrange("p (c d) -> p c d", d=D)
                dve.wait_ge(s.both, part + 1)
                nc.vector.tensor_tensor(x, x, best, ALU.add).then_inc(s.sum, 1)

        @block.scalar
        def _(act):
            for part in range(PARTS):
                load_results(act, m, rows, 1, range(part * PART, (part + 1) * PART), arrived[part])
            for part in range(PARTS):
                act.wait_ge(s.sum, part + 1)
                store(act, part, 1)

        @block.sync
        def _(sp):
            for part in range(PARTS):
                load_results(sp, m, rows, 0, range(part * PART, (part + 1) * PART), arrived[part])
            for part in range(PARTS):
                sp.wait_ge(s.sum, part + 1)
                store(sp, part, 0)
            sp.wait_ge(s.out, 16 * PARTS * B)


def program(nc, a, out):
    with Stage(nc) as ctx:
        m = memory(ctx, nc)

        def rows(name, count, width):
            return [nc.dram_tensor(f"{name}{i}", (count, width), F32, kind="Internal").ap() for i in range(2)]

        dram = Names()
        loads = Names()
        loads.const, loads.attn, loads.x, loads.rates, loads.late = semaphores(ctx, nc, "in_", "const attn x rates late")
        dram.inputs, dram.results = rows("expert_inputs", ROWS, ROW), rows("expert_results", 2 * B * T + 2 * E * P, D)
        with ExitStack() as attention:
            z = zero_padded_operands(attention, nc)
            setup(nc, m, a, dram, z, loads)
            nc.all_engine_barrier()
            attention_and_route(nc, m, a, dram, z, loads)
        nc.all_engine_barrier()
        experts(nc, m, dram.inputs[0], dram.results[0], "ea_")
        nc.all_engine_barrier()
        space_and_route(nc, m, a, dram)
        nc.all_engine_barrier()
        experts(nc, m, dram.inputs[1], dram.results[1], "eb_")
        nc.all_engine_barrier()
        add_and_store(nc, m, dram.results[1], out)


def kernel(**inputs):
    import concourse.bacc as bacc
    from concourse.bass_utils import run_bass_kernel_spmd

    nc = bacc.Bacc("TRN2", target_bir_lowering=False, num_devices=1)
    arrays, args = {}, {}
    for name in [*_INS, "constants"]:
        x = constants()[0] if name == "constants" else np.ascontiguousarray(inputs[name])
        arrays[f"in_{name}_dram"] = x
        args[name] = nc.dram_tensor(f"in_{name}_dram", x.shape, mybir.dt.from_np(x.dtype), kind="ExternalInput").ap()
    out = nc.dram_tensor("out_dram", (B, T, D), F32, kind="ExternalOutput").ap()
    program(nc, args, out)
    r = run_bass_kernel_spmd(nc, [arrays], core_ids=[0])
    return r.results[0]["out_dram"]
```
